# Optimizing a Trainium2 kernel written in Bass

```python
import numpy as np
import jax
import jax.numpy as jnp

def _softmax(x, axis=-1):
    return jax.nn.softmax(x, axis=axis)

def _gelu(x):
    return jax.nn.gelu(x, approximate=True)

def _silu(x):
    return jax.nn.silu(x)

def _sigmoid(x):
    return jax.nn.sigmoid(x)

def _layernorm(x, axis=-1, eps=1e-05):
    m = jnp.mean(x, axis=axis, keepdims=True)
    v = jnp.var(x, axis=axis, keepdims=True)
    return (x - m) / jnp.sqrt(v + eps)

def _scatter_add(tgt, idx, src, axis=0):
    return tgt.at[idx].add(src)

def _segment_sum(src, seg, n):
    return jax.ops.segment_sum(src, seg, n)
kernel_name = 'mk_macaron_d1_jaxref_r8_018005'

def setup_inputs(seed: int=0):
    np.random.seed(seed)
    _w = jnp.asarray

    def _L0_attn_setup():
        import jax, jax.numpy as jnp
        import numpy as np
        B, S, D = (8, 128, 128)
        H, HD = (8, 64)
        HID = H * HD
        P = 2 * D
        K = 4
        EPS = 1e-06
        CAP = 15.0

        def _layernorm(x, g, b):
            mu = jnp.mean(x, -1, keepdims=True)
            var = jnp.var(x, -1, keepdims=True)
            return (x - mu) * jax.lax.rsqrt(var + EPS) * g + b

        def _soft_cap(v):
            return CAP * jnp.tanh(v / CAP)

        def _causal_conv_feat(x, w, b):
            L = x.shape[-1]
            xp = jnp.pad(x, ((0, 0), (0, 0), (K - 1, 0)))
            out = b
            for m in range(K):
                out = out + w[m] * xp[..., m:m + L]
            return out

        def _forward(x, ln_g, ln_b, mh_g, mh_b, W_up_l, b_up_l, W_up_r, b_up_r, W_down, b_down, conv_w, conv_b, W_skip, b_skip, W_i, b_i, W_f, b_f, W_o, b_o, W_q, b_q, W_k, b_k, W_v, b_v):
            Bs, Sl, _ = x.shape
            xn = _layernorm(x, ln_g, ln_b)
            x_t = xn @ W_up_l.T + b_up_l
            r_t = xn @ W_up_r.T + b_up_r
            x_c = jax.nn.silu(_causal_conv_feat(x_t, conv_w, conv_b))
            x_skip = x_c @ W_skip.T + b_skip
            q = (x_c @ W_q.T + b_q).reshape(Bs, Sl, H, HD)
            k = (x_c @ W_k.T + b_k).reshape(Bs, Sl, H, HD) / float(np.sqrt(HD))
            v = (x_t @ W_v.T + b_v).reshape(Bs, Sl, H, HD)
            i_pre = _soft_cap(x_c @ W_i.T + b_i)
            f_pre = _soft_cap(x_c @ W_f.T + b_f)
            o = jax.nn.sigmoid(x_t @ W_o.T + b_o)

            def step(carry, inp):
                c, n, m = carry
                qt, kt, vt, it, ft = inp
                m_t = jnp.maximum(ft + m, it)
                ie = jnp.exp(it - m_t)
                fe = jnp.exp(ft - m_t + m)
                c = fe[:, :, None, None] * c + ie[:, :, None, None] * jnp.einsum('bhd,bhe->bhde', vt, kt)
                n = fe[:, :, None] * n + ie[:, :, None] * kt
                num = jnp.einsum('bhde,bhe->bhd', c, qt)
                den = jnp.maximum(jnp.sum(n * qt, -1, keepdims=True), 1.0)
                return ((c, n, m_t), num / den)
            c0 = jnp.zeros((Bs, H, HD, HD), x.dtype)
            n0 = jnp.ones((Bs, H, HD), x.dtype)
            m0 = jnp.zeros((Bs, H), x.dtype)
            seq = tuple((jnp.moveaxis(a, 1, 0) for a in (q, k, v, i_pre, f_pre)))
            _, hs = jax.lax.scan(step, (c0, n0, m0), seq)
            h = o * jnp.moveaxis(hs, 0, 1).reshape(Bs, Sl, HID)
            hn = _layernorm(h.reshape(Bs, Sl, H, HD), mh_g, mh_b).reshape(Bs, Sl, HID)
            out = (hn + x_skip) * jax.nn.silu(r_t)
            return out @ W_down.T + b_down + x
        key = jax.random.key(seed)
        ks = jax.random.split(key, 16)

        def w(kk, shape):
            return jax.random.normal(kk, shape, jnp.float32) / np.sqrt(shape[-1]).astype(np.float32)
        return {'x': jax.random.normal(ks[0], (B, S, D), jnp.float32), 'ln_g': jnp.ones((D,), jnp.float32), 'ln_b': jnp.zeros((D,), jnp.float32), 'mh_g': jnp.ones((H, HD), jnp.float32), 'mh_b': jnp.zeros((H, HD), jnp.float32), 'W_up_l': w(ks[1], (P, D)), 'b_up_l': jnp.zeros((P,), jnp.float32), 'W_up_r': w(ks[2], (HID, D)), 'b_up_r': jnp.zeros((HID,), jnp.float32), 'W_down': w(ks[3], (D, HID)), 'b_down': jnp.zeros((D,), jnp.float32), 'conv_w': jax.random.normal(ks[4], (K,), jnp.float32) * 0.3, 'conv_b': jnp.zeros((), jnp.float32), 'W_skip': w(ks[5], (HID, P)), 'b_skip': jnp.zeros((HID,), jnp.float32), 'W_i': w(ks[6], (H, P)), 'b_i': jnp.zeros((H,), jnp.float32), 'W_f': w(ks[7], (H, P)), 'b_f': jnp.zeros((H,), jnp.float32), 'W_o': w(ks[8], (HID, P)), 'b_o': jnp.zeros((HID,), jnp.float32), 'W_q': w(ks[9], (HID, P)), 'b_q': jnp.zeros((HID,), jnp.float32), 'W_k': w(ks[10], (HID, P)), 'b_k': jnp.zeros((HID,), jnp.float32), 'W_v': w(ks[11], (HID, P)), 'b_v': jnp.zeros((HID,), jnp.float32)}
    _L0_attn_in = _L0_attn_setup()

    def _L0_ffn_setup():
        import jax, jax.numpy as jnp
        import numpy as np
        B, S, H, F, E = (2, 256, 128, 512, 8)
        key = jax.random.key(seed)
        ks = jax.random.split(key, 4)
        x = jax.random.normal(ks[0], (B, S, H), dtype=jnp.float32)
        w_router = jax.random.normal(ks[1], (H, E), dtype=jnp.float32) * 0.02
        w1 = jax.random.normal(ks[2], (E, H, F), dtype=jnp.float32) * 0.02
        b1 = jnp.zeros((E, F), dtype=jnp.float32)
        w2 = jax.random.normal(ks[3], (E, F, H), dtype=jnp.float32) * 0.02
        b2 = jnp.zeros((E, H), dtype=jnp.float32)
        return {'x': x, 'w_router': w_router, 'w1': w1, 'b1': b1, 'w2': w2, 'b2': b2}
    _L0_ffn_in = _L0_ffn_setup()
    _d = {'L0_attn_x': _L0_attn_in['x'], 'L0_attn_ln_g': _L0_attn_in['ln_g'], 'L0_attn_ln_b': _L0_attn_in['ln_b'], 'L0_attn_mh_g': _L0_attn_in['mh_g'], 'L0_attn_mh_b': _L0_attn_in['mh_b'], 'L0_attn_W_up_l': _L0_attn_in['W_up_l'], 'L0_attn_b_up_l': _L0_attn_in['b_up_l'], 'L0_attn_W_up_r': _L0_attn_in['W_up_r'], 'L0_attn_b_up_r': _L0_attn_in['b_up_r'], 'L0_attn_W_down': _L0_attn_in['W_down'], 'L0_attn_b_down': _L0_attn_in['b_down'], 'L0_attn_conv_w': _L0_attn_in['conv_w'], 'L0_attn_conv_b': _L0_attn_in['conv_b'], 'L0_attn_W_skip': _L0_attn_in['W_skip'], 'L0_attn_b_skip': _L0_attn_in['b_skip'], 'L0_attn_W_i': _L0_attn_in['W_i'], 'L0_attn_b_i': _L0_attn_in['b_i'], 'L0_attn_W_f': _L0_attn_in['W_f'], 'L0_attn_b_f': _L0_attn_in['b_f'], 'L0_attn_W_o': _L0_attn_in['W_o'], 'L0_attn_b_o': _L0_attn_in['b_o'], 'L0_attn_W_q': _L0_attn_in['W_q'], 'L0_attn_b_q': _L0_attn_in['b_q'], 'L0_attn_W_k': _L0_attn_in['W_k'], 'L0_attn_b_k': _L0_attn_in['b_k'], 'L0_attn_W_v': _L0_attn_in['W_v'], 'L0_attn_b_v': _L0_attn_in['b_v'], 'L0_ffn_w_router': _L0_ffn_in['w_router'], 'L0_ffn_w1': _L0_ffn_in['w1'], 'L0_ffn_b1': _L0_ffn_in['b1'], 'L0_ffn_w2': _L0_ffn_in['w2'], 'L0_ffn_b2': _L0_ffn_in['b2']}
    _x0 = _d['L0_attn_x']
    _d['L0_attn_x'] = jax.random.normal(jax.random.fold_in(jax.random.key(seed), 1), (4, 512, 128), dtype=_x0.dtype)
    del _x0
    return _d

def reference(L0_attn_x, L0_attn_ln_g, L0_attn_ln_b, L0_attn_mh_g, L0_attn_mh_b, L0_attn_W_up_l, L0_attn_b_up_l, L0_attn_W_up_r, L0_attn_b_up_r, L0_attn_W_down, L0_attn_b_down, L0_attn_conv_w, L0_attn_conv_b, L0_attn_W_skip, L0_attn_b_skip, L0_attn_W_i, L0_attn_b_i, L0_attn_W_f, L0_attn_b_f, L0_attn_W_o, L0_attn_b_o, L0_attn_W_q, L0_attn_b_q, L0_attn_W_k, L0_attn_b_k, L0_attn_W_v, L0_attn_b_v, L0_ffn_w_router, L0_ffn_w1, L0_ffn_b1, L0_ffn_w2, L0_ffn_b2):

    def _L0_attn_ref(x, ln_g, ln_b, mh_g, mh_b, W_up_l, b_up_l, W_up_r, b_up_r, W_down, b_down, conv_w, conv_b, W_skip, b_skip, W_i, b_i, W_f, b_f, W_o, b_o, W_q, b_q, W_k, b_k, W_v, b_v):
        import jax, jax.numpy as jnp
        import numpy as np
        B, S, D = (8, 128, 128)
        H, HD = (8, 64)
        HID = H * HD
        P = 2 * D
        K = 4
        EPS = 1e-06
        CAP = 15.0

        def _layernorm(x, g, b):
            mu = jnp.mean(x, -1, keepdims=True)
            var = jnp.var(x, -1, keepdims=True)
            return (x - mu) * jax.lax.rsqrt(var + EPS) * g + b

        def _soft_cap(v):
            return CAP * jnp.tanh(v / CAP)

        def _causal_conv_feat(x, w, b):
            L = x.shape[-1]
            xp = jnp.pad(x, ((0, 0), (0, 0), (K - 1, 0)))
            out = b
            for m in range(K):
                out = out + w[m] * xp[..., m:m + L]
            return out

        def _forward(x, ln_g, ln_b, mh_g, mh_b, W_up_l, b_up_l, W_up_r, b_up_r, W_down, b_down, conv_w, conv_b, W_skip, b_skip, W_i, b_i, W_f, b_f, W_o, b_o, W_q, b_q, W_k, b_k, W_v, b_v):
            Bs, Sl, _ = x.shape
            xn = _layernorm(x, ln_g, ln_b)
            x_t = xn @ W_up_l.T + b_up_l
            r_t = xn @ W_up_r.T + b_up_r
            x_c = jax.nn.silu(_causal_conv_feat(x_t, conv_w, conv_b))
            x_skip = x_c @ W_skip.T + b_skip
            q = (x_c @ W_q.T + b_q).reshape(Bs, Sl, H, HD)
            k = (x_c @ W_k.T + b_k).reshape(Bs, Sl, H, HD) / float(np.sqrt(HD))
            v = (x_t @ W_v.T + b_v).reshape(Bs, Sl, H, HD)
            i_pre = _soft_cap(x_c @ W_i.T + b_i)
            f_pre = _soft_cap(x_c @ W_f.T + b_f)
            o = jax.nn.sigmoid(x_t @ W_o.T + b_o)

            def step(carry, inp):
                c, n, m = carry
                qt, kt, vt, it, ft = inp
                m_t = jnp.maximum(ft + m, it)
                ie = jnp.exp(it - m_t)
                fe = jnp.exp(ft - m_t + m)
                c = fe[:, :, None, None] * c + ie[:, :, None, None] * jnp.einsum('bhd,bhe->bhde', vt, kt)
                n = fe[:, :, None] * n + ie[:, :, None] * kt
                num = jnp.einsum('bhde,bhe->bhd', c, qt)
                den = jnp.maximum(jnp.sum(n * qt, -1, keepdims=True), 1.0)
                return ((c, n, m_t), num / den)
            c0 = jnp.zeros((Bs, H, HD, HD), x.dtype)
            n0 = jnp.ones((Bs, H, HD), x.dtype)
            m0 = jnp.zeros((Bs, H), x.dtype)
            seq = tuple((jnp.moveaxis(a, 1, 0) for a in (q, k, v, i_pre, f_pre)))
            _, hs = jax.lax.scan(step, (c0, n0, m0), seq)
            h = o * jnp.moveaxis(hs, 0, 1).reshape(Bs, Sl, HID)
            hn = _layernorm(h.reshape(Bs, Sl, H, HD), mh_g, mh_b).reshape(Bs, Sl, HID)
            out = (hn + x_skip) * jax.nn.silu(r_t)
            return out @ W_down.T + b_down + x
        return _forward(x, ln_g, ln_b, mh_g, mh_b, W_up_l, b_up_l, W_up_r, b_up_r, W_down, b_down, conv_w, conv_b, W_skip, b_skip, W_i, b_i, W_f, b_f, W_o, b_o, W_q, b_q, W_k, b_k, W_v, b_v)

    def _L0_ffn_ref(x, w_router, w1, b1, w2, b2):
        import jax, jax.numpy as jnp
        import numpy as np
        B, S, H, F, E = (2, 256, 128, 512, 8)
        'Top-1 MoE layer: route -> per-expert FFN -> weighted combine.\n\n            Faithful to ExpertParallelWrapper._process_moe_layer on a single group:\n            router picks one expert per token with a routing weight; tokens are\n            dispatched to experts (here expressed as a static mask over the fixed\n            expert set), processed by the expert FFN, and scatter-combined back\n            weighted by the routing probability.\n            '
        Bs, Ss, Hs = x.shape
        n_experts = w1.shape[0]
        logits = jnp.einsum('bsh,he->bse', x, w_router)
        probs = jax.nn.softmax(logits, axis=-1)
        sel = jnp.argmax(probs, axis=-1)
        wgt = jnp.take_along_axis(probs, sel[..., None], axis=-1)[..., 0]
        xt = x.reshape(-1, Hs)
        sel_t = sel.reshape(-1)
        wgt_t = wgt.reshape(-1)
        out = jnp.zeros_like(xt)
        for e in range(n_experts):
            h = jax.nn.relu(xt @ w1[e] + b1[e])
            y = h @ w2[e] + b2[e]
            m = (sel_t == e).astype(xt.dtype) * wgt_t
            out = out + m[:, None] * y
        return out.reshape(Bs, Ss, Hs)
    x = L0_attn_x
    x = x + 0.5 * _L0_ffn_ref(_layernorm(x, axis=-1), L0_ffn_w_router, L0_ffn_w1, L0_ffn_b1, L0_ffn_w2, L0_ffn_b2)
    x = x + _L0_attn_ref(_layernorm(x, axis=-1), L0_attn_ln_g, L0_attn_ln_b, L0_attn_mh_g, L0_attn_mh_b, L0_attn_W_up_l, L0_attn_b_up_l, L0_attn_W_up_r, L0_attn_b_up_r, L0_attn_W_down, L0_attn_b_down, L0_attn_conv_w, L0_attn_conv_b, L0_attn_W_skip, L0_attn_b_skip, L0_attn_W_i, L0_attn_b_i, L0_attn_W_f, L0_attn_b_f, L0_attn_W_o, L0_attn_b_o, L0_attn_W_q, L0_attn_b_q, L0_attn_W_k, L0_attn_b_k, L0_attn_W_v, L0_attn_b_v)
    x = x + 0.5 * _L0_ffn_ref(_layernorm(x, axis=-1), L0_ffn_w_router, L0_ffn_w1, L0_ffn_b1, L0_ffn_w2, L0_ffn_b2)
    return x

_drawn_inputs = setup_inputs


def setup_inputs(seed=0):
    import zlib

    import numpy as np

    out = dict(_drawn_inputs(seed))
    spreads = {'L0_attn_ln_g': (1.0, 0.2),
     'L0_attn_ln_b': (0.0, 0.1),
     'L0_attn_mh_g': (1.0, 0.2),
     'L0_attn_mh_b': (0.0, 0.1),
     'L0_attn_b_up_l': (0.0, 0.1),
     'L0_attn_b_up_r': (0.0, 0.1),
     'L0_attn_b_down': (0.0, 0.1),
     'L0_attn_b_skip': (0.0, 0.27),
     'L0_attn_b_i': (0.0, 0.8),
     'L0_attn_b_f': (0.0, 0.1),
     'L0_attn_b_o': (0.0, 0.715),
     'L0_attn_b_q': (0.0, 0.1),
     'L0_attn_b_k': (0.0, 0.1),
     'L0_attn_b_v': (0.0, 0.1),
     'L0_ffn_b1': (0.0, 0.8),
     'L0_ffn_b2': (0.0, 0.624)}
    factors = {'L0_ffn_w_router': 3.701, 'L0_ffn_w1': 7.197, 'L0_ffn_w2': 5.593}
    for name, (base, spread) in spreads.items():
        noise = np.random.default_rng([zlib.crc32(name.encode()), seed]).standard_normal(out[name].shape)
        drawn = base * np.exp(spread * noise) if base else spread * noise
        out[name] = jnp.asarray(drawn.astype(out[name].dtype))
    for name, factor in factors.items():
        out[name] = (out[name] * factor).astype(out[name].dtype)
    return out
```

```python
from contextlib import ExitStack

import concourse.bass as bass
from concourse import mybir

F32 = mybir.dt.float32
BF16 = mybir.dt.bfloat16
I32 = mybir.dt.int32
U32 = mybir.dt.uint32
ALU = mybir.AluOpType
ACT = mybir.ActivationFunctionType
AX_X = mybir.AxisListType.X

P = 128
D = 128
NT = 16
NB = 4
NC = 4
S = NC * P
NE = 8
F = 512
FC = F // P
NBLK = NT + NE - 1
W1C = F + FC
H = 8
HD = 64
HID = H * HD
NP_ = H // 2
CAP = 15.0
NEG = -1.0e30

CONST = {}
_at = 0
for _n, _w in (("ident", 128), ("tri", 128), ("ones", 128), ("mask", 512), ("sel", 1024), ("decl", 128),
               ("decr", 4), ("rev", 8), ("thr", 16), ("blk", 24), ("reset", 512), ("reset16", 128)):
    CONST[_n] = (_at, _w)
    _at += _w
NCONST = _at
COL = {"g": 0, "b": 1, "bshift": 2, "bul": 10, "bq": 12, "bk": 16, "bif": 20}
NCOL = 21
ROW = {"bv": 0, "bo": 512, "br": 1024, "bsk": 1536, "mhb": 2048, "mhg": 2560, "bdown": 3072, "cw": 3200, "cb": 3204}
NROW = 3205


class Steps:

    def __init__(self, eng, sem):
        self.eng, self.sem, self.base, self.n = eng, sem, 0, 0

    def did(self, ins):
        ins.then_inc(self.sem, 1)
        self.n += 1

    def do(self, ins):
        self.did(ins)
        self.eng.wait_ge(self.sem, self.base + self.n)

    def settle(self):
        self.eng.wait_ge(self.sem, self.base + self.n)

    def loop(self, i, per):
        self.before = self.base + self.n
        self.base, self.n, self.per = self.before + i * per, 0, per

    def looped(self, count):
        assert self.n == self.per, (self.n, self.per)
        self.base, self.n = self.before + count * self.per, 0


def macaron(nc, x, consts, colpack, rowpack, w_router, w1, w2, b2, wul, wult, wurt, wqt, wkt, wskt, wvt, wot,
            wift, wdt, out):
    x_v = x.rearrange("(t p) d -> p t d", p=P)
    out_v = out.rearrange("(t p) d -> p t d", p=P)
    slots_x = nc.dram_tensor("slots_x", [NBLK * P, D], F32, kind="Internal").ap()
    slots_y = nc.dram_tensor("slots_y", [NBLK * P, D], F32, kind="Internal").ap()

    with ExitStack() as ctx:
        def sb(name, shape, dt=F32):
            return ctx.enter_context(nc.sbuf_tensor(name, shape, dt))

        def sem(name):
            return ctx.enter_context(nc.semaphore(name))

        bank = [ctx.enter_context(nc.psum_tensor(f"bank{i}", [P, 512], F32)) for i in range(8)]

        X = sb("X", [P, NT, D])
        K = sb("K", [P, NCONST])
        COLS = sb("COLS", [P, NCOL])
        ROWS = sb("ROWS", [P, NROW])
        W1 = sb("W1", [P, NE, W1C])
        W2 = sb("W2", [P, NE, FC, D])
        B2 = sb("B2", [P, NE, D])
        WR = sb("WR", [P, NE])
        WUL = sb("WUL", [P, 2, D])
        WULT = sb("WULT", [P, 3 + 256])
        WCT = sb("WCT", [P, 256])
        WURT = sb("WURT", [P, HID])
        WQT = sb("WQT", [P, 2, HID])
        WKT = sb("WKT", [P, 2, HID])
        WSKT = sb("WSKT", [P, 2, HID])
        WVT = sb("WVT", [P, 2, HID])
        WOT = sb("WOT", [P, 2, HID])
        WVF = sb("WVF", [P, HID])
        WOF = sb("WOF", [P, HID])
        WIFT = sb("WIFT", [P, 2, 40])
        WDT = sb("WDT", [P, FC, D])
        HBX = sb("HBX", [P, 2])
        BSH = sb("BSH", [P, 2, 4])
        IDB = sb("IDB", [P, P], BF16)
        MASKB = sb("MASKB", [P, 512], BF16)
        BULB = sb("BULB", [P, 2, P])

        def const(name):
            a, w = CONST[name]
            return K[:, a:a + w]

        def row(name, w):
            return ROWS[:, ROW[name]:ROW[name] + w]

        def col(name, i=0, lo=0, hi=P):
            return COLS[lo:hi, COL[name] + i:COL[name] + i + 1]

        ident = const("ident")

        XN = sb("XN", [P, NT, D])
        XNT = sb("XNT", [P, 4, 512])
        ST = sb("ST", [P, NT, 6])
        LNA = sb("LNA", [P, 8, NT])
        LG = sb("LG", [P, NT, NE])
        EX = sb("EX", [P, NT, NE])
        OH = sb("OH", [P, NT, NE])
        RT = sb("RT", [P, 8, NT])
        TOTE = sb("TOTE", [P, NE, NT])
        INCL = sb("INCL", [P, NE, NT])
        RK = sb("RK", [P, NT, NE])
        CMP = sb("CMP", [P, NE, NT])
        EB = sb("EB", [P, 8, NE])
        BE = sb("BE", [P, 24, NE])
        EIDF = sb("EIDF", [P, 24])
        EID = sb("EID", [P, 24], I32)
        POS = sb("POS", [P, NT], U32)
        MHALF = sb("MHALF", [P, NT])
        ZERO = sb("ZERO", [P, D])
        XB = sb("XB", [P, 2, D])
        XBT = sb("XBT", [P, 2, P])
        W1R = sb("W1R", [P, 2, W1C])
        HT = sb("HT", [P, 2, FC, P])
        YB = sb("YB", [P, 2, D])
        YG = XN

        ZB = sb("ZB", [P, 4, D])
        UB = sb("UB", [P, 4, D])
        SA = sb("SA", [P, 4, 6])
        LA = sb("LA", [P, 12, 4])
        XT = sb("XT", [P, 512])
        YH = XNT[:, 0:2, :]
        TH = XNT[:, 2:4, :]
        XC = sb("XC", [P, 2, 512])
        TIF = sb("TIF", [40, 512])
        F15 = sb("F15", [H, 512])
        FS = sb("FS", [H, 512])
        GT = sb("GT", [96, 512])
        MM = sb("MM", [H, 512])
        MIN = sb("MIN", [H, NC + 1])
        G3 = sb("G3", [H, NC])
        G3M = sb("G3M", [H, NC, NP_])
        QT = sb("QT", [P, 4, 512])
        KT = sb("KT", [P, 4, 512])
        AC = sb("AC", [P, NC, H])
        E12 = sb("E12", [P, NC, 2, H])
        DEC = sb("DEC", [P, NC, NP_])
        KW = sb("KW", [P, H, HD])
        VX = sb("VX", [P, H, HD + 1])
        OY = sb("OY", [P, HID])
        OT = sb("OT", [P, HID])
        RY = sb("RY", [P, HID])
        RTH = sb("RTH", [P, HID])
        GR = sb("GR", [P, HID])
        SK = sb("SK", [P, HID])
        DT = sb("DT", [P, 2, 4, P])
        PT = sb("PT", [P, 2, 4, P])
        CS = sb("CS", [P, NP_, HD + 1])
        HN = sb("HN", [P, H, HD + 1])
        DN = sb("DN", [P, 2, H])
        H2 = sb("H2", [P, H, HD])
        SQ = sb("SQ", [P, H, HD])
        HS = sb("HS", [P, 4, H])
        OUT = sb("OUT", [P, HID])
        OUTT = sb("OUTT", [P, FC, P])
        CREDIT = sb("CREDIT", [1, 8])

        x_loaded, consts_loaded, cols_loaded = sem("x_loaded"), sem("consts_loaded"), sem("cols_loaded")
        ffn_loaded, attn_loaded = sem("ffn_loaded"), sem("attn_loaded")
        zero_made, slots_cleared, out_stored = sem("zero_made"), sem("slots_cleared"), sem("out_stored")
        dve_step, pool_step = sem("dve_step"), sem("pool_step")

        def per_ffn(name):
            return [sem(f"{name}_{f}") for f in range(2)]

        var_ready, rstd_ready, xn_ready = per_ffn("var_ready"), per_ffn("rstd_ready"), per_ffn("xn_ready")
        xt_full, xt_copied, logits_full = per_ffn("xt_full"), per_ffn("xt_copied"), per_ffn("logits_full")
        shifted, exp_ready, onehot_ready = per_ffn("shifted"), per_ffn("exp_ready"), per_ffn("onehot_ready")
        ranks_full, pos_ready, scattered = per_ffn("ranks_full"), per_ffn("pos_ready"), per_ffn("scattered")
        eid_ready = per_ffn("eid_ready")
        xb_loaded = [[sem(f"xb_loaded_{f}_{i}") for i in range(2)] for f in range(2)]
        xbt_full, xbt_copied, w1_copied = per_ffn("xbt_full"), per_ffn("xbt_copied"), per_ffn("w1_copied")
        h_full, relu_act, relu_dve = per_ffn("h_full"), per_ffn("relu_act"), per_ffn("relu_dve")
        y_full, y_ready = per_ffn("y_full"), per_ffn("y_ready")
        y_stored = [[sem(f"y_stored_{f}_{i}") for i in range(2)] for f in range(2)]
        gathered = [[sem(f"gathered_{f}_{i}") for i in range(4)] for f in range(2)]
        ffn_done = per_ffn("ffn_done")
        folds_ready, fold_full, fold_copied = sem("folds_ready"), sem("fold_full"), sem("fold_copied")
        attn_consts = sem("attn_consts")

        a_var, a_rstd, z_ready, u_ready = sem("a_var"), sem("a_rstd"), sem("z_ready"), sem("u_ready")
        a_var2, a_rstd2, ubd_ready = sem("a_var2"), sem("a_rstd2"), sem("ubd_ready")
        pj_full, pj_free = sem("pj_full"), [sem(f"pj_free_{i}") for i in range(2)]
        tr_full, tr_free = sem("tr_full"), sem("tr_free")
        tanh_ready, xc_ready, rows_ready = sem("tanh_ready"), sem("xc_ready"), sem("rows_ready")
        ot_ready, rth_ready = sem("ot_ready"), sem("rth_ready")
        dm_full, decay_ready, st_full, pt_ready = sem("dm_full"), sem("decay_ready"), sem("st_full"), sem("pt_ready")
        hv_full, hv_read, cs_ready = sem("hv_full"), sem("hv_read"), sem("cs_ready")
        cen_ready, sq_ready, hvar_ready, hrstd_ready = (sem("cen_ready"), sem("sq_ready"), sem("hvar_ready"),
                                                        sem("hrstd_ready"))
        hn_ready, outg_ready = sem("hn_ready"), sem("outg_ready")

        PJ = bank[0:2]
        TR, DM = bank[2], bank[3]
        SB = bank[4:6]
        NB_ = bank[6:8]
        NPJ = 12 + 4 * NC
        NTR = 1 + 4 * NC

        def pj_read_at(b, u):
            return pj_free[u % 2], b * (NPJ // 2) + u // 2 + 2

        def tr_read_at(b, u):
            return tr_free, b * NTR + u + 2

        block = ctx.enter_context(nc.Block())

        @block.sync
        def _(sp):
            sp.dma_start(X[:, :, :], x_v).then_inc(x_loaded, 16)
            sp.dma_start(K[:, :], consts).then_inc(consts_loaded, 16)
            sp.dma_start(WR[:, :], w_router).then_inc(consts_loaded, 16)
            sp.dma_start(COLS[:, :], colpack).then_inc(cols_loaded, 16)
            sp.dma_start(ROWS[:, :], rowpack.partition_broadcast(P)).then_inc(cols_loaded, 16)
            sp.wait_ge(zero_made, 1)
            sp.dma_start(slots_x.rearrange("(k p) d -> p k d", p=P),
                         ZERO[:, :].unsqueeze(1).to_broadcast([P, NBLK, D])).then_inc(slots_cleared, 16)
            sp.dma_start(W1[:, :, :], w1).then_inc(ffn_loaded, 16)
            sp.dma_start(W2[:, :, :, :], w2).then_inc(ffn_loaded, 16)
            sp.dma_start(B2[:, :, :], b2.partition_broadcast(P)).then_inc(ffn_loaded, 16)

            def load_block(f, k, par):
                sp.dma_start(XB[:, par, :], slots_x[bass.ds(k * P, P), :]).then_inc(xb_loaded[f][par], 16)

            def block_io(f, k, par, more):
                if more:
                    sp.wait_ge(xbt_full[f], k + 1)
                    load_block(f, k + 2, par)
                sp.wait_ge(y_ready[f], k + 1)
                sp.dma_start(slots_y[bass.ds(k * P, P), :], YB[:, par, :]).then_inc(y_stored[f][par], 16)

            for f in range(2):
                sp.wait_ge(scattered[f], 16 * NT)
                load_block(f, 0, 0)
                load_block(f, 1, 1)
                with sp.Fori(0, NBLK // 2 - 1) as i:
                    block_io(f, 2 * i, 0, True)
                    block_io(f, 2 * i + 1, 1, True)
                block_io(f, NBLK - 3, 0, True)
                block_io(f, NBLK - 2, 1, False)
                block_io(f, NBLK - 1, 0, False)
            with sp.Fori(0, NT // 4) as g:
                sp.wait_ge(ffn_done[1], 4 * g + 4)
                sp.dma_start(out_v[:, bass.ds(g * 4, 4), :], X[:, bass.ds(g * 4, 4), :]).then_inc(out_stored, 16)
            sp.wait_ge(out_stored, 16 * (NT // 4))

        @block.gpsimd
        def _(pool):
            g = nc.gpsimd
            step = Steps(pool, pool_step)
            g.memset(ZERO[:, :], 0.0).then_inc(zero_made, 1)
            step.do(g.memset(MHALF[:, :], -0.5))

            def ffn(f):
                pool.wait_ge(var_ready[f], 1)
                g.tensor_tensor(LNA[:, 5, :], LNA[:, 4, :], MHALF[:, :], ALU.pow).then_inc(rstd_ready[f], 1)
                pool.wait_ge(slots_cleared, 16)
                pool.wait_ge(pos_ready[f], 1)
                for t in range(NT):
                    g.indirect_dma_start(out=slots_x, out_offset=bass.IndirectOffsetOnAxis(ap=POS[:, t:t + 1], axis=0),
                                         in_=XN[:, t, :], in_offset=None).then_inc(scattered[f], 16)
                pool.wait_ge(ffn_loaded, 48)
                pool.wait_ge(eid_ready[f], 1)

                def copy_w1(k, par):
                    e = pool.value_load(EID[0:1, bass.ds(k, 1)], min_val=0, max_val=NE - 1)
                    g.tensor_copy(W1R[:, par, :], W1[:, e, :]).then_inc(w1_copied[f], 1)

                copy_w1(0, 0)
                copy_w1(1, 1)
                def next_w1(k, par):
                    pool.wait_ge(relu_act[f], k + 1)
                    pool.wait_ge(relu_dve[f], k + 1)
                    copy_w1(k + 2, par)

                with pool.Fori(0, NBLK // 2 - 1) as i:
                    next_w1(2 * i, 0)
                    next_w1(2 * i + 1, 1)
                next_w1(NBLK - 3, 0)
                pool.wait_ge(y_stored[f][0], 16 * (NBLK // 2 + 1))
                pool.wait_ge(y_stored[f][1], 16 * (NBLK // 2))
                for t in range(NT):
                    g.indirect_dma_start(out=YG[:, t, :], out_offset=None, in_=slots_y,
                                         in_offset=bass.IndirectOffsetOnAxis(ap=POS[:, t:t + 1], axis=0),
                                         ).then_inc(gathered[f][t // 4], 16)

            ffn(0)
            pool.wait_ge(cols_loaded, 32)
            with pool.Fori(0, NB) as b:
                step.loop(b, 2 * NC)
                pool.wait_ge(a_var, b + 1)
                g.tensor_tensor(LA[:, 5, :], LA[:, 4, :], MHALF[:, 0:4], ALU.pow).then_inc(a_rstd, 1)
                pool.wait_ge(a_var2, b + 1)
                g.tensor_tensor(LA[:, 8, :], LA[:, 7, :], MHALF[:, 0:4], ALU.pow).then_inc(a_rstd2, 1)
                pool.wait_ge(z_ready, b + 1)
                g.tensor_tensor(UB[:, :, :], UB[:, :, :],
                                row("bdown", D).unsqueeze(1).to_broadcast([P, 4, D]), ALU.add).then_inc(ubd_ready, 1)
                for c in range(NC):
                    n = b * NC + c
                    pool.wait_ge(hvar_ready, n + 1)
                    step.do(g.tensor_tensor(HS[:, 3, :], HS[:, 2, :], MHALF[:, 0:H], ALU.pow))
                    step.do(g.tensor_tensor(H2[:, :, :], H2[:, :, :],
                                            HS[:, 3, :].unsqueeze(2).to_broadcast([P, H, HD]), ALU.mult))
                    g.tensor_tensor(H2[:, :, :], H2[:, :, :],
                                    row("mhg", HID).rearrange("p (h d) -> p h d", h=H), ALU.mult).then_inc(hn_ready, 1)
            step.looped(NB)
            ffn(1)

        @block.scalar
        def _(act):
            a = nc.scalar
            for dst, src in ((WUL[:, :, :], wul), (WULT[:, :], wult), (WURT[:, :], wurt), (WQT[:, :, :], wqt),
                             (WKT[:, :, :], wkt), (WSKT[:, :, :], wskt), (WVT[:, :, :], wvt), (WOT[:, :, :], wot),
                             (WIFT[:, :, :], wift), (WDT[:, :, :], wdt)):
                act.dma_start(dst, src).then_inc(attn_loaded, 16)

            def ffn(f):
                for q in range(4):
                    act.wait_ge(xt_full[f], q + 1)
                    a.activation(XNT[:, q, :], bank[q % 2][:, :], ACT.Copy).then_inc(xt_copied[f], 1)
                act.wait_ge(shifted[f], 1)
                a.activation(EX[:, :, :], EX[:, :, :], ACT.Exp).then_inc(exp_ready[f], 1)
                if f == 0:
                    for i, dst in enumerate((WVF, WOF)):
                        act.wait_ge(fold_full, 2 * i + 1)
                        a.activation(dst[:, :], bank[4 + 2 * i][:, :], ACT.Copy).then_inc(fold_copied, 1)

                def blk(k, par):
                    act.wait_ge(xbt_full[f], k + 1)
                    a.activation(XBT[:, par, :], bank[par][:, 0:P], ACT.Copy).then_inc(xbt_copied[f], 1)
                    act.wait_ge(h_full[f], 2 * k + 1)
                    for c in range(2):
                        ins = a.activation(HT[:, par, c, :], bank[2 + par][:, c * P:(c + 1) * P], ACT.Relu,
                                           bias=W1R[:, par, F + c:F + c + 1])
                    ins.then_inc(relu_act[f], 1)

                with act.Fori(0, NBLK // 2) as i:
                    blk(2 * i, 0)
                    blk(2 * i + 1, 1)
                blk(NBLK - 1, 0)

            ffn(0)
            act.wait_ge(attn_consts, 1)
            with act.Fori(0, NB) as b:
                act.wait_ge(pj_full, b * NPJ + 1)
                a.activation(XT[:, :], PJ[0][:, :], ACT.Identity, scale=col("g"), bias=col("b"))\
                 .then_inc(pj_free[0], 1)
                act.wait_ge(xc_ready, b + 1)
                for j in range(2):
                    act.wait_ge(pj_full, b * NPJ + 2 + j)
                    a.activation(YH[:, j, :], PJ[(1 + j) % 2][:, :], ACT.Identity, scale=0.5,
                                 bias=HBX[:, j:j + 1]).then_inc(pj_free[(1 + j) % 2], 1)
                act.wait_ge(*pj_read_at(b, 1))
                act.wait_ge(*pj_read_at(b, 2))
                a.activation(TH[:, :, :], YH[:, :, :], ACT.Tanh).then_inc(tanh_ready, 1)
                act.wait_ge(pj_full, b * NPJ + 4)
                a.activation(TIF[0:H, :], PJ[1][0:H, :], ACT.Tanh, scale=1.0 / CAP, bias=col("bif", 0, 0, H))
                a.activation(TIF[32:32 + H, :], PJ[1][32:32 + H, :], ACT.Tanh, scale=1.0 / CAP,
                             bias=col("bif", 0, 32, 32 + H)).then_inc(pj_free[1], 1)
                for m in range(4):
                    act.wait_ge(pj_full, b * NPJ + 5 + m)
                    a.activation(QT[:, m, :], PJ[m % 2][:, :], ACT.Identity, bias=col("bq", m))\
                     .then_inc(pj_free[m % 2], 1)
                act.wait_ge(tr_full, b * NTR + 1)
                cols = TR[:, 0:NC * 96].rearrange("p (c q r) -> p c q r", c=NC, q=3)
                a.activation(AC[:, :, :], cols[:, :, 0, 0:H], ACT.Copy)
                a.activation(E12[:, :, :, :], cols[:, :, 1:3, 0:H], ACT.Exp)
                a.activation(DEC[:, :, :], TR[:, 384:384 + NC * NP_].rearrange("p (c m) -> p c m", c=NC), ACT.Exp)\
                    .then_inc(tr_free, 1)
                act.wait_ge(*tr_read_at(b, 0))
                for c in range(NC):
                    n = b * NC + c
                    for hf in range(2):
                        act.wait_ge(dm_full, 2 * n + hf + 1)
                        act.wait_ge(pt_ready, 2 * n + 1)
                        for m in range(4):
                            h = 2 * m + hf
                            ins = a.activation(DT[:, hf, m, :], DM[:, m * P:(m + 1) * P], ACT.Exp,
                                               bias=AC[:, c, h:h + 1])
                        ins.then_inc(decay_ready, 1)
                    act.wait_ge(*pj_read_at(b, 12 + 4 * c + 1))
                    a.activation(OT[:, :], OY[:, :], ACT.Tanh, scale=0.5).then_inc(ot_ready, 1)
                    act.wait_ge(*pj_read_at(b, 12 + 4 * c + 2))
                    a.activation(RTH[:, :], RY[:, :], ACT.Tanh, scale=0.5).then_inc(rth_ready, 1)
                    act.wait_ge(cen_ready, n + 1)
                    a.activation(SQ[:, :, :], H2[:, :, :], ACT.Square).then_inc(sq_ready, 1)
                    act.wait_ge(tr_full, b * NTR + 1 + 4 * c + 3)
                    a.activation(OUTT[:, :, :].rearrange("p m t -> p (m t)"), TR[:, :], ACT.Copy)\
                        .then_inc(tr_free, 1)
            ffn(1)

        @block.tensor
        def _(pe):
            t_ = nc.tensor

            def mm(o, l, r, start=True, stop=True):
                return t_.matmul(o, l, r, start=start, stop=stop, skip_group_check=True)

            def ffn(f):
                pe.wait_ge(consts_loaded, 32)
                for q in range(4):
                    pe.wait_ge(xn_ready[f], 4 * q + 4)
                    if q >= 2:
                        pe.wait_ge(xt_copied[f], q - 1)
                    for j in range(4):
                        ins = t_.transpose(bank[q % 2][:, j * P:(j + 1) * P], XN[:, 4 * q + j, :], ident)
                    ins.then_inc(xt_full[f], 1)
                for q in range(4):
                    pe.wait_ge(xt_copied[f], q + 1)
                    for j in range(4):
                        t = 4 * q + j
                        ins = mm(bank[2][:, t * NE:(t + 1) * NE], XNT[:, q, j * P:(j + 1) * P], WR[:, :])
                ins.then_inc(logits_full[f], 1)
                pe.wait_ge(onehot_ready[f], 1)
                oh = OH[:, :, :].rearrange("p t e -> p (t e)")
                mm(bank[3][:, 0:P], const("tri"), oh)
                mm(bank[3][:, P:2 * P], const("ones"), oh).then_inc(ranks_full[f], 1)
                if f == 0:
                    pe.wait_ge(attn_loaded, 160)
                    pe.wait_ge(folds_ready, 1)
                    for i, w in enumerate((WVT, WOT)):
                        for j in range(2):
                            ins = mm(bank[4 + 2 * i][:, :], WUL[:, j, :], w[:, j, :], j == 0, j == 1)
                        ins.then_inc(fold_full, 1)
                        for j in range(2):
                            ins = mm(bank[5 + 2 * i][:, :], BULB[:, j, :], w[:, j, :], j == 0, j == 1)
                        ins.then_inc(fold_full, 1)
                    pe.wait_ge(fold_copied, 2)
                    pe.wait_ge(attn_consts, 1)
                pe.wait_ge(ffn_loaded, 48)
                pe.wait_ge(eid_ready[f], 1)

                def up(k, par, first=False):
                    pe.wait_ge(xb_loaded[f][par], 16 * ((k - par) // 2 + 1) if isinstance(k, int)
                               else 8 * (k - par) + 16)
                    t_.transpose(bank[par][:, 0:P], XB[:, par, :], ident).then_inc(xbt_full[f], 1)
                    pe.wait_ge(xbt_copied[f], k + 1)
                    pe.wait_ge(w1_copied[f], k + 1)
                    if not first:
                        pe.wait_ge(relu_act[f], k - 1)
                        pe.wait_ge(relu_dve[f], k - 1)
                    for c in range(FC):
                        ins = mm(bank[2 + par + 2 * (c // 2)][:, (c % 2) * P:(c % 2 + 1) * P],
                                 W1R[:, par, c * P:(c + 1) * P], XBT[:, par, :])
                        if c % 2:
                            ins.then_inc(h_full[f], 1)

                def down(k, par, first=False):
                    e = pe.value_load(EID[0:1, bass.ds(k, 1)], min_val=0, max_val=NE - 1)
                    pe.wait_ge(relu_act[f], k + 1)
                    pe.wait_ge(relu_dve[f], k + 1)
                    if not first:
                        pe.wait_ge(y_ready[f], k - 1)
                    for c in range(FC):
                        ins = mm(bank[6 + par][:, 0:D], HT[:, par, c, :], W2[:, e, c, :], c == 0, c == FC - 1)
                    ins.then_inc(y_full[f], 1)

                up(0, 0, True)
                up(1, 1, True)
                down(0, 0, True)
                up(2, 0)
                down(1, 1, True)
                with pe.Fori(1, NBLK // 2) as i:
                    up(2 * i + 1, 1)
                    down(2 * i, 0)
                    up(2 * i + 2, 0)
                    down(2 * i + 1, 1)
                down(NBLK - 1, 0)

            ffn(0)

            with pe.Fori(0, NB) as b:
                def pj_wait(u):
                    pe.wait_ge(pj_free[u % 2], b * (NPJ // 2) + u // 2 + 1)
                    return PJ[u % 2]

                def tr_wait(u):
                    pe.wait_ge(tr_free, b * NTR + u + 1)
                    return TR

                pe.wait_ge(z_ready, b + 1)
                dst = pj_wait(0)
                for j in range(4):
                    ins = t_.transpose(dst[:, j * P:(j + 1) * P], ZB[:, j, :], ident)
                ins.then_inc(pj_full, 1)
                pe.wait_ge(*pj_read_at(b, 0))
                for j in range(2):
                    mm(pj_wait(1 + j)[:, :], WCT[:, j * P:(j + 1) * P], XT[:, :]).then_inc(pj_full, 1)
                pe.wait_ge(xc_ready, b + 2)
                dst = pj_wait(3)
                for j in range(2):
                    ins = mm(dst[0:40, :], WIFT[:, j, :], XC[:, j, :], j == 0, j == 1)
                ins.then_inc(pj_full, 1)
                for w, u0 in ((WQT, 4), (WKT, 8)):
                    for m in range(4):
                        dst = pj_wait(u0 + m)
                        for j in range(2):
                            ins = mm(dst[:, :], w[:, j, m * P:(m + 1) * P], XC[:, j, :], j == 0, j == 1)
                        ins.then_inc(pj_full, 1)
                pe.wait_ge(rows_ready, b + 1)
                dst = tr_wait(0)
                for c in range(NC):
                    t_.transpose(dst[:, c * 96:(c + 1) * 96], GT[:, c * P:(c + 1) * P], ident[0:96, 0:96])
                mm(dst[:, 384:384 + NC * NP_], const("decl")[0:H, :], G3M[:, :, :].rearrange("p c m -> p (c m)"))\
                    .then_inc(tr_full, 1)
                pe.wait_ge(*pj_read_at(b, 10))
                pe.wait_ge(*pj_read_at(b, 11))
                for c in range(NC):
                    n = b * NC + c
                    at = slice(c * P, (c + 1) * P)
                    u = 12 + 4 * c
                    dst = tr_wait(1 + 4 * c)
                    for m in range(4):
                        ins = t_.transpose(dst[:, m * P:(m + 1) * P], KT[:, m, at], ident)
                    ins.then_inc(tr_full, 1)
                    mm(pj_wait(u)[:, :], XT[:, at], WVF[:, :]).then_inc(pj_full, 1)
                    mm(pj_wait(u + 1)[:, :], XT[:, at], WOF[:, :]).then_inc(pj_full, 1)
                    mm(pj_wait(u + 2)[:, :], XT[:, at], WURT[:, :]).then_inc(pj_full, 1)
                    dst = pj_wait(u + 3)
                    for j in range(2):
                        ins = mm(dst[:, :], XC[:, j, at], WSKT[:, j, :], j == 0, j == 1)
                    ins.then_inc(pj_full, 1)
                    for hf in range(2):
                        rows = slice(hf * HD, (hf + 1) * HD)
                        pe.wait_ge(decay_ready, 2 * n + hf + 1)
                        mm(DM[:, :], IDB[:, :], MASKB[:, :], True, False)
                        for m in range(4):
                            ins = mm(DM[:, m * P:(m + 1) * P],
                                     const("sel")[0:H, (2 * m + hf) * P:(2 * m + hf + 1) * P], MM[:, at], False, m == 3)
                        ins.then_inc(dm_full, 1)
                        pe.wait_ge(hv_read, 2 * n + 1)
                        for m in range(4):
                            ins = mm(SB[hf][:, m * P:(m + 1) * P], KT[rows, m, at], QT[rows, m, at])
                        ins.then_inc(st_full, 1)
                    if c == 0:
                        pe.wait_ge(cs_ready, b + 1)
                    else:
                        pe.wait_ge(*tr_read_at(b, 2 + 4 * (c - 1)))
                    for hf in range(2):
                        rows = slice(hf * HD, (hf + 1) * HD)
                        for m in range(4):
                            mm(NB_[hf][:, m * 65:(m + 1) * 65], QT[rows, m, at], CS[rows, m, :])
                    pe.wait_ge(*tr_read_at(b, 1 + 4 * c))
                    pe.wait_ge(*pj_read_at(b, u))
                    dst = tr_wait(2 + 4 * c)
                    for h in range(H):
                        rows = slice((h % 2) * HD, (h % 2 + 1) * HD)
                        ins = mm(dst[rows, (h // 2) * 65:(h // 2 + 1) * 65], KW[:, h, :], VX[:, h, :])
                    ins.then_inc(tr_full, 1)
                    for hf in range(2):
                        pe.wait_ge(pt_ready, 2 * n + hf + 2)
                        for m in range(4):
                            ins = mm(SB[hf][:, m * 65:(m + 1) * 65], PT[:, hf, m, :], VX[:, 2 * m + hf, :])
                        ins.then_inc(hv_full, 1)
                    pe.wait_ge(outg_ready, n + 1)
                    dst = tr_wait(3 + 4 * c)
                    for m in range(4):
                        ins = t_.transpose(dst[:, m * P:(m + 1) * P], OUT[:, m * P:(m + 1) * P], ident)
                    ins.then_inc(tr_full, 1)
                    pe.wait_ge(*tr_read_at(b, 3 + 4 * c))
                    dst = tr_wait(4 + 4 * c)
                    for m in range(4):
                        ins = mm(dst[:, 0:D], OUTT[:, m, :], WDT[:, m, :], m == 0, m == 3)
                    ins.then_inc(tr_full, 1)
            ffn(1)

        @block.vector
        def _(dve):
            v = nc.vector
            step = Steps(dve, dve_step)
            do, did = step.do, step.did

            def bc(ap, shape):
                return ap.unsqueeze(len(ap.shape)).to_broadcast(shape)

            def moments(st, w, n):
                did(v.tensor_tensor(w[:, 0, :], st[:, :, 1], st[:, :, 4], ALU.add))
                did(v.tensor_tensor(w[:, 1, :], st[:, :, 1], st[:, :, 4], ALU.subtract))
                do(v.tensor_tensor(w[:, 2, :], st[:, :, 2], st[:, :, 5], ALU.add))
                did(v.tensor_scalar(w[:, 0, :], w[:, 0, :], 0.5, None, ALU.mult))
                do(v.scalar_tensor_tensor(out=w[:, 1, :], in0=w[:, 1, :], scalar=0.25, in1=w[:, 1, :],
                                          op0=ALU.mult, op1=ALU.mult))
                do(v.scalar_tensor_tensor(out=w[:, 3, :], in0=w[:, 2, :], scalar=1.0 / n, in1=w[:, 1, :],
                                          op0=ALU.mult, op1=ALU.add))

            def ffn(f):
                with dve.Fori(0, NT) as t:
                    step.loop(t, 1)
                    did(v.bn_stats(ST[:, t, :], X[:, t, :]))
                step.looped(NT)
                step.settle()
                moments(ST, LNA, D)
                v.tensor_scalar(LNA[:, 4, :], LNA[:, 3, :], 1e-5, None, ALU.add).then_inc(var_ready[f], 1)
                dve.wait_ge(rstd_ready[f], 1)
                with dve.Fori(0, NT) as t:
                    v.tensor_scalar(XN[:, t, :], X[:, t, :], LNA[:, 0, bass.ds(t, 1)], LNA[:, 5, bass.ds(t, 1)],
                                    ALU.subtract, ALU.mult).then_inc(xn_ready[f], 1)
                dve.wait_ge(logits_full[f], 1)
                dve.wait_ge(consts_loaded, 32)
                do(v.tensor_copy(LG[:, :, :].rearrange("p t e -> p (t e)"), bank[2][:, 0:NT * NE]))
                do(v.tensor_reduce(RT[:, 0, :], LG[:, :, :], AX_X, ALU.max))
                v.tensor_tensor(EX[:, :, :], LG[:, :, :], bc(RT[:, 0, :], [P, NT, NE]), ALU.subtract)\
                    .then_inc(shifted[f], 1)
                do(v.tensor_tensor(OH[:, :, :], LG[:, :, :], bc(RT[:, 0, :], [P, NT, NE]), ALU.is_equal))
                rev = const("rev").unsqueeze(1).to_broadcast([P, NT, NE])
                do(v.tensor_tensor(OH[:, :, :], OH[:, :, :], rev, ALU.mult))
                do(v.tensor_reduce(RT[:, 1, :], OH[:, :, :], AX_X, ALU.max))
                v.tensor_tensor(OH[:, :, :], rev, bc(RT[:, 1, :], [P, NT, NE]), ALU.is_equal)\
                    .then_inc(onehot_ready[f], 1)
                dve.wait_ge(exp_ready[f], 1)
                do(v.tensor_reduce(RT[:, 2, :], EX[:, :, :], AX_X, ALU.add))
                do(v.reciprocal(RT[:, 3, :], RT[:, 2, :]))
                did(v.tensor_scalar(RT[:, 3, :], RT[:, 3, :], 0.5, None, ALU.mult))
                dve.wait_ge(ranks_full[f], 1)
                do(v.tensor_copy(TOTE[:, :, :], bank[3][:, P:2 * P].rearrange("p (t e) -> p e t", e=NE)))
                do(v.tensor_tensor_scan(INCL[:, :, :].rearrange("p e t -> p (e t)"), const("reset16"),
                                        TOTE[:, :, :].rearrange("p e t -> p (e t)"), 0.0, ALU.mult, ALU.add))
                do(v.tensor_tensor(CMP[:, :, :], bc(INCL[:, :, NT - 1], [P, NE, NT]),
                                   const("thr").unsqueeze(1).to_broadcast([P, NE, NT]), ALU.is_gt))
                do(v.tensor_reduce(EB[:, 0, :], CMP[:, :, :], AX_X, ALU.add))
                do(v.tensor_tensor_scan(EB[:, 1, :], const("ones")[:, 0:NE], EB[:, 0, :], 0.0, ALU.mult, ALU.add))
                did(v.tensor_tensor(EB[:, 2, :], EB[:, 1, :], EB[:, 0, :], ALU.subtract))
                do(v.tensor_tensor(INCL[:, :, :], INCL[:, :, :], TOTE[:, :, :], ALU.subtract))
                do(v.tensor_scalar(EB[:, 2, :], EB[:, 2, :], float(P), None, ALU.mult))
                do(v.tensor_tensor(INCL[:, :, :], INCL[:, :, :], bc(EB[:, 2, :], [P, NE, NT]), ALU.add))
                do(v.tensor_tensor(RK[:, :, :], bank[3][:, 0:P].rearrange("p (t e) -> p t e", e=NE),
                                   INCL[:, :, :].rearrange("p e t -> p t e"), ALU.add))
                do(v.tensor_tensor(RK[:, :, :], RK[:, :, :], OH[:, :, :], ALU.mult))
                do(v.tensor_reduce(RT[:, 4, :], RK[:, :, :], AX_X, ALU.add))
                v.tensor_copy(POS[:, :], RT[:, 4, :]).then_inc(pos_ready[f], 1)
                do(v.tensor_tensor(BE[:, :, :], bc(const("blk"), [P, 24, NE]),
                                   EB[:, 1, :].unsqueeze(1).to_broadcast([P, 24, NE]), ALU.is_ge))
                do(v.tensor_reduce(EIDF[:, :], BE[:, :, :], AX_X, ALU.add))
                do(v.tensor_scalar(EIDF[:, :], EIDF[:, :], float(NE - 1), None, ALU.min))
                v.tensor_copy(EID[:, :], EIDF[:, :]).then_inc(eid_ready[f], 1)
                dve.wait_ge(eid_ready[f], 1)
                if f == 0:
                    attn_setup()
                dve.wait_ge(ffn_loaded, 48)

                relu_first(f)
                blk_pipe(f)
                for q in range(4):
                    dve.wait_ge(gathered[f][q], 64)
                with dve.Fori(0, NT) as t:
                    v.scalar_tensor_tensor(out=X[:, t, :], in0=YG[:, t, :], scalar=RT[:, 3, bass.ds(t, 1)],
                                           in1=X[:, t, :], op0=ALU.mult, op1=ALU.add).then_inc(ffn_done[f], 1)
                dve.wait_ge(ffn_done[f], NT)

            def relu(f, k, par):
                dve.wait_ge(h_full[f], 2 * k + 2)
                for c in range(2):
                    ins = v.tensor_scalar(HT[:, par, 2 + c, :], bank[4 + par][:, c * P:(c + 1) * P],
                                          W1R[:, par, F + 2 + c:F + 3 + c], 0.0, ALU.add, ALU.max)
                ins.then_inc(relu_dve[f], 1)

            def add_b2(f, k, par, first=False):
                e = dve.value_load(EID[0:1, bass.ds(k, 1)], min_val=0, max_val=NE - 1)
                dve.wait_ge(y_full[f], k + 1)
                if not first:
                    dve.wait_ge(y_stored[f][par], 8 * (k - par))
                v.tensor_tensor(YB[:, par, :], bank[6 + par][:, 0:D], B2[:, e, :], ALU.add).then_inc(y_ready[f], 1)

            def relu_first(f):
                relu(f, 0, 0)
                relu(f, 1, 1)
                add_b2(f, 0, 0, True)
                relu(f, 2, 0)
                add_b2(f, 1, 1, True)

            def blk_pipe(f):
                with dve.Fori(1, NBLK // 2) as i:
                    relu(f, 2 * i + 1, 1)
                    add_b2(f, 2 * i, 0)
                    relu(f, 2 * i + 2, 0)
                    add_b2(f, 2 * i + 1, 1)
                add_b2(f, NBLK - 1, 0)

            def attn_setup():
                dve.wait_ge(attn_loaded, 160)
                dve.wait_ge(cols_loaded, 32)
                for j in range(2):
                    ins = v.tensor_copy(BULB[:, j, :], col("bul", j).to_broadcast([P, P]))
                ins.then_inc(folds_ready, 1)
                did(v.tensor_copy(IDB[:, :], ident))
                did(v.tensor_copy(MASKB[:, :], const("mask")))
                do(v.tensor_scalar(WCT[:, :], WULT[:, 0:256], row("cw", 4)[:, 0:1], None, ALU.mult))
                for m in range(1, 4):
                    do(v.scalar_tensor_tensor(out=WCT[:, :], in0=WULT[:, m:m + 256], scalar=row("cw", 4)[:, m:m + 1],
                                              in1=WCT[:, :], op0=ALU.mult, op1=ALU.add))
                do(v.tensor_tensor(BSH[:, :, :], COLS[:, COL["bshift"]:COL["bshift"] + 8]
                                   .rearrange("p (j m) -> p j m", j=2),
                                   row("cw", 4).unsqueeze(1).to_broadcast([P, 2, 4]), ALU.mult))
                do(v.tensor_reduce(HBX[:, :], BSH[:, :, :], AX_X, ALU.add))
                did(v.tensor_scalar(HBX[:, :], HBX[:, :], row("cb", 1), 0.5, ALU.add, ALU.mult))
                did(v.tensor_scalar(WKT[:, :, :], WKT[:, :, :], HD ** -0.5, None, ALU.mult))
                did(v.tensor_scalar(COLS[:, COL["bk"]:COL["bk"] + 4], COLS[:, COL["bk"]:COL["bk"] + 4],
                                    HD ** -0.5, None, ALU.mult))
                did(v.tensor_scalar(WDT[:, :, :], WDT[:, :, :], 0.5, None, ALU.mult))
                did(v.tensor_scalar(col("bif"), col("bif"), 1.0 / CAP, None, ALU.mult))
                did(v.tensor_tensor(row("bsk", HID), row("bsk", HID), row("mhb", HID), ALU.add))
                did(v.memset(VX[:, :, :], 1.0))
                did(v.memset(GT[:, :], 0.0))
                for i, name in enumerate(("bv", "bo")):
                    dve.wait_ge(fold_full, 2 * i + 2)
                    did(v.tensor_tensor(row(name, HID), bank[5 + 2 * i][:, :], row(name, HID), ALU.add))
                for i, s in enumerate((*pj_free, tr_free, xc_ready, pt_ready, decay_ready, hv_read)):
                    v.memset(CREDIT[:, i:i + 1], 0.0).then_inc(s, 1)
                step.settle()
                v.memset(MIN[:, :], 0.0).then_inc(attn_consts, 1)
                dve.wait_ge(attn_consts, 1)

            dve.wait_ge(x_loaded, 16)
            ffn(0)

            ONCE, CH = 28, 12
            with dve.Fori(0, NB) as b:
                step.loop(b, ONCE + CH * NC)
                dve.wait_ge(*tr_read_at(b, -1))
                for j in range(4):
                    did(v.bn_stats(SA[:, j, :], X[:, bass.ds(b * 4 + j, 1), :].rearrange("p a d -> p (a d)")))
                step.settle()
                moments(SA, LA, D)
                v.tensor_scalar(LA[:, 4, :], LA[:, 3, :], 1e-5, None, ALU.add).then_inc(a_var, 1)
                dve.wait_ge(a_rstd, b + 1)
                do(v.tensor_tensor(LA[:, 6, :], LA[:, 5, :], LA[:, 5, :], ALU.mult))
                do(v.tensor_tensor(LA[:, 6, :], LA[:, 6, :], LA[:, 3, :], ALU.mult))
                v.tensor_scalar(LA[:, 7, :], LA[:, 6, :], 1e-6, None, ALU.add).then_inc(a_var2, 1)
                do(v.tensor_tensor(UB[:, :, :], X[:, bass.ds(b * 4, 4), :], bc(LA[:, 0, :], [P, 4, D]), ALU.subtract))
                v.tensor_tensor(UB[:, :, :], UB[:, :, :], bc(LA[:, 5, :], [P, 4, D]), ALU.mult).then_inc(u_ready, 1)
                dve.wait_ge(u_ready, b + 1)
                dve.wait_ge(a_rstd2, b + 1)
                v.tensor_tensor(ZB[:, :, :], UB[:, :, :], bc(LA[:, 8, :], [P, 4, D]), ALU.mult).then_inc(z_ready, 1)
                xs = X[:, bass.ds(b * 4, 4), :]
                dve.wait_ge(ubd_ready, b + 1)
                did(v.tensor_tensor(xs, xs, UB[:, :, :], ALU.add))
                did(v.memset(CS[:, :, 0:HD], 0.0))
                v.memset(CS[:, :, HD:HD + 1], 1.0).then_inc(cs_ready, 1)
                dve.wait_ge(tanh_ready, b + 1)
                v.scalar_tensor_tensor(out=XC[:, :, :], in0=TH, scalar=1.0, in1=YH,
                                       op0=ALU.add, op1=ALU.mult).then_inc(xc_ready, 1)
                dve.wait_ge(*pj_read_at(b, 3))
                do(v.tensor_scalar(F15[:, :], TIF[32:32 + H, :], CAP, None, ALU.mult))
                do(v.tensor_tensor_scan(FS[:, :], const("reset")[0:H, :], F15[:, :], 0.0, ALU.mult, ALU.add))
                do(v.scalar_tensor_tensor(out=GT[0:H, :], in0=TIF[0:H, :], scalar=CAP, in1=FS[:, :],
                                          op0=ALU.mult, op1=ALU.subtract))
                for c in range(NC):
                    at = slice(c * P, (c + 1) * P)
                    do(v.tensor_tensor_scan(MM[:, at], GT[0:H, at], GT[0:H, at], MIN[:, c:c + 1], ALU.max, ALU.max))
                    if c < NC - 1:
                        last = slice((c + 1) * P - 1, (c + 1) * P)
                        do(v.tensor_tensor(MIN[:, c + 1:c + 2], FS[:, last], MM[:, last], ALU.add))
                m4 = MM[:, :].rearrange("p (c t) -> p c t", c=NC)
                a4 = GT[0:H, :].rearrange("p (c t) -> p c t", c=NC)
                did(v.tensor_tensor(GT[32:32 + H, :].rearrange("p (c t) -> p c t", c=NC),
                                    bc(MIN[:, 0:NC], [H, NC, P]), m4, ALU.subtract))
                did(v.tensor_tensor(GT[64:64 + H, :].rearrange("p (c t) -> p c t", c=NC), a4,
                                    bc(m4[:, :, P - 1], [H, NC, P]), ALU.subtract))
                do(v.tensor_tensor(G3[:, :], MIN[:, 0:NC], m4[:, :, P - 1], ALU.subtract))
                v.tensor_tensor(G3M[:, :, :], bc(G3[:, :], [H, NC, NP_]),
                                const("decr")[0:H, :].unsqueeze(1).to_broadcast([H, NC, NP_]), ALU.mult)\
                    .then_inc(rows_ready, 1)
                for m in range(4):
                    dve.wait_ge(pj_full, b * NPJ + 9 + m)
                    v.tensor_scalar(KT[:, m, :], PJ[m % 2][:, :], col("bk", m), None, ALU.add)\
                        .then_inc(pj_free[m % 2], 1)
                dve.wait_ge(*tr_read_at(b, 0))
                assert step.n == ONCE, step.n
                for c in range(NC):
                    n = b * NC + c
                    dve.wait_ge(tr_full, b * NTR + 1 + 4 * c + 1)
                    v.tensor_tensor(KW[:, :, :], TR[:, :].rearrange("p (h d) -> p h d", h=H),
                                    bc(E12[:, c, 1, :], [P, H, HD]), ALU.mult).then_inc(tr_free, 1)
                    u = b * NPJ + 12 + 4 * c
                    dve.wait_ge(pj_full, u + 1)
                    v.tensor_tensor(VX[:, :, 0:HD], PJ[0][:, :].rearrange("p (h d) -> p h d", h=H),
                                    row("bv", HID).rearrange("p (h d) -> p h d", h=H), ALU.add)\
                        .then_inc(pj_free[0], 1)
                    dve.wait_ge(pj_full, u + 2)
                    v.tensor_tensor(OY[:, :], PJ[1][:, :], row("bo", HID), ALU.add)\
                        .then_inc(pj_free[1], 1)
                    dve.wait_ge(pj_full, u + 3)
                    v.tensor_tensor(RY[:, :], PJ[0][:, :], row("br", HID), ALU.add)\
                        .then_inc(pj_free[0], 1)
                    dve.wait_ge(pj_full, u + 4)
                    v.tensor_tensor(SK[:, :], PJ[1][:, :], row("bsk", HID), ALU.add).then_inc(pj_free[1], 1)
                    for hf in range(2):
                        dve.wait_ge(st_full, 2 * n + hf + 1)
                        dve.wait_ge(decay_ready, 2 * n + hf + 2)
                        v.tensor_tensor(PT[:, hf, :, :].rearrange("p m t -> p (m t)"), SB[hf][:, :],
                                        DT[:, hf, :, :].rearrange("p m t -> p (m t)"), ALU.mult).then_inc(pt_ready, 1)
                    dve.wait_ge(*pj_read_at(b, 12 + 4 * c + 2))
                    dve.wait_ge(rth_ready, n + 1)
                    did(v.scalar_tensor_tensor(out=GR[:, :], in0=RTH[:, :], scalar=1.0, in1=RY[:, :],
                                               op0=ALU.add, op1=ALU.mult))
                    for hf in range(2):
                        hn = HN[:, :, :].rearrange("p (m two) d -> p two m d", two=2)[:, hf]
                        e1 = E12[:, c, 0, :].rearrange("p (m two) -> p two m", two=2)[:, hf]
                        dve.wait_ge(hv_full, 2 * n + hf + 1)
                        do(v.tensor_tensor(hn, NB_[hf][:, 0:260].rearrange("p (m d) -> p m d", m=4),
                                           bc(e1, [P, 4, HD + 1]), ALU.mult))
                        v.tensor_tensor(hn, hn, SB[hf][:, 0:260].rearrange("p (m d) -> p m d", m=4), ALU.add)\
                         .then_inc(hv_read, 1)
                    dve.wait_ge(tr_full, b * NTR + 1 + 4 * c + 2)
                    do(v.tensor_tensor(CS[:, :, :], CS[:, :, :], bc(DEC[:, c, :], [P, NP_, HD + 1]), ALU.mult))
                    v.tensor_tensor(CS[:, :, :], CS[:, :, :], TR[:, 0:260].rearrange("p (m d) -> p m d", m=4),
                                    ALU.add).then_inc(tr_free, 1)
                    dve.wait_ge(*tr_read_at(b, 2 + 4 * c))
                    dve.wait_ge(hv_read, 2 * n + 3)
                    do(v.tensor_scalar(DN[:, 0, :], HN[:, :, HD], 1.0, 2.0, ALU.max, ALU.mult))
                    do(v.reciprocal(DN[:, 1, :], DN[:, 0, :]))
                    do(v.tensor_tensor(H2[:, :, :], HN[:, :, 0:HD], bc(DN[:, 1, :], [P, H, HD]), ALU.mult))
                    dve.wait_ge(ot_ready, n + 1)
                    do(v.scalar_tensor_tensor(out=H2[:, :, :].rearrange("p h d -> p (h d)"), in0=OT[:, :], scalar=1.0,
                                              in1=H2[:, :, :].rearrange("p h d -> p (h d)"),
                                              op0=ALU.add, op1=ALU.mult))
                    do(v.tensor_reduce(HS[:, 0, :], H2[:, :, :], AX_X, ALU.add))
                    do(v.tensor_scalar(HS[:, 0, :], HS[:, 0, :], 1.0 / HD, None, ALU.mult))
                    v.tensor_tensor(H2[:, :, :], H2[:, :, :], bc(HS[:, 0, :], [P, H, HD]), ALU.subtract)\
                     .then_inc(cen_ready, 1)
                    dve.wait_ge(sq_ready, n + 1)
                    do(v.tensor_reduce(HS[:, 1, :], SQ[:, :, :], AX_X, ALU.add))
                    v.tensor_scalar(HS[:, 2, :], HS[:, 1, :], 1.0 / HD, 1e-6, ALU.mult, ALU.add)\
                     .then_inc(hvar_ready, 1)
                    dve.wait_ge(hn_ready, n + 1)
                    dve.wait_ge(*pj_read_at(b, 12 + 4 * c + 3))
                    do(v.tensor_tensor(SK[:, :], SK[:, :], H2[:, :, :].rearrange("p h d -> p (h d)"), ALU.add))
                    v.tensor_tensor(OUT[:, :], SK[:, :], GR[:, :], ALU.mult).then_inc(outg_ready, 1)
                    dve.wait_ge(tr_full, b * NTR + 1 + 4 * c + 4)
                    t = X[:, bass.ds(b * 4 + c, 1), :].rearrange("p a d -> p (a d)")
                    v.tensor_tensor(t, t, TR[:, 0:D], ALU.add).then_inc(tr_free, 1)
                    if c == 0:
                        assert step.n == ONCE + CH, step.n - ONCE
            step.looped(NB)
            dve.wait_ge(*tr_read_at(NB - 1, NTR - 1))
            ffn(1)


def _shape_constants(np):
    k = np.zeros((P, NCONST), np.float32)

    def put(name, a):
        at, w = CONST[name]
        k[:a.shape[0], at:at + w] = a

    p, c = np.arange(P)[:, None], np.arange(P)[None, :]
    put("ident", np.eye(P))
    put("tri", p < c)
    put("ones", np.ones((P, P)))
    put("mask", np.tile(np.where(p <= c, 0.0, NEG), (1, 4)))
    put("sel", -np.repeat(np.eye(H), P, axis=1))
    put("decl", (np.arange(H)[:, None] % 2) == (np.arange(P)[None, :] >= HD))
    put("decr", (np.arange(H)[:, None] // 2) == np.arange(NP_)[None, :])
    put("rev", np.tile(NE - np.arange(NE), (P, 1)))
    put("thr", np.tile(P * np.arange(NT), (P, 1)))
    put("blk", np.tile(np.arange(24), (P, 1)))
    put("reset", np.tile(np.arange(S) % P != 0, (P, 1)))
    put("reset16", np.tile(np.arange(NE * NT) % NT != 0, (P, 1)))
    return k


def kernel(**inputs):
    import numpy as np
    import concourse.bacc as _bacc
    from concourse import mybir as _mybir
    from concourse.bass_utils import run_bass_kernel_spmd as _run

    a = {n.replace("L0_attn_", "").replace("L0_ffn_", "f_"): np.asarray(v) for n, v in inputs.items()}

    def kmajor(w):
        return w.T.reshape(-1, P, w.shape[0]).transpose(1, 0, 2)

    cols = np.zeros((P, NCOL), np.float32)
    cols[:, 0], cols[:, 1] = a["ln_g"], a["ln_b"]
    padded = np.concatenate([np.zeros(3, np.float32), a["b_up_l"]])
    for j in range(2):
        for m in range(4):
            cols[:, COL["bshift"] + 4 * j + m] = padded[j * P + m:j * P + m + P]
        cols[:, COL["bul"] + j] = a["b_up_l"][j * P:(j + 1) * P]
    cols[:, COL["bq"]:COL["bq"] + 4] = a["b_q"].reshape(4, P).T
    cols[:, COL["bk"]:COL["bk"] + 4] = a["b_k"].reshape(4, P).T
    cols[0:H, COL["bif"]], cols[32:32 + H, COL["bif"]] = a["b_i"], a["b_f"]
    rows = np.concatenate([a["b_v"], a["b_o"], a["b_up_r"], a["b_skip"], a["mh_b"].ravel(), a["mh_g"].ravel(),
                           a["b_down"], a["conv_w"], a["conv_b"].reshape(1)])
    gates = np.zeros((P, 2, 40), np.float32)
    gates[:, :, 0:H], gates[:, :, 32:32 + H] = kmajor(a["W_i"]), kmajor(a["W_f"])
    w1 = np.concatenate([a["f_w1"].transpose(1, 0, 2), a["f_b1"].reshape(NE, FC, P).transpose(2, 0, 1)], axis=2)
    arrays = {
        "x": a["x"].reshape(NT * P, D), "consts": _shape_constants(np), "colpack": cols, "rowpack": rows,
        "w_router": a["f_w_router"], "w1": w1, "w2": a["f_w2"].reshape(NE, FC, P, D).transpose(2, 0, 1, 3),
        "b2": a["f_b2"], "wul": a["W_up_l"].reshape(2, P, D).transpose(1, 0, 2),
        "wult": np.concatenate([np.zeros((P, 3), np.float32), a["W_up_l"].T], axis=1), "wurt": a["W_up_r"].T,
        "wqt": kmajor(a["W_q"]), "wkt": kmajor(a["W_k"]), "wskt": kmajor(a["W_skip"]), "wvt": kmajor(a["W_v"]),
        "wot": kmajor(a["W_o"]), "wift": gates, "wdt": kmajor(a["W_down"]),
    }
    nc = _bacc.Bacc("TRN2", target_bir_lowering=False, num_devices=1)
    args = []
    for name, v in arrays.items():
        arrays[name] = v = np.ascontiguousarray(v)
        args.append(nc.dram_tensor(name, v.shape, _mybir.dt.from_np(v.dtype), kind="ExternalInput").ap())
    args.append(nc.dram_tensor("out", (NT * P, D), F32, kind="ExternalOutput").ap())
    macaron(nc, *args)
    r = _run(nc, [arrays], core_ids=[0])
    return r.results[0]["out"].reshape(a["x"].shape)
```

```python
from contextlib import ExitStack

import concourse.bass as bass
from concourse import mybir

F32 = mybir.dt.float32
BF16 = mybir.dt.bfloat16
I32 = mybir.dt.int32
U32 = mybir.dt.uint32
ALU = mybir.AluOpType
ACT = mybir.ActivationFunctionType
AX_X = mybir.AxisListType.X

P = 128
D = 128
NT = 16
NB = 4
NC = 4
S = NC * P
NE = 8
F = 512
FC = F // P
NBLK = NT + NE - 1
W1C = F + FC
SLOT = D + 1
RING = 4
H = 8
HD = 64
HID = H * HD
NP_ = H // 2
CAP = 15.0
NEG = -1.0e30

CONST = {}
_at = 0
for _n, _w in (("ident", 128), ("tri", 128), ("ones", 128), ("mask", 512), ("sel", 1024), ("decl", 128),
               ("decr", 4), ("fill", 23), ("token", 16), ("rev", 8), ("thr", 16), ("blk", 24), ("reset", 512), ("reset16", 128)):
    CONST[_n] = (_at, _w)
    _at += _w
NCONST = _at
COL = {"g": 0, "b": 1, "bshift": 2, "bul": 10, "bq": 12, "bk": 16, "bif": 20}
NCOL = 21
ROW = {"bv": 0, "bo": 512, "br": 1024, "bsk": 1536, "mhb": 2048, "mhg": 2560, "bdown": 3072, "cw": 3200, "cb": 3204}
NROW = 3205


class Steps:

    def __init__(self, eng, sem):
        self.eng, self.sem, self.base, self.n = eng, sem, 0, 0

    def did(self, ins):
        ins.then_inc(self.sem, 1)
        self.n += 1

    def do(self, ins):
        self.did(ins)
        self.eng.wait_ge(self.sem, self.base + self.n)

    def settle(self):
        self.eng.wait_ge(self.sem, self.base + self.n)

    def loop(self, i, per):
        self.before = self.base + self.n
        self.base, self.n, self.per = self.before + i * per, 0, per

    def looped(self, count):
        assert self.n == self.per, (self.n, self.per)
        self.base, self.n = self.before + count * self.per, 0


def macaron(nc, x, consts, colpack, rowpack, w_router, w1, w2, b2, wul, wult, wurt, wqt, wkt, wskt, wvt, wot,
            wift, wdt, out):
    x_v = x.rearrange("(t p) d -> p t d", p=P)
    out_v = out.rearrange("(t p) d -> p t d", p=P)
    slots = [nc.dram_tensor(f"slots_{f}", [NBLK * P, SLOT], F32, kind="Internal").ap() for f in range(2)]
    by_token = [nc.dram_tensor(f"by_token_{f}", [NT * P + NBLK * P, D], F32, kind="Internal").ap() for f in range(2)]

    with ExitStack() as ctx:
        def sb(name, shape, dt=F32):
            return ctx.enter_context(nc.sbuf_tensor(name, shape, dt))

        def sem(name):
            return ctx.enter_context(nc.semaphore(name))

        bank = [ctx.enter_context(nc.psum_tensor(f"bank{i}", [P, 512], F32)) for i in range(8)]

        X = sb("X", [P, NT, D])
        K = sb("K", [P, NCONST])
        COLS = sb("COLS", [P, NCOL])
        ROWS = sb("ROWS", [P, NROW])
        W1 = sb("W1", [P, NE, W1C])
        W2 = sb("W2", [P, NE, FC, D])
        B2 = sb("B2", [P, NE, D])
        WR = sb("WR", [P, NE])
        WUL = sb("WUL", [P, 2, D])
        WULT = sb("WULT", [P, 3 + 256])
        WCT = sb("WCT", [P, 256])
        WURT = sb("WURT", [P, HID])
        WQT = sb("WQT", [P, 2, HID])
        WKT = sb("WKT", [P, 2, HID])
        WSKT = sb("WSKT", [P, 2, HID])
        WVT = sb("WVT", [P, 2, HID])
        WOT = sb("WOT", [P, 2, HID])
        WVF = sb("WVF", [P, HID])
        WOF = sb("WOF", [P, HID])
        WIFT = sb("WIFT", [P, 2, 40])
        WDT = sb("WDT", [P, FC, D])
        HBX = sb("HBX", [P, 2])
        BSH = sb("BSH", [P, 2, 4])
        IDB = sb("IDB", [P, P], BF16)
        MASKB = sb("MASKB", [P, 512], BF16)
        BULB = sb("BULB", [P, 2, P])
        BIAS3 = sb("BIAS3", [65, 4 * HID], BF16)
        BMID = sb("BMID", [1, 4 * HID], BF16)
        ONES3 = sb("ONES3", [65, P], BF16)
        SEL3 = sb("SEL3", [72, H * P], BF16)

        def const(name):
            a, w = CONST[name]
            return K[:, a:a + w]

        def row(name, w):
            return ROWS[:, ROW[name]:ROW[name] + w]

        def col(name, i=0, lo=0, hi=P):
            return COLS[lo:hi, COL[name] + i:COL[name] + i + 1]

        ident = const("ident")

        XN = sb("XN", [P, NT, SLOT])
        XNT = sb("XNT", [P, 4, 512])
        ST = sb("ST", [P, NT, 6])
        LNA = sb("LNA", [P, 8, NT])
        LG = sb("LG", [P, NT, NE])
        EX = sb("EX", [P, NT, NE])
        OH = sb("OH", [P, NT, NE])
        RT = sb("RT", [P, 8, NT])
        TOTE = sb("TOTE", [P, NE, NT])
        INCL = sb("INCL", [P, NE, NT])
        RK = sb("RK", [P, NT, NE])
        CMP = sb("CMP", [P, NE, NT])
        EB = sb("EB", [P, 8, NE])
        BE = sb("BE", [P, 24, NE])
        EIDF = sb("EIDF", [P, 24])
        EID = sb("EID", [P, 24], I32)
        POS = sb("POS", [P, NT], U32)
        MHALF = sb("MHALF", [P, NT])
        XB = sb("XB", [P, RING, SLOT])
        IDX = sb("IDX", [P, RING], U32)
        XBT = sb("XBT", [P, 2, P])
        W1R = sb("W1R", [P, 2, W1C])
        HT = sb("HT", [P, 2, FC, P])
        YB = sb("YB", [P, RING, D])

        QKT = sb("QKT", [P, 8, 512])
        QT, KT = QKT[:, 0:4, :], QKT[:, 4:8, :]
        FILL = QKT[:, :, :].rearrange("p a n -> p (a n)")[:, 0:NBLK * SLOT].rearrange("p (k w) -> p k w", w=SLOT)
        YG = QT.rearrange("p a (t d) -> p (a t) d", d=D)
        ZB = sb("ZB", [P, 4, D])
        UB = sb("UB", [P, 4, D])
        SA = sb("SA", [P, 4, 6])
        LA = sb("LA", [P, 12, 4])
        XT = sb("XT", [P, 512])
        YH = XNT[:, 0:2, :]
        TH = XNT[:, 2:4, :]
        XC = sb("XC", [P, 2, 512])
        TIF = sb("TIF", [40, 512])
        F15 = sb("F15", [H, 512])
        FS = sb("FS", [H, 512])
        GT = sb("GT", [96, 512])
        MM = sb("MM", [H, 512])
        MMID = sb("MMID", [H, 512], BF16)
        M3 = sb("M3", [72, 512], BF16)
        MIN = sb("MIN", [H, NC + 1])
        G3 = sb("G3", [H, NC])
        G3M = sb("G3M", [H, NC, NP_])
        AC = sb("AC", [P, NC, H])
        E12 = sb("E12", [P, NC, 2, H])
        DEC = sb("DEC", [P, NC, NP_])
        KW = sb("KW", [P, H, HD])
        VX = sb("VX", [P, H, HD + 1])
        RTH = sb("RTH", [P, HID])
        xn_flat = XN[:, :, :].rearrange("p t w -> p (t w)")
        OT = xn_flat[:, 0:2 * HID].rearrange("p (i n) -> p i n", i=2)
        GR = xn_flat[:, 2 * HID:4 * HID].rearrange("p (i n) -> p i n", i=2)
        SK = HT[:, :, :, :].rearrange("p i c t -> p i (c t)")
        DT = WVT[:, :, :].rearrange("p i (m t) -> p i m t", t=P)
        PT = WOT[:, :, :].rearrange("p i (m t) -> p i m t", t=P)
        w1r_flat = W1R[:, :, :].rearrange("p i n -> p (i n)")
        H2 = w1r_flat[:, 0:HID].rearrange("p (h d) -> p h d", h=H)
        SQ = w1r_flat[:, HID:2 * HID].rearrange("p (h d) -> p h d", h=H)
        CS = sb("CS", [P, NP_, HD + 1])
        HN = sb("HN", [P, H, HD + 1])
        DN = sb("DN", [P, 2, H])
        HS = sb("HS", [P, 4, H])
        OUT = sb("OUT", [P, HID])
        OUTT = sb("OUTT", [P, FC, P])
        CREDIT = sb("CREDIT", [1, 9])

        x_loaded, consts_loaded, cols_loaded = sem("x_loaded"), sem("consts_loaded"), sem("cols_loaded")
        ffn_loaded, attn_loaded = sem("ffn_loaded"), sem("attn_loaded")
        fill_made, slots_filled, out_stored = sem("fill_made"), sem("slots_filled"), sem("out_stored")
        dve_step, pool_step = sem("dve_step"), sem("pool_step")

        def per_ffn(name):
            return [sem(f"{name}_{f}") for f in range(2)]

        def per_ffn_ring(name, n=RING):
            return [[sem(f"{name}_{f}_{i}") for i in range(n)] for f in range(2)]

        var_ready, rstd_ready, xn_ready = per_ffn("var_ready"), per_ffn("rstd_ready"), per_ffn("xn_ready")
        xt_full, xt_copied, logits_full = per_ffn("xt_full"), per_ffn("xt_copied"), per_ffn("logits_full")
        shifted, exp_ready, onehot_ready = per_ffn("shifted"), per_ffn("exp_ready"), per_ffn("onehot_ready")
        ranks_full, pos_ready, scattered = per_ffn("ranks_full"), per_ffn("pos_ready"), per_ffn("scattered")
        eid_ready, xb_loaded = per_ffn("eid_ready"), per_ffn_ring("xb_loaded")
        xbt_full, xbt_copied, w1_copied = per_ffn("xbt_full"), per_ffn("xbt_copied"), per_ffn("w1_copied")
        idx_copied = per_ffn("idx_copied")
        h_full, relu_act, relu_dve = per_ffn("h_full"), per_ffn("relu_act"), per_ffn("relu_dve")
        y_full, y_ready, y_sent = per_ffn("y_full"), per_ffn("y_ready"), per_ffn_ring("y_sent")
        y_loaded, ffn_done = per_ffn_ring("y_loaded"), per_ffn("ffn_done")
        folds_ready, fold_full, fold_copied = sem("folds_ready"), sem("fold_full"), sem("fold_copied")
        attn_consts, bias_hi, bias_rest, bias_mid = (sem("attn_consts"), sem("bias_hi"), sem("bias_rest"),
                                                     sem("bias_mid"))

        a_var, a_rstd, z_ready, u_ready = sem("a_var"), sem("a_rstd"), sem("z_ready"), sem("u_ready")
        a_var2, a_rstd2, ubd_ready = sem("a_var2"), sem("a_rstd2"), sem("ubd_ready")
        pj_full, pj_free = sem("pj_full"), [sem(f"pj_free_{i}") for i in range(2)]
        tr_full, tr_free = sem("tr_full"), sem("tr_free")
        tanh_ready, xc_ready, rows_ready = sem("tanh_ready"), sem("xc_ready"), sem("rows_ready")
        rth_ready, m3_ready = sem("rth_ready"), sem("m3_ready")
        dm_full, decay_ready, st_full, pt_ready = sem("dm_full"), sem("decay_ready"), sem("st_full"), sem("pt_ready")
        hv_full, hv_read, cs_ready = sem("hv_full"), sem("hv_read"), sem("cs_ready")
        cen_ready, sq_ready, hvar_ready = sem("cen_ready"), sem("sq_ready"), sem("hvar_ready")
        hn_ready, outg_ready = sem("hn_ready"), sem("outg_ready")

        PJ = bank[0:2]
        TR, DM = bank[2], bank[3]
        SB = bank[4:6]
        NB_ = bank[6:8]
        NPJ = 12 + 4 * NC
        TR_USES = ["g", "k0", "o-1", "d-1", "u0", "k1", "u1", "k2", "o0", "d0", "u2", "k3", "o1", "d1", "o2", "d2"]
        NTR = len(TR_USES)

        def pj_use(c, what):
            return 12 + 4 * c + "vors".index(what)

        def pj_read_at(b, u):
            return pj_free[u % 2], b * (NPJ // 2) + u // 2 + 2

        def tr_at(b, use):
            last = use in ("o3", "d3")
            n = TR_USES.index(use[0] + "-1" if last else use) + 1
            if isinstance(b, int) and (use in ("g", "k0") and b == 0 or last and b == NB - 1):
                return b * NTR + n if b == 0 else (b + 1) * NTR + n - 4
            return (b + last) * NTR + n - 2

        def tr_read_at(b, use):
            return tr_free, tr_at(b, use) + 1

        def tr_full_at(b, use):
            return tr_full, tr_at(b, use)

        block = ctx.enter_context(nc.Block())

        def over_blocks(eng, turn):
            for j in range(RING):
                turn(j, j, 0, True)
            with eng.Fori(1, NBLK // RING) as n:
                for j in range(RING):
                    turn(RING * n + j, j, n, False)
            for j in range(NBLK % RING):
                turn(NBLK // RING * RING + j, j, NBLK // RING, False)

        TAIL = NBLK // RING * RING

        @block.sync
        def _(sp):
            for q in range(4):
                sp.dma_start(X[:, 4 * q:4 * q + 4, :], x_v[:, 4 * q:4 * q + 4, :]).then_inc(x_loaded, 16)
            sp.dma_start(K[:, :], consts).then_inc(consts_loaded, 16)
            sp.dma_start(WR[:, :], w_router).then_inc(consts_loaded, 16)
            sp.dma_start(COLS[:, :], colpack).then_inc(cols_loaded, 16)
            sp.dma_start(ROWS[:, :], rowpack.partition_broadcast(P)).then_inc(cols_loaded, 16)
            sp.wait_ge(fill_made, 1)
            for f in range(2):
                sp.dma_start(slots[f].rearrange("(k p) w -> p k w", p=P), FILL).then_inc(slots_filled, 16)
            sp.dma_start(W1[:, :, :], w1).then_inc(ffn_loaded, 16)
            sp.dma_start(W2[:, :, :, :], w2).then_inc(ffn_loaded, 16)
            sp.dma_start(B2[:, :, :], b2.partition_broadcast(P)).then_inc(ffn_loaded, 16)

            for f in range(2):
                def load_block(k, j):
                    sp.dma_start(XB[:, j, :], slots[f][bass.ds(k * P, P), :]).then_inc(xb_loaded[f][j], 16)

                def turn(k, j, n, first):
                    if isinstance(k, int) and k + RING >= NBLK:
                        return
                    sp.wait_ge(xbt_full[f], k + 1)
                    sp.wait_ge(idx_copied[f], k + 1)
                    load_block(k + RING, j)

                sp.wait_ge(scattered[f], 16 * NT)
                for j in range(RING):
                    load_block(j, j)
                with sp.Fori(0, TAIL // RING - 1) as n:
                    for j in range(RING):
                        turn(RING * n + j, j, n, False)
                for k in range(TAIL - RING, NBLK):
                    turn(k, k % RING, k // RING, False)
                for j in range(RING):
                    sp.wait_ge(y_sent[f][j], 16 * len(range(j, NBLK, RING)))
                for q in range(4):
                    sp.dma_start(YG[:, 4 * q:4 * q + 4, :], by_token[f][512 * q:512 * (q + 1), :]
                                 .rearrange("(t p) d -> p t d", p=P)).then_inc(y_loaded[f][q], 16)
            for g in range(4):
                sp.wait_ge(ffn_done[1], 4 * g + 4)
                sp.dma_start(out_v[:, 4 * g:4 * g + 4, :], X[:, 4 * g:4 * g + 4, :]).then_inc(out_stored, 16)
            sp.wait_ge(out_stored, 64)

        @block.gpsimd
        def _(pool):
            g = nc.gpsimd
            step = Steps(pool, pool_step)
            step.did(g.memset(MHALF[:, :], -0.5))
            step.did(g.memset(FILL, 0.0))
            pool.wait_ge(consts_loaded, 32)
            step.settle()
            g.tensor_copy(FILL[:, :, D], const("fill")).then_inc(fill_made, 1)

            def ffn(f):
                pool.wait_ge(var_ready[f], 1)
                g.tensor_tensor(LNA[:, 5, :], LNA[:, 4, :], MHALF[:, :], ALU.pow).then_inc(rstd_ready[f], 1)
                step.do(g.tensor_copy(XN[:, :, D], const("token")))
                pool.wait_ge(slots_filled, 32)
                pool.wait_ge(pos_ready[f], 1)
                for t in range(NT):
                    g.indirect_dma_start(out=slots[f], out_offset=bass.IndirectOffsetOnAxis(ap=POS[:, t:t + 1], axis=0),
                                         in_=XN[:, t, :], in_offset=None).then_inc(scattered[f], 16)
                if f == 0:
                    rows = ROWS[0:1, 0:4 * HID]
                    pool.wait_ge(bias_hi, 1)
                    g.tensor_tensor(rows, rows, BIAS3[0:1, :], ALU.subtract).then_inc(bias_rest, 1)
                    pool.wait_ge(bias_mid, 1)
                    g.tensor_tensor(rows, rows, BMID[:, :], ALU.subtract).then_inc(bias_rest, 1)

                for k in range(NBLK):
                    j = k % RING
                    pool.wait_ge(y_ready[f], k + 1)
                    g.indirect_dma_start(out=by_token[f],
                                         out_offset=bass.IndirectOffsetOnAxis(ap=IDX[:, j:j + 1], axis=0),
                                         in_=YB[:, j, :], in_offset=None).then_inc(y_sent[f][j], 16)

            def norms(b):
                pool.wait_ge(a_var, b + 1)
                g.tensor_tensor(LA[:, 5, :], LA[:, 4, :], MHALF[:, 0:4], ALU.pow).then_inc(a_rstd, 1)
                pool.wait_ge(a_var2, b + 1)
                g.tensor_tensor(LA[:, 8, :], LA[:, 7, :], MHALF[:, 0:4], ALU.pow).then_inc(a_rstd2, 1)
                pool.wait_ge(z_ready, b + 1)
                g.tensor_tensor(UB[:, :, :], UB[:, :, :],
                                row("bdown", D).unsqueeze(1).to_broadcast([P, 4, D]), ALU.add).then_inc(ubd_ready, 1)

            def head_norm(b, c):
                n = b * NC + c
                pool.wait_ge(hvar_ready, n + 1)
                step.do(g.tensor_tensor(HS[:, 3, :], HS[:, 2, :], MHALF[:, 0:H], ALU.pow))
                step.do(g.tensor_tensor(H2[:, :, :], H2[:, :, :],
                                        HS[:, 3, :].unsqueeze(2).to_broadcast([P, H, HD]), ALU.mult))
                step.do(g.tensor_tensor(H2[:, :, :], H2[:, :, :],
                                        row("mhg", HID).rearrange("p (h d) -> p h d", h=H), ALU.mult))
                pool.wait_ge(*pj_read_at(b, pj_use(c, "s")))
                g.tensor_tensor(H2[:, :, :].rearrange("p h d -> p (h d)"), H2[:, :, :].rearrange("p h d -> p (h d)"),
                                SK[:, c % 2, :], ALU.add).then_inc(hn_ready, 1)

            def sequence(b, last):
                head_norm(b, 0)
                if not last:
                    norms(b + 1)
                for c in range(1, NC):
                    head_norm(b, c)

            ffn(0)
            pool.wait_ge(cols_loaded, 32)
            norms(0)
            with pool.Fori(0, NB - 1) as b:
                step.loop(b, 3 * NC)
                sequence(b, False)
            step.looped(NB - 1)
            sequence(NB - 1, True)
            ffn(1)

        @block.scalar
        def _(act):
            a = nc.scalar
            for dst, src in ((WUL[:, :, :], wul), (WULT[:, :], wult), (WURT[:, :], wurt), (WQT[:, :, :], wqt),
                             (WKT[:, :, :], wkt), (WSKT[:, :, :], wskt), (WVT[:, :, :], wvt), (WOT[:, :, :], wot),
                             (WIFT[:, :, :], wift), (WDT[:, :, :], wdt)):
                act.dma_start(dst, src).then_inc(attn_loaded, 16)

            def ffn(f):
                for q in range(4):
                    act.wait_ge(xt_full[f], q + 1)
                    a.activation(XNT[:, q, :], bank[q % 2][:, :], ACT.Copy).then_inc(xt_copied[f], 1)
                act.wait_ge(shifted[f], 1)
                a.activation(EX[:, :, :], EX[:, :, :], ACT.Exp).then_inc(exp_ready[f], 1)
                if f == 0:
                    for i, dst in enumerate((WVF, WOF)):
                        act.wait_ge(fold_full, 2 * i + 1)
                        a.activation(dst[:, :], bank[4 + 2 * i][:, :], ACT.Copy).then_inc(fold_copied, 1)
                    rows = ROWS[0:1, 0:4 * HID]
                    act.wait_ge(attn_consts, 1)
                    a.activation(BIAS3[0:1, :], rows, ACT.Copy).then_inc(bias_hi, 1)
                    act.wait_ge(bias_rest, 1)
                    a.activation(BMID[:, :], rows, ACT.Copy).then_inc(bias_mid, 1)
                    act.wait_ge(bias_mid, 1)
                    a.activation(BIAS3[32:33, :], BMID[:, :], ACT.Copy)
                    act.wait_ge(bias_rest, 2)
                    a.activation(BIAS3[64:65, :], rows, ACT.Copy).then_inc(bias_hi, 1)

                def x_block(k, j):
                    act.wait_ge(xbt_full[f], k + 1)
                    a.activation(XBT[:, j % 2, :], bank[j % 2][:, 0:P], ACT.Copy).then_inc(xbt_copied[f], 1)

                def relu(k, j):
                    act.wait_ge(h_full[f], 2 * k + 1)
                    for c in range(2):
                        ins = a.activation(HT[:, j % 2, c, :], bank[2 + j % 2][:, c * P:(c + 1) * P], ACT.Relu,
                                           bias=W1R[:, j % 2, F + c:F + c + 1])
                    ins.then_inc(relu_act[f], 1)

                def turn(k, j, n, first):
                    if not (isinstance(k, int) and k + 2 >= NBLK):
                        x_block(k + 2, (j + 2) % RING)
                    if not (isinstance(k, int) and k + 1 >= NBLK):
                        relu(k + 1, (j + 1) % RING)

                x_block(0, 0)
                x_block(1, 1)
                relu(0, 0)
                over_blocks(act, turn)

            def head_in(b):
                act.wait_ge(pj_full, b * NPJ + 1)
                a.activation(XT[:, :], PJ[0][:, :], ACT.Identity, scale=col("g"), bias=col("b")).then_inc(pj_free[0], 1)

            def head_silu(b):
                act.wait_ge(xc_ready, b + 1)
                for j in range(2):
                    act.wait_ge(pj_full, b * NPJ + 2 + j)
                    a.activation(YH[:, j, :], PJ[(1 + j) % 2][:, :], ACT.Identity, scale=0.5,
                                 bias=HBX[:, j:j + 1]).then_inc(pj_free[(1 + j) % 2], 1)
                act.wait_ge(*pj_read_at(b, 1))
                act.wait_ge(*pj_read_at(b, 2))
                a.activation(TH, YH, ACT.Tanh).then_inc(tanh_ready, 1)

            def head_gates(b):
                act.wait_ge(pj_full, b * NPJ + 4)
                a.activation(TIF[0:H, :], PJ[1][0:H, :], ACT.Tanh, scale=1.0 / CAP, bias=col("bif", 0, 0, H))
                a.activation(TIF[32:32 + H, :], PJ[1][32:32 + H, :], ACT.Tanh, scale=1.0 / CAP,
                             bias=col("bif", 0, 32, 32 + H)).then_inc(pj_free[1], 1)

            def head_qk(b):
                for m in range(8):
                    act.wait_ge(pj_full, b * NPJ + 5 + m)
                    a.activation(QKT[:, m, :], PJ[m % 2][:, :], ACT.Identity, bias=col("bq", m))\
                     .then_inc(pj_free[m % 2], 1)
                act.wait_ge(*tr_full_at(b, "g"))
                cols = TR[:, 0:NC * 96].rearrange("p (c q r) -> p c q r", c=NC, q=3)
                a.activation(AC[:, :, :], cols[:, :, 0, 0:H], ACT.Copy)
                a.activation(E12[:, :, :, :], cols[:, :, 1:3, 0:H], ACT.Exp)
                a.activation(DEC[:, :, :], TR[:, 384:384 + NC * NP_].rearrange("p (c m) -> p c m", c=NC), ACT.Exp)\
                    .then_inc(tr_free, 1)
                act.wait_ge(*tr_read_at(b, "g"))

            def take(b, c):
                act.wait_ge(pj_full, b * NPJ + pj_use(c, "v") + 1)
                a.activation(VX[:, :, 0:HD], PJ[0][:, :].rearrange("p (h d) -> p h d", h=H), ACT.Copy)\
                    .then_inc(pj_free[0], 1)
                act.wait_ge(pj_full, b * NPJ + pj_use(c, "o") + 1)
                a.activation(OT[:, c % 2, :], PJ[1][:, :], ACT.Tanh, scale=0.5).then_inc(pj_free[1], 1)
                act.wait_ge(pj_full, b * NPJ + pj_use(c, "r") + 1)
                a.activation(RTH[:, :], PJ[0][:, :], ACT.Tanh, scale=0.5).then_inc(rth_ready, 1)
                act.wait_ge(pj_full, b * NPJ + pj_use(c, "s") + 1)
                if not (isinstance(b, int) and b * NC + c == 0):
                    act.wait_ge(hn_ready, b * NC + c)
                a.activation(SK[:, c % 2, :], PJ[1][:, :], ACT.Copy).then_inc(pj_free[1], 1)

            def decays(b, c):
                n = b * NC + c
                act.wait_ge(pt_ready, 2 * n + 1)
                for hf in range(2):
                    act.wait_ge(dm_full, 2 * n + hf + 1)
                    for m in range(4):
                        h = 2 * m + hf
                        ins = a.activation(DT[:, hf, m, :], DM[:, m * P:(m + 1) * P], ACT.Exp, bias=AC[:, c, h:h + 1])
                    ins.then_inc(decay_ready, 1)

            def squares(b, c):
                act.wait_ge(cen_ready, b * NC + c + 1)
                a.activation(SQ[:, :, :], H2[:, :, :], ACT.Square).then_inc(sq_ready, 1)

            def out_t(b, c):
                act.wait_ge(*tr_full_at(b, f"o{c}"))
                a.activation(OUTT[:, :, :].rearrange("p m t -> p (m t)"), TR[:, :], ACT.Copy).then_inc(tr_free, 1)

            def sequence(b, last):
                decays(b, 0)
                take(b, 1)
                decays(b, 1)
                squares(b, 0)
                take(b, 2)
                out_t(b, 0)
                decays(b, 2)
                squares(b, 1)
                take(b, 3)
                if not last:
                    head_in(b + 1)
                out_t(b, 1)
                if not last:
                    head_silu(b + 1)
                decays(b, 3)
                squares(b, 2)
                out_t(b, 2)
                if not last:
                    head_gates(b + 1)
                squares(b, 3)
                if not last:
                    head_qk(b + 1)
                    take(b + 1, 0)
                out_t(b, 3)

            ffn(0)
            head_in(0)
            head_silu(0)
            head_gates(0)
            head_qk(0)
            take(0, 0)
            with act.Fori(0, NB - 1) as b:
                sequence(b, False)
            sequence(NB - 1, True)
            ffn(1)

        @block.tensor
        def _(pe):
            t_ = nc.tensor

            def mm(o, l, r, start=True, stop=True):
                return t_.matmul(o, l, r, start=start, stop=stop, skip_group_check=True)

            def ffn(f):
                pe.wait_ge(consts_loaded, 32)
                for q in range(4):
                    pe.wait_ge(xn_ready[f], 4 * q + 4)
                    if q >= 2:
                        pe.wait_ge(xt_copied[f], q - 1)
                    for j in range(4):
                        ins = t_.transpose(bank[q % 2][:, j * P:(j + 1) * P], XN[:, 4 * q + j, 0:D], ident)
                    ins.then_inc(xt_full[f], 1)
                for q in range(4):
                    pe.wait_ge(xt_copied[f], q + 1)
                    for j in range(4):
                        t = 4 * q + j
                        ins = mm(bank[2][:, t * NE:(t + 1) * NE], XNT[:, q, j * P:(j + 1) * P], WR[:, :])
                ins.then_inc(logits_full[f], 1)
                pe.wait_ge(onehot_ready[f], 1)
                oh = OH[:, :, :].rearrange("p t e -> p (t e)")
                mm(bank[3][:, 0:P], const("tri"), oh)
                mm(bank[3][:, P:2 * P], const("ones"), oh).then_inc(ranks_full[f], 1)
                if f == 0:
                    pe.wait_ge(attn_loaded, 160)
                    pe.wait_ge(folds_ready, 1)
                    for i, w in enumerate((WVT, WOT)):
                        for j in range(2):
                            ins = mm(bank[4 + 2 * i][:, :], WUL[:, j, :], w[:, j, :], j == 0, j == 1)
                        ins.then_inc(fold_full, 1)
                        for j in range(2):
                            ins = mm(bank[5 + 2 * i][:, :], BULB[:, j, :], w[:, j, :], j == 0, j == 1)
                        ins.then_inc(fold_full, 1)
                    pe.wait_ge(fold_copied, 2)
                    pe.wait_ge(attn_consts, 1)
                pe.wait_ge(ffn_loaded, 48)
                pe.wait_ge(eid_ready[f], 1)

                def turn_x(k, j, n):
                    pe.wait_ge(xb_loaded[f][j], 16 * (n + 1))
                    if not (isinstance(k, int) and k < 2):
                        pe.wait_ge(xbt_copied[f], k - 1)
                    t_.transpose(bank[j % 2][:, 0:P], XB[:, j, 0:D], ident).then_inc(xbt_full[f], 1)

                def up(k, j):
                    pe.wait_ge(xbt_copied[f], k + 1)
                    pe.wait_ge(w1_copied[f], k + 1)
                    if not (isinstance(k, int) and k < 2):
                        pe.wait_ge(relu_act[f], k - 1)
                        pe.wait_ge(relu_dve[f], k - 1)
                    for c in range(FC):
                        ins = mm(bank[2 + j % 2 + 2 * (c // 2)][:, (c % 2) * P:(c % 2 + 1) * P],
                                 W1R[:, j % 2, c * P:(c + 1) * P], XBT[:, j % 2, :])
                        if c % 2:
                            ins.then_inc(h_full[f], 1)

                def down(k, j):
                    e = pe.value_load(EID[0:1, bass.ds(k, 1)], min_val=0, max_val=NE - 1)
                    pe.wait_ge(relu_act[f], k + 1)
                    pe.wait_ge(relu_dve[f], k + 1)
                    if not (isinstance(k, int) and k < 2):
                        pe.wait_ge(y_ready[f], k - 1)
                    for c in range(FC):
                        ins = mm(bank[6 + j % 2][:, 0:D], HT[:, j % 2, c, :], W2[:, e, c, :], c == 0, c == FC - 1)
                    ins.then_inc(y_full[f], 1)

                def turn(k, j, n, first):
                    if not (isinstance(k, int) and k + 2 >= NBLK):
                        turn_x(k + 2, (j + 2) % RING, n + (j + 2) // RING)
                    if not (isinstance(k, int) and k + 1 >= NBLK):
                        up(k + 1, (j + 1) % RING)
                    down(k, j)

                turn_x(0, 0, 0)
                turn_x(1, 1, 0)
                up(0, 0)
                over_blocks(pe, turn)

            def pj_wait(b, u):
                pe.wait_ge(pj_free[u % 2], b * (NPJ // 2) + u // 2 + 1)
                return PJ[u % 2]

            def tr_wait(b, use):
                pe.wait_ge(tr_free, tr_at(b, use))
                return TR

            def head_z(b):
                pe.wait_ge(z_ready, b + 1)
                dst = pj_wait(b, 0)
                for j in range(4):
                    ins = t_.transpose(dst[:, j * P:(j + 1) * P], ZB[:, j, :], ident)
                ins.then_inc(pj_full, 1)

            def head_x(b):
                pe.wait_ge(*pj_read_at(b, 0))
                for j in range(2):
                    mm(pj_wait(b, 1 + j)[:, :], WCT[:, j * P:(j + 1) * P], XT[:, :]).then_inc(pj_full, 1)

            def head_rest(b):
                pe.wait_ge(xc_ready, b + 2)
                dst = pj_wait(b, 3)
                for j in range(2):
                    ins = mm(dst[0:40, :], WIFT[:, j, :], XC[:, j, :], j == 0, j == 1)
                ins.then_inc(pj_full, 1)
                for w, u0 in ((WQT, 4), (WKT, 8)):
                    for m in range(4):
                        dst = pj_wait(b, u0 + m)
                        for j in range(2):
                            ins = mm(dst[:, :], w[:, j, m * P:(m + 1) * P], XC[:, j, :], j == 0, j == 1)
                        ins.then_inc(pj_full, 1)
                pe.wait_ge(rows_ready, b + 1)
                dst = tr_wait(b, "g")
                for c in range(NC):
                    t_.transpose(dst[:, c * 96:(c + 1) * 96], GT[:, c * P:(c + 1) * P], ident[0:96, 0:96])
                mm(dst[:, 384:384 + NC * NP_], const("decl")[0:H, :], G3M[:, :, :].rearrange("p c m -> p (c m)"))\
                    .then_inc(tr_full, 1)

            def project(b, c):
                at = slice(c * P, (c + 1) * P)
                if c == 0:
                    pe.wait_ge(*pj_read_at(b, 10))
                    pe.wait_ge(*pj_read_at(b, 11))
                dst = tr_wait(b, f"k{c}")
                for m in range(4):
                    ins = t_.transpose(dst[:, m * P:(m + 1) * P], KT[:, m, at], ident)
                ins.then_inc(tr_full, 1)
                for i, (what, parts) in enumerate((("v", [(XT[:, at], WVF[:, :])]), ("o", [(XT[:, at], WOF[:, :])]),
                                                   ("r", [(XT[:, at], WURT[:, :])]),
                                                   ("s", [(XC[:, j, at], WSKT[:, j, :]) for j in range(2)]))):
                    dst = pj_wait(b, pj_use(c, what))
                    mm(dst[:, :], ONES3[:, :], BIAS3[:, i * HID:(i + 1) * HID], True, False)
                    for x_, w_ in parts:
                        ins = mm(dst[:, :], x_, w_, False, x_ is parts[-1][0])
                    ins.then_inc(pj_full, 1)

            def attend(b, c):
                n = b * NC + c
                at = slice(c * P, (c + 1) * P)
                if c == 0:
                    pe.wait_ge(m3_ready, b + 1)
                    pe.wait_ge(*tr_read_at(b, "g"))
                for hf in range(2):
                    rows = slice(hf * HD, (hf + 1) * HD)
                    pe.wait_ge(decay_ready, 2 * n + hf + 1)
                    mm(DM[:, :], IDB[:, :], MASKB[:, :], True, False)
                    for m in range(4):
                        h = 2 * m + hf
                        ins = mm(DM[:, m * P:(m + 1) * P], SEL3[:, h * P:(h + 1) * P], M3[:, at], False, m == 3)
                    ins.then_inc(dm_full, 1)
                    pe.wait_ge(hv_read, 2 * n + 1)
                    for m in range(4):
                        ins = mm(SB[hf][:, m * P:(m + 1) * P], KT[rows, m, at], QT[rows, m, at])
                    ins.then_inc(st_full, 1)
                if c == 0:
                    pe.wait_ge(cs_ready, b + 1)
                else:
                    pe.wait_ge(*tr_read_at(b, f"u{c - 1}"))
                for hf in range(2):
                    rows = slice(hf * HD, (hf + 1) * HD)
                    for m in range(4):
                        mm(NB_[hf][:, m * 65:(m + 1) * 65], QT[rows, m, at], CS[rows, m, :])
                pe.wait_ge(*pj_read_at(b, pj_use(c, "v")))
                if c < NC - 1:
                    pe.wait_ge(*tr_read_at(b, f"k{c}"))
                    dst = tr_wait(b, f"u{c}")
                    for h in range(H):
                        rows = slice((h % 2) * HD, (h % 2 + 1) * HD)
                        ins = mm(dst[rows, (h // 2) * 65:(h // 2 + 1) * 65], KW[:, h, :], VX[:, h, :])
                    ins.then_inc(tr_full, 1)
                for hf in range(2):
                    pe.wait_ge(pt_ready, 2 * n + hf + 2)
                    for m in range(4):
                        ins = mm(SB[hf][:, m * 65:(m + 1) * 65], PT[:, hf, m, :], VX[:, 2 * m + hf, :])
                    ins.then_inc(hv_full, 1)

            def finish(b, c):
                pe.wait_ge(outg_ready, b * NC + c + 2)
                dst = tr_wait(b, f"o{c}")
                for m in range(4):
                    ins = t_.transpose(dst[:, m * P:(m + 1) * P], OUT[:, m * P:(m + 1) * P], ident)
                ins.then_inc(tr_full, 1)
                dst = tr_wait(b, f"d{c}")
                for m in range(4):
                    ins = mm(dst[:, 0:D], OUTT[:, m, :], WDT[:, m, :], m == 0, m == 3)
                ins.then_inc(tr_full, 1)

            def sequence(b, last):
                attend(b, 0)
                project(b, 1)
                attend(b, 1)
                project(b, 2)
                finish(b, 0)
                attend(b, 2)
                project(b, 3)
                if not last:
                    head_z(b + 1)
                finish(b, 1)
                if not last:
                    head_x(b + 1)
                attend(b, 3)
                finish(b, 2)
                if not last:
                    head_rest(b + 1)
                    project(b + 1, 0)
                finish(b, 3)

            ffn(0)
            head_z(0)
            head_x(0)
            head_rest(0)
            pe.wait_ge(bias_hi, 2)
            project(0, 0)
            with pe.Fori(0, NB - 1) as b:
                sequence(b, False)
            sequence(NB - 1, True)
            ffn(1)

        @block.vector
        def _(dve):
            v = nc.vector
            step = Steps(dve, dve_step)
            do, did = step.do, step.did

            def bc(ap, shape):
                return ap.unsqueeze(len(ap.shape)).to_broadcast(shape)

            def moments(st, w, n):
                did(v.tensor_tensor(w[:, 0, :], st[:, :, 1], st[:, :, 4], ALU.add))
                did(v.tensor_tensor(w[:, 1, :], st[:, :, 1], st[:, :, 4], ALU.subtract))
                do(v.tensor_tensor(w[:, 2, :], st[:, :, 2], st[:, :, 5], ALU.add))
                did(v.tensor_scalar(w[:, 0, :], w[:, 0, :], 0.5, None, ALU.mult))
                do(v.scalar_tensor_tensor(out=w[:, 1, :], in0=w[:, 1, :], scalar=0.25, in1=w[:, 1, :],
                                          op0=ALU.mult, op1=ALU.mult))
                do(v.scalar_tensor_tensor(out=w[:, 3, :], in0=w[:, 2, :], scalar=1.0 / n, in1=w[:, 1, :],
                                          op0=ALU.mult, op1=ALU.add))

            def combine(f, q):
                dve.wait_ge(y_loaded[f][q], 16)
                for t in range(4 * q, 4 * q + 4):
                    v.scalar_tensor_tensor(out=X[:, t, :], in0=YG[:, t, :], scalar=RT[:, 3, t:t + 1],
                                           in1=X[:, t, :], op0=ALU.mult, op1=ALU.add).then_inc(ffn_done[f], 1)
                dve.wait_ge(ffn_done[f], 4 * q + 4)

            def ffn(f):
                with dve.Fori(0, NT) as t:
                    step.loop(t, 1)
                    did(v.bn_stats(ST[:, t, :], X[:, t, :]))
                step.looped(NT)
                step.settle()
                moments(ST, LNA, D)
                v.tensor_scalar(LNA[:, 4, :], LNA[:, 3, :], 1e-5, None, ALU.add).then_inc(var_ready[f], 1)
                dve.wait_ge(rstd_ready[f], 1)
                with dve.Fori(0, NT) as t:
                    v.tensor_scalar(XN[:, t, 0:D], X[:, t, :], LNA[:, 0, bass.ds(t, 1)], LNA[:, 5, bass.ds(t, 1)],
                                    ALU.subtract, ALU.mult).then_inc(xn_ready[f], 1)
                dve.wait_ge(logits_full[f], 1)
                dve.wait_ge(consts_loaded, 32)
                do(v.tensor_copy(LG[:, :, :].rearrange("p t e -> p (t e)"), bank[2][:, 0:NT * NE]))
                do(v.tensor_reduce(RT[:, 0, :], LG[:, :, :], AX_X, ALU.max))
                v.tensor_tensor(EX[:, :, :], LG[:, :, :], bc(RT[:, 0, :], [P, NT, NE]), ALU.subtract)\
                    .then_inc(shifted[f], 1)
                do(v.tensor_tensor(OH[:, :, :], LG[:, :, :], bc(RT[:, 0, :], [P, NT, NE]), ALU.is_equal))
                rev = const("rev").unsqueeze(1).to_broadcast([P, NT, NE])
                do(v.tensor_tensor(OH[:, :, :], OH[:, :, :], rev, ALU.mult))
                do(v.tensor_reduce(RT[:, 1, :], OH[:, :, :], AX_X, ALU.max))
                v.tensor_tensor(OH[:, :, :], rev, bc(RT[:, 1, :], [P, NT, NE]), ALU.is_equal)\
                    .then_inc(onehot_ready[f], 1)
                dve.wait_ge(ranks_full[f], 1)
                do(v.tensor_copy(TOTE[:, :, :], bank[3][:, P:2 * P].rearrange("p (t e) -> p e t", e=NE)))
                do(v.tensor_tensor_scan(INCL[:, :, :].rearrange("p e t -> p (e t)"), const("reset16"),
                                        TOTE[:, :, :].rearrange("p e t -> p (e t)"), 0.0, ALU.mult, ALU.add))
                do(v.tensor_tensor(CMP[:, :, :], bc(INCL[:, :, NT - 1], [P, NE, NT]),
                                   const("thr").unsqueeze(1).to_broadcast([P, NE, NT]), ALU.is_gt))
                did(v.tensor_tensor(INCL[:, :, :], INCL[:, :, :], TOTE[:, :, :], ALU.subtract))
                do(v.tensor_reduce(EB[:, 0, :], CMP[:, :, :], AX_X, ALU.add))
                do(v.tensor_tensor_scan(EB[:, 1, :], const("ones")[:, 0:NE], EB[:, 0, :], 0.0, ALU.mult, ALU.add))
                do(v.tensor_tensor(EB[:, 2, :], EB[:, 1, :], EB[:, 0, :], ALU.subtract))
                do(v.tensor_scalar(EB[:, 2, :], EB[:, 2, :], float(P), None, ALU.mult))
                do(v.tensor_tensor(INCL[:, :, :], INCL[:, :, :], bc(EB[:, 2, :], [P, NE, NT]), ALU.add))
                do(v.tensor_tensor(RK[:, :, :], bank[3][:, 0:P].rearrange("p (t e) -> p t e", e=NE),
                                   INCL[:, :, :].rearrange("p e t -> p t e"), ALU.add))
                do(v.tensor_tensor(RK[:, :, :], RK[:, :, :], OH[:, :, :], ALU.mult))
                do(v.tensor_reduce(RT[:, 4, :], RK[:, :, :], AX_X, ALU.add))
                v.tensor_copy(POS[:, :], RT[:, 4, :]).then_inc(pos_ready[f], 1)
                dve.wait_ge(exp_ready[f], 1)
                did(v.tensor_reduce(RT[:, 2, :], EX[:, :, :], AX_X, ALU.add))
                do(v.tensor_tensor(BE[:, :, :], bc(const("blk"), [P, 24, NE]),
                                   EB[:, 1, :].unsqueeze(1).to_broadcast([P, 24, NE]), ALU.is_ge))
                did(v.reciprocal(RT[:, 3, :], RT[:, 2, :]))
                do(v.tensor_reduce(EIDF[:, :], BE[:, :, :], AX_X, ALU.add))
                did(v.tensor_scalar(RT[:, 3, :], RT[:, 3, :], 0.5, None, ALU.mult))
                do(v.tensor_scalar(EIDF[:, :], EIDF[:, :], float(NE - 1), None, ALU.min))
                v.tensor_copy(EID[:, :], EIDF[:, :]).then_inc(eid_ready[f], 1)
                dve.wait_ge(eid_ready[f], 1)
                if f == 0:
                    attn_setup()
                dve.wait_ge(ffn_loaded, 48)

                def copy_idx(k, j):
                    dve.wait_ge(xbt_full[f], k + 1)
                    if not (isinstance(k, int) and k < RING):
                        dve.wait_ge(y_sent[f][j], 4 * (k - j))
                    v.tensor_copy(IDX[:, j:j + 1], XB[:, j, D:D + 1]).then_inc(idx_copied[f], 1)

                def copy_w1(k, j):
                    e = dve.value_load(EID[0:1, bass.ds(k, 1)], min_val=0, max_val=NE - 1)
                    if not (isinstance(k, int) and k < 2):
                        dve.wait_ge(relu_act[f], k - 1)
                        dve.wait_ge(relu_dve[f], k - 1)
                    v.tensor_copy(W1R[:, j % 2, :], W1[:, e, :]).then_inc(w1_copied[f], 1)

                def relu(k, j):
                    dve.wait_ge(h_full[f], 2 * k + 2)
                    for c in range(2):
                        ins = v.tensor_scalar(HT[:, j % 2, 2 + c, :], bank[4 + j % 2][:, c * P:(c + 1) * P],
                                              W1R[:, j % 2, F + 2 + c:F + 3 + c], 0.0, ALU.add, ALU.max)
                    ins.then_inc(relu_dve[f], 1)

                def add_b2(k, j):
                    e = dve.value_load(EID[0:1, bass.ds(k, 1)], min_val=0, max_val=NE - 1)
                    dve.wait_ge(y_full[f], k + 1)
                    v.tensor_tensor(YB[:, j, :], bank[6 + j % 2][:, 0:D], B2[:, e, :], ALU.add).then_inc(y_ready[f], 1)

                def turn(k, j, n, first):
                    def within(i):
                        return not (isinstance(k, int) and k + i >= NBLK)

                    if within(2):
                        copy_idx(k + 2, (j + 2) % RING)
                    if within(1):
                        relu(k + 1, (j + 1) % RING)
                    if within(3):
                        copy_w1(k + 3, (j + 3) % RING)
                    add_b2(k, j)

                copy_w1(0, 0)
                copy_w1(1, 1)
                copy_idx(0, 0)
                copy_idx(1, 1)
                relu(0, 0)
                copy_w1(2, 2)
                over_blocks(dve, turn)
                combine(f, 0)
                if f == 0:
                    norms(0)
                for q in range(1, 4):
                    combine(f, q)

            def attn_setup():
                dve.wait_ge(attn_loaded, 160)
                dve.wait_ge(cols_loaded, 32)
                for j in range(2):
                    ins = v.tensor_copy(BULB[:, j, :], col("bul", j).to_broadcast([P, P]))
                ins.then_inc(folds_ready, 1)
                did(v.tensor_copy(IDB[:, :], ident))
                did(v.tensor_copy(MASKB[:, :], const("mask")))
                did(v.tensor_copy(SEL3[:, :], const("sel")[0:72, :]))
                did(v.memset(ONES3[:, :], 1.0))
                did(v.memset(BIAS3[:, :].bitcast(U32), 0))
                did(v.memset(M3[:, :], 0.0))
                do(v.tensor_scalar(WCT[:, :], WULT[:, 0:256], row("cw", 4)[:, 0:1], None, ALU.mult))
                for m in range(1, 4):
                    do(v.scalar_tensor_tensor(out=WCT[:, :], in0=WULT[:, m:m + 256], scalar=row("cw", 4)[:, m:m + 1],
                                              in1=WCT[:, :], op0=ALU.mult, op1=ALU.add))
                do(v.tensor_tensor(BSH[:, :, :], COLS[:, COL["bshift"]:COL["bshift"] + 8]
                                   .rearrange("p (j m) -> p j m", j=2),
                                   row("cw", 4).unsqueeze(1).to_broadcast([P, 2, 4]), ALU.mult))
                do(v.tensor_reduce(HBX[:, :], BSH[:, :, :], AX_X, ALU.add))
                did(v.tensor_scalar(HBX[:, :], HBX[:, :], row("cb", 1), 0.5, ALU.add, ALU.mult))
                did(v.tensor_scalar(WKT[:, :, :], WKT[:, :, :], HD ** -0.5, None, ALU.mult))
                did(v.tensor_scalar(COLS[:, COL["bk"]:COL["bk"] + 4], COLS[:, COL["bk"]:COL["bk"] + 4],
                                    HD ** -0.5, None, ALU.mult))
                did(v.tensor_scalar(WDT[:, :, :], WDT[:, :, :], 0.5, None, ALU.mult))
                did(v.tensor_scalar(col("bif"), col("bif"), 1.0 / CAP, None, ALU.mult))
                did(v.tensor_tensor(row("bsk", HID), row("bsk", HID), row("mhb", HID), ALU.add))
                did(v.memset(VX[:, :, :], 1.0))
                did(v.memset(GT[:, :], 0.0))
                for i, name in enumerate(("bv", "bo")):
                    dve.wait_ge(fold_full, 2 * i + 2)
                    did(v.tensor_tensor(row(name, HID), bank[5 + 2 * i][:, :], row(name, HID), ALU.add))
                for i, s in enumerate((*pj_free, tr_free, xc_ready, pt_ready, decay_ready, hv_read,
                                       outg_ready, hn_ready)):
                    v.memset(CREDIT[:, i:i + 1], 0.0).then_inc(s, 1)
                step.settle()
                v.memset(MIN[:, :], 0.0).then_inc(attn_consts, 1)
                dve.wait_ge(attn_consts, 1)

            def norms(b):
                for j in range(4):
                    did(v.bn_stats(SA[:, j, :], X[:, bass.ds(b * 4 + j, 1), :].rearrange("p a d -> p (a d)")))
                step.settle()
                moments(SA, LA, D)
                v.tensor_scalar(LA[:, 4, :], LA[:, 3, :], 1e-5, None, ALU.add).then_inc(a_var, 1)
                xs = X[:, bass.ds(b * 4, 4), :]
                did(v.tensor_tensor(UB[:, :, :], xs, bc(LA[:, 0, :], [P, 4, D]), ALU.subtract))
                dve.wait_ge(a_rstd, b + 1)
                do(v.tensor_tensor(LA[:, 6, :], LA[:, 5, :], LA[:, 5, :], ALU.mult))
                do(v.tensor_tensor(LA[:, 6, :], LA[:, 6, :], LA[:, 3, :], ALU.mult))
                v.tensor_scalar(LA[:, 7, :], LA[:, 6, :], 1e-6, None, ALU.add).then_inc(a_var2, 1)
                v.tensor_tensor(UB[:, :, :], UB[:, :, :], bc(LA[:, 5, :], [P, 4, D]), ALU.mult).then_inc(u_ready, 1)
                dve.wait_ge(u_ready, b + 1)
                dve.wait_ge(a_rstd2, b + 1)
                v.tensor_tensor(ZB[:, :, :], UB[:, :, :], bc(LA[:, 8, :], [P, 4, D]), ALU.mult).then_inc(z_ready, 1)

            def add_u(b):
                xs = X[:, bass.ds(b * 4, 4), :]
                dve.wait_ge(ubd_ready, b + 1)
                do(v.tensor_tensor(xs, xs, UB[:, :, :], ALU.add))

            def silu(b):
                dve.wait_ge(tanh_ready, b + 1)
                v.scalar_tensor_tensor(out=XC[:, :, :], in0=TH, scalar=1.0, in1=YH,
                                       op0=ALU.add, op1=ALU.mult).then_inc(xc_ready, 1)

            def reset_state():
                did(v.memset(CS[:, :, 0:HD], 0.0))
                v.memset(CS[:, :, HD:HD + 1], 1.0).then_inc(cs_ready, 1)

            def gates(b):
                dve.wait_ge(*pj_read_at(b, 3))
                do(v.tensor_scalar(F15[:, :], TIF[32:32 + H, :], CAP, None, ALU.mult))
                do(v.tensor_tensor_scan(FS[:, :], const("reset")[0:H, :], F15[:, :], 0.0, ALU.mult, ALU.add))
                do(v.scalar_tensor_tensor(out=GT[0:H, :], in0=TIF[0:H, :], scalar=CAP, in1=FS[:, :],
                                          op0=ALU.mult, op1=ALU.subtract))
                for c in range(NC):
                    at = slice(c * P, (c + 1) * P)
                    do(v.tensor_tensor_scan(MM[:, at], GT[0:H, at], GT[0:H, at], MIN[:, c:c + 1], ALU.max, ALU.max))
                    if c < NC - 1:
                        last = slice((c + 1) * P - 1, (c + 1) * P)
                        do(v.tensor_tensor(MIN[:, c + 1:c + 2], FS[:, last], MM[:, last], ALU.add))
                m4 = MM[:, :].rearrange("p (c t) -> p c t", c=NC)
                a4 = GT[0:H, :].rearrange("p (c t) -> p c t", c=NC)
                did(v.tensor_tensor(GT[32:32 + H, :].rearrange("p (c t) -> p c t", c=NC),
                                    bc(MIN[:, 0:NC], [H, NC, P]), m4, ALU.subtract))
                did(v.tensor_tensor(GT[64:64 + H, :].rearrange("p (c t) -> p c t", c=NC), a4,
                                    bc(m4[:, :, P - 1], [H, NC, P]), ALU.subtract))
                do(v.tensor_tensor(G3[:, :], MIN[:, 0:NC], m4[:, :, P - 1], ALU.subtract))
                v.tensor_tensor(G3M[:, :, :], bc(G3[:, :], [H, NC, NP_]),
                                const("decr")[0:H, :].unsqueeze(1).to_broadcast([H, NC, NP_]), ALU.mult)\
                    .then_inc(rows_ready, 1)
                do(v.tensor_copy(M3[0:H, :], MM[:, :]))
                do(v.tensor_tensor(MM[:, :], MM[:, :], M3[0:H, :], ALU.subtract))
                do(v.tensor_copy(MMID[:, :], MM[:, :]))
                did(v.tensor_copy(M3[32:32 + H, :], MMID[:, :]))
                do(v.tensor_tensor(MM[:, :], MM[:, :], MMID[:, :], ALU.subtract))
                v.tensor_copy(M3[64:64 + H, :], MM[:, :]).then_inc(m3_ready, 1)

            def take(b, c):
                if c == 0:
                    dve.wait_ge(*tr_read_at(b, "g"))
                dve.wait_ge(*tr_full_at(b, f"k{c}"))
                v.tensor_tensor(KW[:, :, :], TR[:, :].rearrange("p (h d) -> p h d", h=H),
                                bc(E12[:, c, 1, :], [P, H, HD]), ALU.mult).then_inc(tr_free, 1)
                dve.wait_ge(rth_ready, b * NC + c + 1)
                if not (isinstance(b, int) and b * NC + c == 0):
                    dve.wait_ge(outg_ready, b * NC + c)
                v.scalar_tensor_tensor(out=GR[:, c % 2, :], in0=RTH[:, :], scalar=1.0, in1=PJ[0][:, :],
                                       op0=ALU.add, op1=ALU.mult).then_inc(pj_free[0], 1)

            def weigh(b, c):
                n = b * NC + c
                for hf in range(2):
                    dve.wait_ge(st_full, 2 * n + hf + 1)
                    dve.wait_ge(decay_ready, 2 * n + hf + 2)
                    v.tensor_tensor(PT[:, hf, :, :].rearrange("p m t -> p (m t)"), SB[hf][:, :],
                                    DT[:, hf, :, :].rearrange("p m t -> p (m t)"), ALU.mult).then_inc(pt_ready, 1)

            def collect(b, c):
                n = b * NC + c
                hn = HN[:, :, :].rearrange("p (m two) d -> p two m d", two=2)
                e1 = E12[:, c, 0, :].rearrange("p (m two) -> p two m", two=2)
                for hf in range(2):
                    dve.wait_ge(hv_full, 2 * n + hf + 1)
                    do(v.tensor_tensor(hn[:, hf], NB_[hf][:, 0:260].rearrange("p (m d) -> p m d", m=4),
                                       bc(e1[:, hf], [P, 4, HD + 1]), ALU.mult))
                    v.tensor_tensor(hn[:, hf], hn[:, hf], SB[hf][:, 0:260].rearrange("p (m d) -> p m d", m=4),
                                    ALU.add).then_inc(hv_read, 1)
                if c < NC - 1:
                    dve.wait_ge(*tr_full_at(b, f"u{c}"))
                    if c == 0:
                        dve.wait_ge(cs_ready, b + 1)
                    do(v.tensor_tensor(CS[:, :, :], CS[:, :, :], bc(DEC[:, c, :], [P, NP_, HD + 1]), ALU.mult))
                    v.tensor_tensor(CS[:, :, :], CS[:, :, :], TR[:, 0:260].rearrange("p (m d) -> p m d", m=4),
                                    ALU.add).then_inc(tr_free, 1)
                    dve.wait_ge(*tr_read_at(b, f"u{c}"))

            def centre(b, c):
                n = b * NC + c
                dve.wait_ge(hv_read, 2 * n + 3)
                do(v.tensor_scalar(DN[:, 0, :], HN[:, :, HD], 1.0, 2.0, ALU.max, ALU.mult))
                do(v.reciprocal(DN[:, 1, :], DN[:, 0, :]))
                do(v.tensor_tensor(H2[:, :, :], HN[:, :, 0:HD], bc(DN[:, 1, :], [P, H, HD]), ALU.mult))
                dve.wait_ge(*pj_read_at(b, pj_use(c, "o")))
                flat = H2[:, :, :].rearrange("p h d -> p (h d)")
                do(v.scalar_tensor_tensor(out=flat, in0=OT[:, c % 2, :], scalar=1.0, in1=flat,
                                          op0=ALU.add, op1=ALU.mult))
                do(v.tensor_reduce(HS[:, 0, :], H2[:, :, :], AX_X, ALU.add))
                do(v.tensor_scalar(HS[:, 0, :], HS[:, 0, :], 1.0 / HD, None, ALU.mult))
                v.tensor_tensor(H2[:, :, :], H2[:, :, :], bc(HS[:, 0, :], [P, H, HD]), ALU.subtract)\
                 .then_inc(cen_ready, 1)

            def variance(b, c):
                dve.wait_ge(sq_ready, b * NC + c + 1)
                do(v.tensor_reduce(HS[:, 1, :], SQ[:, :, :], AX_X, ALU.add))
                v.tensor_scalar(HS[:, 2, :], HS[:, 1, :], 1.0 / HD, 1e-6, ALU.mult, ALU.add).then_inc(hvar_ready, 1)

            def gate(b, c):
                dve.wait_ge(hn_ready, b * NC + c + 2)
                dve.wait_ge(*pj_read_at(b, pj_use(c, "r")))
                v.tensor_tensor(OUT[:, :], H2[:, :, :].rearrange("p h d -> p (h d)"), GR[:, c % 2, :], ALU.mult)\
                 .then_inc(outg_ready, 1)

            def update_x(b, c):
                dve.wait_ge(*tr_full_at(b, f"d{c}"))
                t = X[:, bass.ds(b * 4 + c, 1), :].rearrange("p a d -> p (a d)")
                v.tensor_tensor(t, t, TR[:, 0:D], ALU.add).then_inc(tr_free, 1)

            def sequence(b, last):
                weigh(b, 0)
                collect(b, 0)
                take(b, 1)
                centre(b, 0)
                weigh(b, 1)
                variance(b, 0)
                collect(b, 1)
                gate(b, 0)
                take(b, 2)
                if not last:
                    norms(b + 1)
                centre(b, 1)
                update_x(b, 0)
                weigh(b, 2)
                variance(b, 1)
                collect(b, 2)
                gate(b, 1)
                take(b, 3)
                if not last:
                    add_u(b + 1)
                centre(b, 2)
                update_x(b, 1)
                weigh(b, 3)
                variance(b, 2)
                collect(b, 3)
                if not last:
                    reset_state()
                    silu(b + 1)
                gate(b, 2)
                centre(b, 3)
                update_x(b, 2)
                if not last:
                    gates(b + 1)
                variance(b, 3)
                if not last:
                    take(b + 1, 0)
                gate(b, 3)
                update_x(b, 3)

            dve.wait_ge(x_loaded, 64)
            ffn(0)
            add_u(0)
            reset_state()
            silu(0)
            gates(0)
            take(0, 0)
            PER = 72
            with dve.Fori(0, NB - 1) as b:
                step.loop(b, PER)
                sequence(b, False)
            step.looped(NB - 1)
            sequence(NB - 1, True)
            dve.wait_ge(*tr_read_at(NB - 1, "d3"))
            ffn(1)


def _shape_constants(np):
    k = np.zeros((P, NCONST), np.float32)

    def put(name, a):
        at, w = CONST[name]
        k[:a.shape[0], at:at + w] = a

    p, c = np.arange(P)[:, None], np.arange(P)[None, :]
    put("ident", np.eye(P))
    put("tri", p < c)
    put("ones", np.ones((P, P)))
    put("mask", np.tile(np.where(p <= c, 0.0, NEG), (1, 4)))
    for part in range(3):
        k[32 * part:32 * part + H, CONST["sel"][0]:CONST["sel"][0] + H * P] = -np.repeat(np.eye(H), P, axis=1)
    put("decl", (np.arange(H)[:, None] % 2) == (np.arange(P)[None, :] >= HD))
    put("decr", (np.arange(H)[:, None] // 2) == np.arange(NP_)[None, :])
    put("rev", np.tile(NE - np.arange(NE), (P, 1)))
    put("thr", np.tile(P * np.arange(NT), (P, 1)))
    put("fill", NT * P + P * np.arange(NBLK)[None, :] + p)
    put("token", P * np.arange(NT)[None, :] + p)
    put("blk", np.tile(np.arange(24), (P, 1)))
    put("reset", np.tile(np.arange(S) % P != 0, (P, 1)))
    put("reset16", np.tile(np.arange(NE * NT) % NT != 0, (P, 1)))
    return k


def kernel(**inputs):
    import numpy as np
    import concourse.bacc as _bacc
    from concourse import mybir as _mybir
    from concourse.bass_utils import run_bass_kernel_spmd as _run

    a = {n.replace("L0_attn_", "").replace("L0_ffn_", "f_"): np.asarray(v) for n, v in inputs.items()}

    def kmajor(w):
        return w.T.reshape(-1, P, w.shape[0]).transpose(1, 0, 2)

    cols = np.zeros((P, NCOL), np.float32)
    cols[:, 0], cols[:, 1] = a["ln_g"], a["ln_b"]
    padded = np.concatenate([np.zeros(3, np.float32), a["b_up_l"]])
    for j in range(2):
        for m in range(4):
            cols[:, COL["bshift"] + 4 * j + m] = padded[j * P + m:j * P + m + P]
        cols[:, COL["bul"] + j] = a["b_up_l"][j * P:(j + 1) * P]
    cols[:, COL["bq"]:COL["bq"] + 4] = a["b_q"].reshape(4, P).T
    cols[:, COL["bk"]:COL["bk"] + 4] = a["b_k"].reshape(4, P).T
    cols[0:H, COL["bif"]], cols[32:32 + H, COL["bif"]] = a["b_i"], a["b_f"]
    rows = np.concatenate([a["b_v"], a["b_o"], a["b_up_r"], a["b_skip"], a["mh_b"].ravel(), a["mh_g"].ravel(),
                           a["b_down"], a["conv_w"], a["conv_b"].reshape(1)])
    gates = np.zeros((P, 2, 40), np.float32)
    gates[:, :, 0:H], gates[:, :, 32:32 + H] = kmajor(a["W_i"]), kmajor(a["W_f"])
    w1 = np.concatenate([a["f_w1"].transpose(1, 0, 2), a["f_b1"].reshape(NE, FC, P).transpose(2, 0, 1)], axis=2)
    arrays = {
        "x": a["x"].reshape(NT * P, D), "consts": _shape_constants(np), "colpack": cols, "rowpack": rows,
        "w_router": a["f_w_router"], "w1": w1, "w2": a["f_w2"].reshape(NE, FC, P, D).transpose(2, 0, 1, 3),
        "b2": a["f_b2"], "wul": a["W_up_l"].reshape(2, P, D).transpose(1, 0, 2),
        "wult": np.concatenate([np.zeros((P, 3), np.float32), a["W_up_l"].T], axis=1), "wurt": a["W_up_r"].T,
        "wqt": kmajor(a["W_q"]), "wkt": kmajor(a["W_k"]), "wskt": kmajor(a["W_skip"]), "wvt": kmajor(a["W_v"]),
        "wot": kmajor(a["W_o"]), "wift": gates, "wdt": kmajor(a["W_down"]),
    }
    nc = _bacc.Bacc("TRN2", target_bir_lowering=False, num_devices=1)
    args = []
    for name, v in arrays.items():
        arrays[name] = v = np.ascontiguousarray(v)
        args.append(nc.dram_tensor(name, v.shape, _mybir.dt.from_np(v.dtype), kind="ExternalInput").ap())
    args.append(nc.dram_tensor("out", (NT * P, D), F32, kind="ExternalOutput").ap())
    macaron(nc, *args)
    r = _run(nc, [arrays], core_ids=[0])
    return r.results[0]["out"].reshape(a["x"].shape)
```

```python
from contextlib import ExitStack

import concourse.bass as bass
from concourse import mybir

F32 = mybir.dt.float32
F32R = mybir.dt.float32r
BF16 = mybir.dt.bfloat16
I32 = mybir.dt.int32
U32 = mybir.dt.uint32
ALU = mybir.AluOpType
ACT = mybir.ActivationFunctionType
AX_X = mybir.AxisListType.X

P = 128
D = 128
NT = 16
NB = 4
NC = 4
S = NC * P
NE = 8
F = 512
FC = F // P
NBLK = NT + NE - 1
W1C = F + FC
SLOT = D + 1
RING = 4
H = 8
HD = 64
HID = H * HD
NP_ = H // 2
CAP = 15.0
NEG = -1.0e30

CONST = {}
_at = 0
for _n, _w in (("ident", 128), ("tri", 128), ("ones", 128), ("mask", 512), ("sel", 1024), ("decl", 128),
               ("decr", 4), ("fill", 23), ("token", 16), ("rev", 8), ("thr", 16), ("blk", 24),
               ("reset", 512), ("reset16", 128)):
    CONST[_n] = (_at, _w)
    _at += _w
NCONST = _at
FIRST = CONST["mask"][0]
COL = {"g": 0, "b": 1, "bshift": 2, "bul": 10, "bq": 12, "bk": 16, "bif": 20}
NCOL = 21
BROW = {"bv": 0, "bo": 512, "br": 1024, "bsk": 1536}
ROW = {"mhb": 0, "mhg": 512, "bdown": 1024, "cw": 1152, "cb": 1156}
NBROW, NROW = 2048, 1157


class Steps:

    def __init__(self, eng, sem):
        self.eng, self.sem, self.base, self.n = eng, sem, 0, 0

    def did(self, ins):
        ins.then_inc(self.sem, 1)
        self.n += 1

    def do(self, ins):
        self.did(ins)
        self.eng.wait_ge(self.sem, self.base + self.n)

    def settle(self):
        self.eng.wait_ge(self.sem, self.base + self.n)

    def loop(self, i, per):
        self.before = self.base + self.n
        self.base, self.n, self.per = self.before + i * per, 0, per

    def looped(self, count):
        assert self.n == self.per, (self.n, self.per)
        self.base, self.n = self.before + count * self.per, 0


def macaron(nc, x, consts, colpack, rowpack, w_router, w1, w2, b2, wul, wult, wurt, wqt, wkt, wskt, wvt, wot,
            wift, wdt, out):
    x_v = x.rearrange("(t p) d -> p t d", p=P)
    out_v = out.rearrange("(t p) d -> p t d", p=P)
    slots = [nc.dram_tensor(f"slots_{f}", [NBLK * P, SLOT], F32, kind="Internal").ap() for f in range(2)]
    by_token = [nc.dram_tensor(f"by_token_{f}", [NT * P + NBLK * P, D], F32, kind="Internal").ap() for f in range(2)]

    with ExitStack() as ctx:
        def sb(name, shape, dt=F32):
            return ctx.enter_context(nc.sbuf_tensor(name, shape, dt))

        def sem(name):
            return ctx.enter_context(nc.semaphore(name))

        bank = [ctx.enter_context(nc.psum_tensor(f"bank{i}", [P, 512], F32)) for i in range(8)]

        with ExitStack() as first:
            def whole(name, shape):
                return first.enter_context(nc.sbuf_tensor(name, shape, F32))

            W2 = whole("W2", [P, NE, FC, D])
            BROWS = whole("BROWS", [P, 4 * HID])
            WQT, WKT, WSKT = (whole(name, [P, 2, HID]) for name in ("WQT", "WKT", "WSKT"))
            WVF, WOF, WURT = (whole(name, [P, HID]) for name in ("WVF", "WOF", "WURT"))
            WCT, WIFT = whole("WCT", [P, 256]), whole("WIFT", [P, 2, 40])
            XT, XC = whole("XT", [P, 512]), whole("XC", [P, 2, 512])
        with ExitStack() as second:
            second.enter_context(nc.sbuf_tensor("BEFORE_XN1", [P, NE * FC * D + 4 * HID], F32))
            XN1 = second.enter_context(nc.sbuf_tensor("XN1", [P, NT, SLOT], F32))
        WQH, WKH, WSKH = (sb(name, [P, 2, HID], F32R) for name in ("WQH", "WKH", "WSKH"))
        XCH = sb("XCH", [P, 2, 512], F32R)
        WVH, WOH, WURH, XTH = (sb(name, [P, HID], F32R) for name in ("WVH", "WOH", "WURH", "XTH"))
        WQL, WKL, WSKL = (sb(name, [P, 2, HID], F32R) for name in ("WQL", "WKL", "WSKL"))
        WVL, WOL, WURL = (sb(name, [P, HID], F32R) for name in ("WVL", "WOL", "WURL"))
        WCL, WIFL = sb("WCL", [P, 256], F32R), sb("WIFL", [P, 2, 40], F32R)
        XTL, XCL = sb("XTL", [P, 512], F32R), sb("XCL", [P, 2, 512], F32R)

        X = sb("X", [P, NT, D])
        K = sb("K", [P, NCONST])
        COLS = sb("COLS", [P, NCOL])
        ROWS = sb("ROWS", [P, NROW])
        W1 = sb("W1", [P, NE, W1C])
        B2 = sb("B2", [P, NE, D])
        WR = sb("WR", [P, NE])
        WUL = sb("WUL", [P, 2, D])
        WULT = sb("WULT", [P, 3 + 256])
        WCH, WIFH = sb("WCH", [P, 256], F32R), sb("WIFH", [P, 2, 40], F32R)
        WVT = sb("WVT", [P, 2, HID])
        WOT = sb("WOT", [P, 2, HID])
        WDT = sb("WDT", [P, FC, D])
        HBX = sb("HBX", [P, 2])
        BSH = sb("BSH", [P, 2, 4])
        IDB = sb("IDB", [P, P], BF16)
        MASKB = sb("MASKB", [P, 512], BF16)
        BULB = sb("BULB", [P, 2, P])
        BIAS3 = sb("BIAS3", [65, 4 * HID], BF16)
        SK23 = sb("SK23", [P, 2, HID])
        BMID = SK23[0:1, :, :].rearrange("p i n -> p (i n)").bitcast(BF16)
        ONES3 = sb("ONES3", [65, P], BF16)
        SEL3 = sb("SEL3", [72, H * P], BF16)

        def const(name):
            a, w = CONST[name]
            return K[:, a:a + w]

        def row(name, w):
            if name in BROW:
                return BROWS[:, BROW[name]:BROW[name] + w]
            return ROWS[:, ROW[name]:ROW[name] + w]

        def col(name, i=0, lo=0, hi=P):
            return COLS[lo:hi, COL[name] + i:COL[name] + i + 1]

        ident = const("ident")

        XN0 = sb("XN0", [P, NT, SLOT])
        XN = [XN0, XN1]
        XNT = sb("XNT", [P, 4, 512])
        ST = sb("ST", [P, NT, 6])
        LNA = sb("LNA", [P, 8, NT])
        EX = sb("EX", [P, NT, NE])
        OH = sb("OH", [P, NT, NE])
        RT = sb("RT", [P, 8, NT])
        TOTE = sb("TOTE", [P, NE, NT])
        INCL = sb("INCL", [P, NE, NT])
        RK = sb("RK", [P, NT, NE])
        CMP = sb("CMP", [P, NE, NT])
        EB = sb("EB", [P, 8, NE])
        BE = sb("BE", [P, 24, NE])
        EIDF = sb("EIDF", [P, 24])
        EID = sb("EID", [P, 24], I32)
        POS = sb("POS", [P, NT], U32)
        MHALF = sb("MHALF", [P, NT])
        XB = sb("XB", [P, RING, SLOT])
        IDX = sb("IDX", [P, RING], U32)
        XBT = sb("XBT", [P, 2, P])
        W1R = sb("W1R", [P, 2, W1C])
        HT = sb("HT", [P, 2, FC, P])
        YB = sb("YB", [P, RING, D])

        QKT = sb("QKT", [P, 8, 512])
        QT, KT = QKT[:, 0:4, :], QKT[:, 4:8, :]
        FILL = QKT[:, :, :].rearrange("p a n -> p (a n)")[:, 0:NBLK * SLOT].rearrange("p (k w) -> p k w", w=SLOT)
        YG = QT.rearrange("p a (t d) -> p (a t) d", d=D)
        ZB = sb("ZB", [P, 4, D])
        UB = sb("UB", [P, 4, D])
        SA = sb("SA", [P, 4, 6])
        LA = sb("LA", [P, 12, 4])
        YH = XNT[:, 0:2, :]
        TH = XNT[:, 2:4, :]
        TIF = sb("TIF", [40, 512])
        F15 = sb("F15", [H, 512])
        FS = sb("FS", [H, 512])
        GT = sb("GT", [96, 512])
        MM = sb("MM", [H, 512])
        MMID = sb("MMID", [H, 512], BF16)
        M3 = sb("M3", [72, 512], BF16)
        MIN = sb("MIN", [H, NC + 1])
        G3 = sb("G3", [H, NC])
        G3M = sb("G3M", [H, NC, NP_])
        AC = sb("AC", [P, NC, H])
        EW = sb("EW", [P, NC, H])
        DEC = sb("DEC", [P, NC, NP_])
        MINM = sb("MINM", [H, NC, NP_])
        MINB = sb("MINB", [P, NC, NP_])
        E1 = sb("E1", [P, NP_, P])
        QS = sb("QS", [P, NP_, P])
        KW = sb("KW", [P, 2, H, HD])
        VX = sb("VX", [P, 2, H, HD + 1])
        RTH = sb("RTH", [P, HID])
        xn_flat = XN0[:, :, :].rearrange("p t w -> p (t w)")
        OT = xn_flat[:, 0:2 * HID].rearrange("p (i n) -> p i n", i=2)
        sel_at = CONST["sel"][0]
        GR = [xn_flat[:, 2 * HID:3 * HID], xn_flat[:, 3 * HID:4 * HID],
              K[:, sel_at:sel_at + HID], K[:, sel_at + HID:sel_at + 2 * HID]]
        SK = [HT[:, i, :, :].rearrange("p c t -> p (c t)") for i in range(2)] + [SK23[:, i, :] for i in range(2)]
        DT = WVT[:, :, :].rearrange("p i (m t) -> p i m t", t=P)
        PT = WOT[:, :, :].rearrange("p i (m t) -> p i m t", t=P)
        w1r_flat = W1R[:, :, :].rearrange("p i n -> p (i n)")
        H2 = w1r_flat[:, 0:HID].rearrange("p (h d) -> p h d", h=H)
        SQ = w1r_flat[:, HID:2 * HID].rearrange("p (h d) -> p h d", h=H)
        CS = sb("CS", [P, NP_, HD + 1])
        DN = sb("DN", [P, 2, 2, NP_])
        HS = sb("HS", [P, 4, H])
        OUT = sb("OUT", [P, HID])
        B2R = OUT[:, :].rearrange("p (j d) -> p j d", j=RING)
        OUTT = sb("OUTT", [P, FC, P])
        CREDIT = sb("CREDIT", [1, 10])

        x_loaded = [sem(f"x_loaded_{q}") for q in range(4)]
        first_loaded, consts_loaded, cols_loaded = sem("first_loaded"), sem("consts_loaded"), sem("cols_loaded")
        ffn_loaded, attn_loaded = sem("ffn_loaded"), sem("attn_loaded")
        cleared, constants_cast = sem("cleared"), sem("constants_cast")
        fill_made, out_stored = sem("fill_made"), sem("out_stored")
        slots_filled = [sem(f"slots_filled_{f}") for f in range(2)]
        dve_step, pool_step = sem("dve_step"), sem("pool_step")

        def per_ffn(name):
            return [sem(f"{name}_{f}") for f in range(2)]

        def per_ffn_ring(name, n=RING):
            return [[sem(f"{name}_{f}_{i}") for i in range(n)] for f in range(2)]

        var_ready, rstd_ready, xn_ready = per_ffn("var_ready"), per_ffn("rstd_ready"), per_ffn("xn_ready")
        xt_full, xt_copied, logits_full = per_ffn("xt_full"), per_ffn("xt_copied"), per_ffn("logits_full")
        shifted, exp_ready, onehot_ready = per_ffn("shifted"), per_ffn("exp_ready"), per_ffn("onehot_ready")
        ranks_full, pos_ready, scattered = per_ffn("ranks_full"), per_ffn("pos_ready"), per_ffn("scattered")
        eid_ready, xb_loaded = per_ffn("eid_ready"), per_ffn_ring("xb_loaded")
        xbt_full, xbt_copied, w1_copied = per_ffn("xbt_full"), per_ffn("xbt_copied"), per_ffn("w1_copied")
        idx_copied = per_ffn("idx_copied")
        h_full, relu_act, relu_dve = per_ffn("h_full"), per_ffn("relu_act"), per_ffn("relu_dve")
        y_full, y_ready, y_sent = per_ffn("y_full"), per_ffn("y_ready"), per_ffn_ring("y_sent")
        y_loaded, ffn_done = per_ffn_ring("y_loaded"), per_ffn("ffn_done")
        folds_ready, fold_full, fold_copied = sem("folds_ready"), sem("fold_full"), sem("fold_copied")
        attn_consts = sem("attn_consts")

        w2_loaded, w_high, w_low = sem("w2_loaded"), sem("w_high"), sem("w_low")
        xt_low, xc_high, xc_low = sem("xt_low"), sem("xc_high"), sem("xc_low")
        a_var, a_rstd, z_ready, u_ready = sem("a_var"), sem("a_rstd"), sem("z_ready"), sem("u_ready")
        a_var2, a_rstd2, ubd_ready = sem("a_var2"), sem("a_rstd2"), sem("ubd_ready")
        pj_full, pj_free = sem("pj_full"), [sem(f"pj_free_{i}") for i in range(2)]
        tr_full, tr_free = sem("tr_full"), sem("tr_free")
        tanh_ready, xc_ready, rows_ready = sem("tanh_ready"), sem("xc_ready"), sem("rows_ready")
        rth_ready, m3_ready = sem("rth_ready"), sem("m3_ready")
        dm_full, dm_free, st_full, pt_ready = sem("dm_full"), sem("dm_free"), sem("st_full"), sem("pt_ready")
        hv_full, hv_read, cs_ready, qs_ready = sem("hv_full"), sem("hv_read"), sem("cs_ready"), sem("qs_ready")
        cen_ready, sq_ready, hvar_ready = sem("cen_ready"), sem("sq_ready"), sem("hvar_ready")
        hn_ready, outg_ready = sem("hn_ready"), sem("outg_ready")

        PJ = bank[0:2]
        TR, DM = bank[2], bank[3]
        SB = bank[4:6]
        NB_ = bank[6:8]
        PJ_USES = ["z", "x0", "x1", "v0", "o0", "r0", "gates", "q0", "q1", "q2", "q3", "k0", "k1", "k2", "k3", "s0",
                   *(f"{what}{c}" for c in range(1, NC) for what in "vors")]
        NPJ = len(PJ_USES)
        TR_USES = ["k0", "k1", "u0", "k2", "u1", "o0", "d0", "k3", "u2", "o1", "d1", "o2", "d2", "o3", "d3"]
        NTR = len(TR_USES)

        def pj_bank(use):
            return PJ_USES.index(use) % 2

        def pj_full_at(b, use):
            return pj_full, b * NPJ + PJ_USES.index(use) + 1

        def pj_read_at(b, use):
            return pj_free[pj_bank(use)], b * (NPJ // 2) + PJ_USES.index(use) // 2 + 2

        DM_USES = ["columns", *(f"{what}{c}" for c in range(NC) for what in ("even", "odd", "state"))]
        NDM = len(DM_USES)

        def dm_full_at(b, use):
            return dm_full, b * NDM + DM_USES.index(use) + 1

        def dm_read_at(b, use):
            return dm_free, b * NDM + DM_USES.index(use) + 2

        def tr_at(b, use):
            return b * NTR + TR_USES.index(use) + 1

        def tr_read_at(b, use):
            return tr_free, tr_at(b, use) + 1

        def tr_full_at(b, use):
            return tr_full, tr_at(b, use)

        block = ctx.enter_context(nc.Block())

        def over_blocks(eng, turn):
            for j in range(RING):
                turn(j, j, 0)
            with eng.Fori(1, NBLK // RING) as n:
                for j in range(RING):
                    turn(RING * n + j, j, n)
            for j in range(NBLK % RING):
                turn(NBLK // RING * RING + j, j, NBLK // RING)

        GROUPS = [[(0, NT // 2), (NT // 2, NT)], [(0, NT - 4), (NT - 4, NT)]]

        TAIL = NBLK // RING * RING

        @block.sync
        def _(sp):
            for q in range(4):
                sp.dma_start(X[:, 4 * q:4 * q + 4, :], x_v[:, 4 * q:4 * q + 4, :]).then_inc(x_loaded[q], 16)
            sp.dma_start(K[:, FIRST:], consts[:, FIRST:]).then_inc(consts_loaded, 16)
            sp.dma_start(COLS[:, :], colpack).then_inc(cols_loaded, 16)
            sp.dma_start(BROWS[:, :], rowpack[0:NBROW].partition_broadcast(P)).then_inc(cols_loaded, 16)
            sp.dma_start(ROWS[:, :], rowpack[NBROW:NBROW + NROW].partition_broadcast(P)).then_inc(cols_loaded, 16)
            sp.wait_ge(fill_made, 1)
            sp.dma_start(slots[0].rearrange("(k p) w -> p k w", p=P), FILL).then_inc(slots_filled[0], 16)
            sp.dma_start(W1[:, :, :], w1).then_inc(ffn_loaded, 16)
            sp.dma_start(W2[:, :, :, :], w2).then_inc(ffn_loaded, 16)
            sp.dma_start(B2[:, :, :], b2.partition_broadcast(P)).then_inc(ffn_loaded, 16)
            sp.dma_start(slots[1].rearrange("(k p) w -> p k w", p=P), FILL).then_inc(slots_filled[1], 16)

            for f in range(2):
                if f == 1:
                    sp.wait_ge(pj_full, NB * NPJ)
                    sp.dma_start(W2[:, :, :, :], w2).then_inc(w2_loaded, 16)

                def load_block(k, j):
                    sp.dma_start(XB[:, j, :], slots[f][bass.ds(k * P, P), :]).then_inc(xb_loaded[f][j], 16)

                def turn(k, j, n):
                    if isinstance(k, int) and k + RING >= NBLK:
                        return
                    sp.wait_ge(xbt_full[f], k + 1)
                    sp.wait_ge(idx_copied[f], k + 1)
                    load_block(k + RING, j)

                sp.wait_ge(scattered[f], 16 * NT)
                for j in range(RING):
                    load_block(j, j)
                with sp.Fori(0, TAIL // RING - 1) as n:
                    for j in range(RING):
                        turn(RING * n + j, j, n)
                for k in range(TAIL - RING, NBLK):
                    turn(k, k % RING, k // RING)
                for j in range(RING):
                    sp.wait_ge(y_sent[f][j], 16 * len(range(j, NBLK, RING)))
                if f == 0:
                    sp.wait_ge(slots_filled[1], 16)
                for q in range(4):
                    sp.dma_start(YG[:, 4 * q:4 * q + 4, :], by_token[f][512 * q:512 * (q + 1), :]
                                 .rearrange("(t p) d -> p t d", p=P)).then_inc(y_loaded[f][q], 16)
            for g in range(4):
                sp.wait_ge(ffn_done[1], 4 * g + 4)
                sp.dma_start(out_v[:, 4 * g:4 * g + 4, :], X[:, 4 * g:4 * g + 4, :]).then_inc(out_stored, 16)
            sp.wait_ge(out_stored, 64)

        @block.gpsimd
        def _(pool):
            g = nc.gpsimd
            step = Steps(pool, pool_step)
            step.did(g.memset(MHALF[:, :], -0.5))
            step.did(g.memset(FILL, 0.0))
            step.settle()

            def rstd(f, group):
                lo, hi = GROUPS[f][group]
                pool.wait_ge(var_ready[f], group + 1)
                g.tensor_tensor(LNA[:, 5, lo:hi], LNA[:, 4, lo:hi], MHALF[:, lo:hi], ALU.pow).then_inc(rstd_ready[f], 1)

            def token_numbers(f):
                step.do(g.tensor_copy(XN[f][:, :, D], const("token")))

            def ffn(f):
                if f == 0:
                    rstd(0, 0)
                rstd(f, 1)
                if f == 0:
                    pool.wait_ge(consts_loaded, 16)
                    g.tensor_copy(FILL[:, :, D], const("fill")).then_inc(fill_made, 1)
                    for buffer, value in ((ONES3[:, :], 1.0), (M3[:, :], 0.0), (GT[:, :], 0.0), (VX[:, :, :, :], 1.0)):
                        g.memset(buffer, value)
                    g.memset(BIAS3[:, :].bitcast(U32), 0).then_inc(cleared, 1)
                token_numbers(f)
                pool.wait_ge(slots_filled[f], 16)
                pool.wait_ge(pos_ready[f], 1)
                for t in range(NT):
                    g.indirect_dma_start(out=slots[f], out_offset=bass.IndirectOffsetOnAxis(ap=POS[:, t:t + 1], axis=0),
                                         in_=XN[f][:, t, :], in_offset=None).then_inc(scattered[f], 16)
                for k in range(NBLK):
                    j = k % RING
                    pool.wait_ge(y_ready[f], k + 1)
                    g.indirect_dma_start(out=by_token[f],
                                         out_offset=bass.IndirectOffsetOnAxis(ap=IDX[:, j:j + 1], axis=0),
                                         in_=YB[:, j, :], in_offset=None).then_inc(y_sent[f][j], 16)

            def norms(b):
                pool.wait_ge(a_var, b + 1)
                g.tensor_tensor(LA[:, 5, :], LA[:, 4, :], MHALF[:, 0:4], ALU.pow).then_inc(a_rstd, 1)
                pool.wait_ge(a_var2, b + 1)
                g.tensor_tensor(LA[:, 8, :], LA[:, 7, :], MHALF[:, 0:4], ALU.pow).then_inc(a_rstd2, 1)

            def add_bdown(b):
                pool.wait_ge(z_ready, b + 1)
                g.tensor_tensor(UB[:, :, :], UB[:, :, :],
                                row("bdown", D).unsqueeze(1).to_broadcast([P, 4, D]), ALU.add).then_inc(ubd_ready, 1)

            def head_norm(b, c):
                n = b * NC + c
                pool.wait_ge(hvar_ready, n + 1)
                step.do(g.tensor_tensor(HS[:, 3, :], HS[:, 2, :], MHALF[:, 0:H], ALU.pow))
                step.do(g.tensor_tensor(H2[:, :, :], H2[:, :, :],
                                        HS[:, 3, :].unsqueeze(2).to_broadcast([P, H, HD]), ALU.mult))
                step.do(g.tensor_tensor(H2[:, :, :], H2[:, :, :],
                                        row("mhg", HID).rearrange("p (h d) -> p h d", h=H), ALU.mult))
                pool.wait_ge(*pj_read_at(b, f"s{c}"))
                g.tensor_tensor(H2[:, :, :].rearrange("p h d -> p (h d)"), H2[:, :, :].rearrange("p h d -> p (h d)"),
                                SK[c], ALU.add).then_inc(hn_ready, 1)

            def sequence(b, last):
                head_norm(b, 0)
                if not last:
                    norms(b + 1)
                if last:
                    rstd(1, 0)
                head_norm(b, 1)
                if not last:
                    add_bdown(b + 1)
                head_norm(b, 2)
                head_norm(b, 3)

            ffn(0)
            pool.wait_ge(cols_loaded, 48)
            norms(0)
            add_bdown(0)
            with pool.Fori(0, NB - 1) as b:
                step.loop(b, 3 * NC)
                sequence(b, False)
            step.looped(NB - 1)
            sequence(NB - 1, True)
            ffn(1)

        @block.scalar
        def _(act):
            a = nc.scalar
            act.dma_start(K[:, 0:FIRST], consts[:, 0:FIRST]).then_inc(first_loaded, 16)
            act.dma_start(WR[:, :], w_router).then_inc(first_loaded, 16)
            for dst, src in ((WUL[:, :, :], wul), (WULT[:, :], wult), (WURT[:, :], wurt), (WQT[:, :, :], wqt),
                             (WKT[:, :, :], wkt), (WSKT[:, :, :], wskt), (WVT[:, :, :], wvt), (WOT[:, :, :], wot),
                             (WIFT[:, :, :], wift), (WDT[:, :, :], wdt)):
                act.dma_start(dst, src).then_inc(attn_loaded, 16)

            def xn_channels(f, q):
                act.wait_ge(xt_full[f], q + 1)
                a.activation(XNT[:, q, :], bank[q % 2][:, :], ACT.Copy).then_inc(xt_copied[f], 1)

            def ffn(f):
                for q in range(3 * f, 4):
                    xn_channels(f, q)
                act.wait_ge(shifted[f], 1)
                a.activation(EX[:, :, :], EX[:, :, :], ACT.Exp).then_inc(exp_ready[f], 1)
                if f == 0:
                    act.wait_ge(consts_loaded, 16)
                    a.activation(IDB[:, :], ident, ACT.Copy)
                    a.activation(MASKB[:, :], const("mask"), ACT.Copy)
                    a.activation(SEL3[:, :], const("sel")[0:72, :], ACT.Copy).then_inc(constants_cast, 1)
                    for i, dst in enumerate((WVF, WOF)):
                        act.wait_ge(fold_full, 2 * i + 1)
                        a.activation(dst[:, :], bank[4 + 2 * i][:, :], ACT.Copy).then_inc(fold_copied, 1)

                def x_block(k, j):
                    act.wait_ge(xbt_full[f], k + 1)
                    a.activation(XBT[:, j % 2, :], bank[j % 2][:, 0:P], ACT.Copy).then_inc(xbt_copied[f], 1)

                def relu(k, j):
                    act.wait_ge(h_full[f], 2 * k + 1)
                    for c in range(2):
                        ins = a.activation(HT[:, j % 2, c, :], bank[2 + j % 2][:, c * P:(c + 1) * P], ACT.Relu,
                                           bias=W1R[:, j % 2, F + c:F + c + 1])
                    ins.then_inc(relu_act[f], 1)

                def turn(k, j, n):
                    if not (isinstance(k, int) and k + 2 >= NBLK):
                        x_block(k + 2, (j + 2) % RING)
                    if not (isinstance(k, int) and k + 1 >= NBLK):
                        relu(k + 1, (j + 1) % RING)

                x_block(0, 0)
                x_block(1, 1)
                relu(0, 0)
                over_blocks(act, turn)

            def head_in(b):
                act.wait_ge(*pj_full_at(b, "z"))
                a.activation(XT[:, :], PJ[0][:, :], ACT.Identity, scale=col("g"), bias=col("b"))
                a.activation(XTH[:, :], PJ[0][:, :], ACT.Identity, scale=col("g"), bias=col("b"))\
                 .then_inc(pj_free[0], 1)

            def head_silu(b):
                act.wait_ge(xc_ready, b + 1)
                for j in range(2):
                    act.wait_ge(*pj_full_at(b, f"x{j}"))
                    i = pj_bank(f"x{j}")
                    a.activation(YH[:, j, :], PJ[i][:, :], ACT.Identity, scale=0.5, bias=HBX[:, j:j + 1])\
                     .then_inc(pj_free[i], 1)
                act.wait_ge(*pj_read_at(b, "x0"))
                act.wait_ge(*pj_read_at(b, "x1"))
                a.activation(TH, YH, ACT.Tanh).then_inc(tanh_ready, 1)

            def round_xc(b):
                act.wait_ge(xc_ready, b + 2)
                a.activation(XCH[:, :, :], XC[:, :, :], ACT.Copy).then_inc(xc_high, 1)

            def head_gates(b):
                act.wait_ge(*pj_full_at(b, "gates"))
                i = pj_bank("gates")
                a.activation(TIF[0:H, :], PJ[i][0:H, :], ACT.Tanh, scale=1.0 / CAP, bias=col("bif", 0, 0, H))
                a.activation(TIF[32:32 + H, :], PJ[i][32:32 + H, :], ACT.Tanh, scale=1.0 / CAP,
                             bias=col("bif", 0, 32, 32 + H)).then_inc(pj_free[i], 1)

            def head_qk(b, m):
                use = f"q{m}" if m < 4 else f"k{m - 4}"
                act.wait_ge(*pj_full_at(b, use))
                i = pj_bank(use)
                a.activation(QKT[:, m, :], PJ[i][:, :], ACT.Identity, bias=col("bq", m)).then_inc(pj_free[i], 1)

            def head_columns(b):
                act.wait_ge(*dm_full_at(b, "columns"))
                cols = DM[:, 0:NC * 96].rearrange("p (c r) -> p c r", c=NC)
                per_chunk = DM[:, 384:384 + 2 * NC * NP_].rearrange("p (i c m) -> p i c m", i=2, c=NC)
                a.activation(AC[:, :, :], cols[:, :, 0:H], ACT.Copy)
                a.activation(EW[:, :, :], cols[:, :, 64:64 + H], ACT.Exp)
                a.activation(MINB[:, :, :], per_chunk[:, 1], ACT.Copy)
                a.activation(DEC[:, :, :], per_chunk[:, 0], ACT.Exp).then_inc(dm_free, 1)
                act.wait_ge(*dm_read_at(b, "columns"))

            def take(b, c, what):
                act.wait_ge(*pj_full_at(b, f"{what}{c}"))
                i = pj_bank(f"{what}{c}")
                if what == "v":
                    a.activation(VX[:, c % 2, :, 0:HD], PJ[i][:, :].rearrange("p (h d) -> p h d", h=H), ACT.Copy)\
                        .then_inc(pj_free[i], 1)
                elif what == "o":
                    a.activation(OT[:, c % 2, :], PJ[i][:, :], ACT.Tanh, scale=0.5).then_inc(pj_free[i], 1)
                elif what == "r":
                    a.activation(RTH[:, :], PJ[i][:, :], ACT.Tanh, scale=0.5).then_inc(rth_ready, 1)
                else:
                    a.activation(SK[c], PJ[i][:, :], ACT.Copy).then_inc(pj_free[i], 1)

            def decays(b, c, hf):
                n = b * NC + c
                act.wait_ge(pt_ready, 2 * n + 1)
                act.wait_ge(*dm_full_at(b, f"{('even', 'odd')[hf]}{c}"))
                for m in range(4):
                    h = 2 * m + hf
                    ins = a.activation(DT[:, hf, m, :], DM[:, m * P:(m + 1) * P], ACT.Exp, bias=AC[:, c, h:h + 1])
                ins.then_inc(dm_free, 1)

            def state_decays(b, c):
                n = b * NC + c
                act.wait_ge(qs_ready, n + 1)
                act.wait_ge(*dm_full_at(b, f"state{c}"))
                for m in range(4):
                    ins = a.activation(E1[:, m, :], DM[:, m * P:(m + 1) * P], ACT.Exp, bias=MINB[:, c, m:m + 1])
                ins.then_inc(dm_free, 1)

            def squares(b, c):
                act.wait_ge(cen_ready, b * NC + c + 1)
                a.activation(SQ[:, :, :], H2[:, :, :], ACT.Square).then_inc(sq_ready, 1)

            def out_t(b, c):
                act.wait_ge(*tr_full_at(b, f"o{c}"))
                a.activation(OUTT[:, :, :].rearrange("p m t -> p (m t)"), TR[:, :], ACT.Copy).then_inc(tr_free, 1)

            def chunk(b, c, last):
                nxt = (b, c + 1) if c < NC - 1 else None if last else (b + 1, 0)
                decays(b, c, 0)
                if c >= 2:
                    out_t(b, c - 2)
                if last and c == 3:
                    xn_channels(1, 0)
                if nxt:
                    take(*nxt, "v")
                decays(b, c, 1)
                if c:
                    squares(b, c - 1)
                if last and c == 3:
                    xn_channels(1, 1)
                if nxt:
                    take(*nxt, "o")
                state_decays(b, c)
                if nxt:
                    take(*nxt, "r")
                if c < NC - 1:
                    take(*nxt, "s")
                elif not last:
                    round_xc(b + 1)
                    head_gates(b + 1)
                else:
                    xn_channels(1, 2)
                if c == 2 and not last:
                    head_in(b + 1)
                    head_silu(b + 1)

            def sequence(b, last):
                for c in range(NC):
                    chunk(b, c, last)
                if not last:
                    for m in range(3):
                        head_qk(b + 1, m)
                squares(b, 3)
                if not last:
                    head_qk(b + 1, 3)
                out_t(b, 2)
                if not last:
                    for m in range(4, 8):
                        head_qk(b + 1, m)
                    take(b + 1, 0, "s")
                out_t(b, 3)
                if not last:
                    head_columns(b + 1)

            def split_weights():
                act.wait_ge(y_full[0], NBLK)
                act.wait_ge(attn_consts, 1)
                for high, weights in ((WVH, WVF), (WOH, WOF), (WURH, WURT)):
                    a.activation(high[:, :], weights[:, :], ACT.Copy).then_inc(w_high, 1)
                for high, weights in ((WQH, WQT), (WKH, WKT), (WSKH, WSKT)):
                    a.activation(high[:, :, :], weights[:, :, :], ACT.Copy).then_inc(w_high, 1)

            ffn(0)
            split_weights()
            head_in(0)
            head_silu(0)
            take(0, 0, "v")
            take(0, 0, "o")
            round_xc(0)
            take(0, 0, "r")
            head_gates(0)
            for m in range(8):
                head_qk(0, m)
            take(0, 0, "s")
            head_columns(0)
            with act.Fori(0, NB - 1) as b:
                sequence(b, False)
            sequence(NB - 1, True)
            ffn(1)

        @block.tensor
        def _(pe):
            t_ = nc.tensor

            def mm(o, l, r, start=True, stop=True):
                return t_.matmul(o, l, r, start=start, stop=stop, skip_group_check=True)

            def mm3(o, l, r, start=True, stop=True):
                mm(o, l[0], r[0], start, False)
                mm(o, l[0], r[1], False, False)
                return mm(o, l[1], r[0], False, stop)

            def xn_channels(f, q):
                pe.wait_ge(xn_ready[f], 4 * q + 4)
                if q >= 2:
                    pe.wait_ge(xt_copied[f], q - 1)
                elif f == 1:
                    pe.wait_ge(*pj_read_at(NB - 1, PJ_USES[NPJ - 2 + q]))
                for j in range(4):
                    ins = t_.transpose(bank[q % 2][:, j * P:(j + 1) * P], XN[f][:, 4 * q + j, 0:D], ident)
                ins.then_inc(xt_full[f], 1)

            def logits(f, q):
                pe.wait_ge(xt_copied[f], q + 1)
                if f == 1:
                    pe.wait_ge(*dm_read_at(NB - 1, DM_USES[-1]))
                for t in range(4 * q, 4 * q + 4):
                    ins = mm(bank[3][:, t * NE:(t + 1) * NE], XNT[:, q, t % 4 * P:(t % 4 + 1) * P], WR[:, :])
                ins.then_inc(logits_full[f], 1)

            def ffn(f):
                if f == 0:
                    pe.wait_ge(first_loaded, 32)
                for q in range(3 * f, 4):
                    xn_channels(f, q)
                    if q > 3 * f:
                        logits(f, q - 1)
                logits(f, 3)
                pe.wait_ge(onehot_ready[f], 1)
                oh = OH[:, :, :].rearrange("p t e -> p (t e)")
                mm(bank[2][:, 0:P], const("tri"), oh)
                mm(bank[2][:, P:2 * P], const("ones"), oh).then_inc(ranks_full[f], 1)
                if f == 0:
                    pe.wait_ge(attn_loaded, 160)
                    pe.wait_ge(folds_ready, 1)
                    for i, w in enumerate((WVT, WOT)):
                        for j in range(2):
                            ins = mm(bank[4 + 2 * i][:, :], WUL[:, j, :], w[:, j, :], j == 0, j == 1)
                        ins.then_inc(fold_full, 1)
                        for j in range(2):
                            ins = mm(bank[5 + 2 * i][:, :], BULB[:, j, :], w[:, j, :], j == 0, j == 1)
                        ins.then_inc(fold_full, 1)
                    pe.wait_ge(fold_copied, 2)
                    pe.wait_ge(attn_consts, 1)
                pe.wait_ge(ffn_loaded, 48)
                if f == 1:
                    pe.wait_ge(w2_loaded, 16)
                pe.wait_ge(eid_ready[f], 1)

                def turn_x(k, j, n):
                    pe.wait_ge(xb_loaded[f][j], 16 * (n + 1))
                    t_.transpose(bank[j % 2][:, 0:P], XB[:, j, 0:D], ident).then_inc(xbt_full[f], 1)

                def up(k, j):
                    pe.wait_ge(xbt_copied[f], k + 1)
                    pe.wait_ge(w1_copied[f], k + 1)
                    for c in range(FC):
                        ins = mm(bank[2 + j % 2 + 2 * (c // 2)][:, (c % 2) * P:(c % 2 + 1) * P],
                                 W1R[:, j % 2, c * P:(c + 1) * P], XBT[:, j % 2, :])
                        if c % 2:
                            ins.then_inc(h_full[f], 1)

                def down(k, j, e):
                    pe.wait_ge(relu_act[f], k + 1)
                    pe.wait_ge(relu_dve[f], k + 1)
                    if not (isinstance(k, int) and k < 2):
                        pe.wait_ge(y_ready[f], k - 1)
                    for c in range(FC):
                        ins = mm(bank[6 + j % 2][:, 0:D], HT[:, j % 2, c, :], W2[:, e, c, :], c == 0, c == FC - 1)
                    ins.then_inc(y_full[f], 1)

                def turn(k, j, n):
                    e = pe.value_load(EID[0:1, bass.ds(k, 1)], min_val=0, max_val=NE - 1)
                    if not (isinstance(k, int) and k + 2 >= NBLK):
                        turn_x(k + 2, (j + 2) % RING, n + (j + 2) // RING)
                    if not (isinstance(k, int) and k + 1 >= NBLK):
                        up(k + 1, (j + 1) % RING)
                    down(k, j, e)

                turn_x(0, 0, 0)
                turn_x(1, 1, 0)
                up(0, 0)
                over_blocks(pe, turn)

            def pj_wait(b, use):
                u = PJ_USES.index(use)
                pe.wait_ge(pj_free[u % 2], b * (NPJ // 2) + u // 2 + 1)
                return PJ[u % 2]

            def dm_wait(b, use):
                pe.wait_ge(dm_free, b * NDM + DM_USES.index(use) + 1)
                return DM

            def tr_wait(b, use):
                pe.wait_ge(tr_free, tr_at(b, use))
                return TR

            def head_z(b):
                pe.wait_ge(z_ready, b + 1)
                dst = pj_wait(b, "z")
                for j in range(4):
                    ins = t_.transpose(dst[:, j * P:(j + 1) * P], ZB[:, j, :], ident)
                ins.then_inc(pj_full, 1)

            def head_x(b):
                pe.wait_ge(xt_low, b + 1)
                for j in range(2):
                    at = slice(j * P, (j + 1) * P)
                    mm3(pj_wait(b, f"x{j}")[:, :], (WCH[:, at], WCL[:, at]), (XTH[:, :], XTL[:, :]))\
                        .then_inc(pj_full, 1)

            def head_gates(b):
                pe.wait_ge(xc_low, b + 1)
                dst = pj_wait(b, "gates")
                for j in range(2):
                    ins = mm3(dst[0:40, :], (WIFH[:, j, :], WIFL[:, j, :]), (XCH[:, j, :], XCL[:, j, :]),
                              j == 0, j == 1)
                ins.then_inc(pj_full, 1)

            def head_qk(b, high, low, name, between=None):
                for m in range(4):
                    if m == 1 and between:
                        between()
                    dst = pj_wait(b, f"{name}{m}")
                    for j in range(2):
                        at = slice(m * P, (m + 1) * P)
                        ins = mm3(dst[:, :], (high[:, j, at], low[:, j, at]), (XCH[:, j, :], XCL[:, j, :]),
                                  j == 0, j == 1)
                    ins.then_inc(pj_full, 1)

            def head_columns(b):
                pe.wait_ge(rows_ready, b + 1)
                dst = dm_wait(b, "columns")
                for c in range(NC):
                    t_.transpose(dst[:, c * 96:(c + 1) * 96], GT[:, c * P:(c + 1) * P], ident[0:96, 0:96])
                for i, per_chunk in enumerate((G3M, MINM)):
                    ins = mm(dst[:, 384 + i * NC * NP_:384 + (i + 1) * NC * NP_], const("decl")[0:H, :],
                             per_chunk[:, :, :].rearrange("p c m -> p (c m)"))
                ins.then_inc(dm_full, 1)

            def k_tokens(b, c):
                dst = tr_wait(b, f"k{c}")
                for m in range(4):
                    ins = t_.transpose(dst[:, m * P:(m + 1) * P], KT[:, m, c * P:(c + 1) * P], ident)
                ins.then_inc(tr_full, 1)

            def project(b, c, what):
                at = slice(c * P, (c + 1) * P)
                i = "vors".index(what)
                if what == "s":
                    parts = [((XCH[:, j, at], XCL[:, j, at]), (WSKH[:, j, :], WSKL[:, j, :])) for j in range(2)]
                else:
                    high, low = {"v": (WVH, WVL), "o": (WOH, WOL), "r": (WURH, WURL)}[what]
                    parts = [((XTH[:, at], XTL[:, at]), (high[:, :], low[:, :]))]
                dst = pj_wait(b, f"{what}{c}")
                mm(dst[:, :], ONES3[:, :], BIAS3[:, i * HID:(i + 1) * HID], True, False)
                for x_, w_ in parts:
                    ins = mm3(dst[:, :], x_, w_, False, x_ is parts[-1][0])
                ins.then_inc(pj_full, 1)

            def decays(b, c, hf):
                dm_wait(b, f"{('even', 'odd')[hf]}{c}")
                mm(DM[:, :], IDB[:, :], MASKB[:, :], True, False)
                for m in range(4):
                    h = 2 * m + hf
                    ins = mm(DM[:, m * P:(m + 1) * P], SEL3[:, h * P:(h + 1) * P], M3[:, c * P:(c + 1) * P],
                             False, m == 3)
                ins.then_inc(dm_full, 1)

            def state_decays(b, c):
                dm_wait(b, f"state{c}")
                for m in range(4):
                    ins = mm(DM[:, m * P:(m + 1) * P], SEL3[:, 2 * m * P + HD:2 * m * P + HD + P],
                             M3[:, c * P:(c + 1) * P])
                ins.then_inc(dm_full, 1)

            def scores(b, c):
                if c == 0:
                    pe.wait_ge(*pj_read_at(b, "k2"))
                    pe.wait_ge(*pj_read_at(b, "k3"))
                for m in range(4):
                    for hf in range(2):
                        rows = slice(hf * HD, (hf + 1) * HD)
                        ins = mm(SB[hf][:, m * P:(m + 1) * P], KT[rows, m, c * P:(c + 1) * P],
                                 QT[rows, m, c * P:(c + 1) * P])
                        if m == 3:
                            ins.then_inc(st_full, 1)

            def from_state(b, c):
                n = b * NC + c
                if c == 0:
                    pe.wait_ge(cs_ready, b + 1)
                else:
                    pe.wait_ge(*tr_read_at(b, f"u{c - 1}"))
                pe.wait_ge(hv_read, n + 1)
                pe.wait_ge(qs_ready, n + 2)
                for m in range(4):
                    for hf in range(2):
                        rows = slice(hf * HD, (hf + 1) * HD)
                        mm(NB_[hf][:, m * 65:(m + 1) * 65], QS[rows, m, :], CS[rows, m, :], m == 0, False)

            def to_state(b, c):
                pe.wait_ge(*pj_read_at(b, f"v{c}"))
                pe.wait_ge(*tr_read_at(b, f"k{c}"))
                dst = tr_wait(b, f"u{c}")
                for h in range(H):
                    rows = slice((h % 2) * HD, (h % 2 + 1) * HD)
                    ins = mm(dst[rows, (h // 2) * 65:(h // 2 + 1) * 65], KW[:, c % 2, h, :], VX[:, c % 2, h, :])
                ins.then_inc(tr_full, 1)

            def values(b, c):
                pe.wait_ge(*pj_read_at(b, f"v{c}"))
                for hf in range(2):
                    pe.wait_ge(pt_ready, 2 * (b * NC + c) + hf + 2)
                    for m in range(4):
                        ins = mm(NB_[hf][:, m * 65:(m + 1) * 65], PT[:, hf, m, :], VX[:, c % 2, 2 * m + hf, :],
                                 False, True)
                    ins.then_inc(hv_full, 1)

            def transpose_out(b, c):
                pe.wait_ge(outg_ready, b * NC + c + 2)
                dst = tr_wait(b, f"o{c}")
                for m in range(4):
                    ins = t_.transpose(dst[:, m * P:(m + 1) * P], OUT[:, m * P:(m + 1) * P], ident)
                ins.then_inc(tr_full, 1)

            def down_out(b, c):
                dst = tr_wait(b, f"d{c}")
                for m in range(4):
                    ins = mm(dst[:, 0:D], OUTT[:, m, :], WDT[:, m, :], m == 0, m == 3)
                ins.then_inc(tr_full, 1)

            def chunk(b, c, last):
                more = c < NC - 1
                nxt = (b, c + 1) if more else None if last else (b + 1, 0)
                if c == 0:
                    pe.wait_ge(m3_ready, b + 1)
                decays(b, c, 0)
                scores(b, c)
                if c == 0:
                    k_tokens(b, 0)
                if c >= 2:
                    transpose_out(b, c - 2)
                if last and c == 3:
                    xn_channels(1, 0)
                if nxt:
                    project(*nxt, "v")
                decays(b, c, 1)
                if c >= 2:
                    down_out(b, c - 2)
                if nxt:
                    project(*nxt, "o")
                if last and c == 3:
                    xn_channels(1, 1)
                if more:
                    k_tokens(b, c + 1)
                state_decays(b, c)
                if last and c == 3:
                    xn_channels(1, 2)
                if nxt:
                    project(*nxt, "r")
                if more:
                    project(b, c + 1, "s")
                if c == 2 and not last:
                    head_z(b + 1)
                from_state(b, c)
                if more:
                    to_state(b, c)
                values(b, c)
                if last and c == 3:
                    for q in range(3):
                        logits(1, q)
                if c == 2 and not last:
                    head_x(b + 1)

            def sequence(b, last):
                for c in range(NC):
                    chunk(b, c, last)
                if last:
                    for c in (2, 3):
                        transpose_out(b, c)
                        down_out(b, c)
                    return
                head_gates(b + 1)
                head_qk(b + 1, WQH, WQL, "q")
                transpose_out(b, 2)
                head_qk(b + 1, WKH, WKL, "k", lambda: down_out(b, 2))
                project(b + 1, 0, "s")
                transpose_out(b, 3)
                head_columns(b + 1)
                down_out(b, 3)

            ffn(0)
            pe.wait_ge(w_low, 1)
            head_z(0)
            head_x(0)
            for what in "vor":
                project(0, 0, what)
            head_gates(0)
            head_qk(0, WQH, WQL, "q")
            head_qk(0, WKH, WKL, "k")
            project(0, 0, "s")
            head_columns(0)
            with pe.Fori(0, NB - 1) as b:
                sequence(b, False)
            sequence(NB - 1, True)
            ffn(1)

        @block.vector
        def _(dve):
            v = nc.vector
            step = Steps(dve, dve_step)
            do, did = step.do, step.did

            def bc(ap, shape):
                return ap.unsqueeze(len(ap.shape)).to_broadcast(shape)

            def moments(st, w, n):
                did(v.tensor_tensor(w[:, 0, :], st[:, :, 1], st[:, :, 4], ALU.add))
                did(v.tensor_tensor(w[:, 1, :], st[:, :, 1], st[:, :, 4], ALU.subtract))
                do(v.tensor_tensor(w[:, 2, :], st[:, :, 2], st[:, :, 5], ALU.add))
                did(v.tensor_scalar(w[:, 0, :], w[:, 0, :], 0.5, None, ALU.mult))
                do(v.scalar_tensor_tensor(out=w[:, 1, :], in0=w[:, 1, :], scalar=0.25, in1=w[:, 1, :],
                                          op0=ALU.mult, op1=ALU.mult))
                do(v.scalar_tensor_tensor(out=w[:, 3, :], in0=w[:, 2, :], scalar=1.0 / n, in1=w[:, 1, :],
                                          op0=ALU.mult, op1=ALU.add))

            def combine(f, q):
                dve.wait_ge(y_loaded[f][q], 16)
                for t in range(4 * q, 4 * q + 4):
                    v.scalar_tensor_tensor(out=X[:, t, :], in0=YG[:, t, :], scalar=RT[:, 3, t:t + 1],
                                           in1=X[:, t, :], op0=ALU.mult, op1=ALU.add).then_inc(ffn_done[f], 1)
                dve.wait_ge(ffn_done[f], 4 * q + 4)

            def layer_moments(f, group):
                lo, hi = GROUPS[f][group]
                for t in range(lo, hi):
                    if f == 0 and t % 4 == 0:
                        dve.wait_ge(x_loaded[t // 4], 16)
                    did(v.bn_stats(ST[:, t, :], X[:, t, :]))
                step.settle()
                moments(ST[:, lo:hi, :], LNA[:, :, lo:hi], D)
                v.tensor_scalar(LNA[:, 4, lo:hi], LNA[:, 3, lo:hi], 1e-5, None, ALU.add).then_inc(var_ready[f], 1)

            def layer_norm(f, group):
                dve.wait_ge(rstd_ready[f], group + 1)
                for t in range(*GROUPS[f][group]):
                    v.tensor_scalar(XN[f][:, t, 0:D], X[:, t, :], LNA[:, 0, t:t + 1], LNA[:, 5, t:t + 1],
                                    ALU.subtract, ALU.mult).then_inc(xn_ready[f], 1)

            def ffn(f):
                if f == 0:
                    layer_moments(0, 0)
                layer_moments(f, 1)
                if f == 0:
                    layer_norm(0, 0)
                layer_norm(f, 1)
                dve.wait_ge(logits_full[f], 4)
                dve.wait_ge(first_loaded, 32)
                dve.wait_ge(consts_loaded, 16)
                logits = bank[3][:, 0:NT * NE].rearrange("p (t e) -> p t e", e=NE)
                do(v.tensor_reduce(RT[:, 0, :], logits, AX_X, ALU.max))
                do(v.tensor_tensor(OH[:, :, :], logits, bc(RT[:, 0, :], [P, NT, NE]), ALU.is_equal))
                rev = const("rev").unsqueeze(1).to_broadcast([P, NT, NE])
                do(v.tensor_tensor(OH[:, :, :], OH[:, :, :], rev, ALU.mult))
                do(v.tensor_reduce(RT[:, 1, :], OH[:, :, :], AX_X, ALU.max))
                v.tensor_tensor(OH[:, :, :], rev, bc(RT[:, 1, :], [P, NT, NE]), ALU.is_equal)\
                    .then_inc(onehot_ready[f], 1)
                v.tensor_tensor(EX[:, :, :], logits, bc(RT[:, 0, :], [P, NT, NE]), ALU.subtract)\
                    .then_inc(shifted[f], 1)
                dve.wait_ge(ranks_full[f], 1)
                do(v.tensor_copy(TOTE[:, :, :], bank[2][:, P:2 * P].rearrange("p (t e) -> p e t", e=NE)))
                do(v.tensor_tensor_scan(INCL[:, :, :].rearrange("p e t -> p (e t)"), const("reset16"),
                                        TOTE[:, :, :].rearrange("p e t -> p (e t)"), 0.0, ALU.mult, ALU.add))
                do(v.tensor_tensor(CMP[:, :, :], bc(INCL[:, :, NT - 1], [P, NE, NT]),
                                   const("thr").unsqueeze(1).to_broadcast([P, NE, NT]), ALU.is_gt))
                did(v.tensor_tensor(INCL[:, :, :], INCL[:, :, :], TOTE[:, :, :], ALU.subtract))
                do(v.tensor_reduce(EB[:, 0, :], CMP[:, :, :], AX_X, ALU.add))
                do(v.tensor_tensor_scan(EB[:, 1, :], const("ones")[:, 0:NE], EB[:, 0, :], 0.0, ALU.mult, ALU.add))
                do(v.tensor_tensor(EB[:, 2, :], EB[:, 1, :], EB[:, 0, :], ALU.subtract))
                do(v.scalar_tensor_tensor(out=INCL[:, :, :], in0=bc(EB[:, 2, :], [P, NE, NT]), scalar=float(P),
                                          in1=INCL[:, :, :], op0=ALU.mult, op1=ALU.add))
                do(v.tensor_tensor(RK[:, :, :], bank[2][:, 0:P].rearrange("p (t e) -> p t e", e=NE),
                                   INCL[:, :, :].rearrange("p e t -> p t e"), ALU.add))
                do(v.tensor_tensor(RK[:, :, :], RK[:, :, :], OH[:, :, :], ALU.mult))
                do(v.tensor_reduce(RT[:, 4, :], RK[:, :, :], AX_X, ALU.add))
                v.tensor_copy(POS[:, :], RT[:, 4, :]).then_inc(pos_ready[f], 1)
                dve.wait_ge(exp_ready[f], 1)
                did(v.tensor_reduce(RT[:, 2, :], EX[:, :, :], AX_X, ALU.add))
                do(v.tensor_tensor(BE[:, :, :], bc(const("blk"), [P, 24, NE]),
                                   EB[:, 1, :].unsqueeze(1).to_broadcast([P, 24, NE]), ALU.is_ge))
                did(v.reciprocal(RT[:, 3, :], RT[:, 2, :]))
                do(v.tensor_reduce(EIDF[:, :], BE[:, :, :], AX_X, ALU.add))
                did(v.tensor_scalar(RT[:, 3, :], RT[:, 3, :], 0.5, None, ALU.mult))
                do(v.tensor_scalar(EIDF[:, :], EIDF[:, :], float(NE - 1), None, ALU.min))
                v.tensor_copy(EID[:, :], EIDF[:, :]).then_inc(eid_ready[f], 1)
                dve.wait_ge(eid_ready[f], 1)
                if f == 0:
                    attn_setup()
                dve.wait_ge(ffn_loaded, 48)

                def copy_idx(k, j):
                    dve.wait_ge(xbt_full[f], k + 1)
                    if not (isinstance(k, int) and k < RING):
                        dve.wait_ge(y_sent[f][j], 4 * (k - j))
                    v.tensor_copy(IDX[:, j:j + 1], XB[:, j, D:D + 1]).then_inc(idx_copied[f], 1)

                def copy_w1(k, j):
                    e = dve.value_load(EID[0:1, bass.ds(k, 1)], min_val=0, max_val=NE - 1)
                    if not (isinstance(k, int) and k < 2):
                        dve.wait_ge(relu_act[f], k - 1)
                        dve.wait_ge(relu_dve[f], k - 1)
                    v.tensor_copy(B2R[:, j, :], B2[:, e, :])
                    v.tensor_copy(W1R[:, j % 2, :], W1[:, e, :]).then_inc(w1_copied[f], 1)

                def relu(k, j):
                    dve.wait_ge(h_full[f], 2 * k + 2)
                    for c in range(2):
                        ins = v.tensor_scalar(HT[:, j % 2, 2 + c, :], bank[4 + j % 2][:, c * P:(c + 1) * P],
                                              W1R[:, j % 2, F + 2 + c:F + 3 + c], 0.0, ALU.add, ALU.max)
                    ins.then_inc(relu_dve[f], 1)

                def add_b2(k, j):
                    dve.wait_ge(y_full[f], k + 1)
                    v.tensor_tensor(YB[:, j, :], bank[6 + j % 2][:, 0:D], B2R[:, j, :], ALU.add).then_inc(y_ready[f], 1)

                def turn(k, j, n):
                    def within(i):
                        return not (isinstance(k, int) and k + i >= NBLK)

                    if within(1):
                        relu(k + 1, (j + 1) % RING)
                        copy_idx(k + 1, (j + 1) % RING)
                    if within(3):
                        copy_w1(k + 3, (j + 3) % RING)
                    add_b2(k, j)

                copy_w1(0, 0)
                copy_w1(1, 1)
                copy_idx(0, 0)
                relu(0, 0)
                copy_w1(2, 2)
                over_blocks(dve, turn)
                if f == 0:
                    low_weights()
                combine(f, 0)
                if f == 0:
                    norm_moments(0)
                    scale_norm(0)
                    second_norm(0)
                    combine(0, 1)
                    low_xt(0)
                for q in range(2 - f, 4):
                    combine(f, q)

            def attn_setup():
                dve.wait_ge(attn_loaded, 160)
                dve.wait_ge(cols_loaded, 48)
                for j in range(2):
                    ins = v.tensor_copy(BULB[:, j, :], col("bul", j).to_broadcast([P, P]))
                ins.then_inc(folds_ready, 1)
                dve.wait_ge(cleared, 1)
                dve.wait_ge(constants_cast, 1)
                do(v.tensor_scalar(WCT[:, :], WULT[:, 0:256], row("cw", 4)[:, 0:1], None, ALU.mult))
                for m in range(1, 4):
                    do(v.scalar_tensor_tensor(out=WCT[:, :], in0=WULT[:, m:m + 256], scalar=row("cw", 4)[:, m:m + 1],
                                              in1=WCT[:, :], op0=ALU.mult, op1=ALU.add))
                do(v.tensor_tensor(BSH[:, :, :], COLS[:, COL["bshift"]:COL["bshift"] + 8]
                                   .rearrange("p (j m) -> p j m", j=2),
                                   row("cw", 4).unsqueeze(1).to_broadcast([P, 2, 4]), ALU.mult))
                do(v.tensor_reduce(HBX[:, :], BSH[:, :, :], AX_X, ALU.add))
                did(v.tensor_scalar(HBX[:, :], HBX[:, :], row("cb", 1), 0.5, ALU.add, ALU.mult))
                did(v.tensor_scalar(WKT[:, :, :], WKT[:, :, :], HD ** -0.5, None, ALU.mult))
                did(v.tensor_scalar(COLS[:, COL["bk"]:COL["bk"] + 4], COLS[:, COL["bk"]:COL["bk"] + 4],
                                    HD ** -0.5, None, ALU.mult))
                did(v.tensor_scalar(WDT[:, :, :], WDT[:, :, :], 0.5, None, ALU.mult))
                did(v.tensor_scalar(col("bif"), col("bif"), 1.0 / CAP, None, ALU.mult))
                did(v.tensor_tensor(row("bsk", HID), row("bsk", HID), row("mhb", HID), ALU.add))
                for i, name in enumerate(("bv", "bo")):
                    dve.wait_ge(fold_full, 2 * i + 2)
                    did(v.tensor_tensor(row(name, HID), bank[5 + 2 * i][:, :], row(name, HID), ALU.add))
                rows = BROWS[0:1, :]
                step.settle()
                do(v.tensor_copy(BIAS3[0:1, :], rows))
                do(v.tensor_tensor(rows, rows, BIAS3[0:1, :], ALU.subtract))
                do(v.tensor_copy(BMID, rows))
                did(v.tensor_copy(BIAS3[32:33, :], BMID))
                do(v.tensor_tensor(rows, rows, BMID, ALU.subtract))
                did(v.tensor_copy(BIAS3[64:65, :], rows))
                step.settle()
                did(v.tensor_copy(WCH[:, :], WCT[:, :]))
                do(v.tensor_copy(WIFH[:, :, :], WIFT[:, :, :]))
                did(v.tensor_tensor(WCL[:, :], WCT[:, :], WCH[:, :].bitcast(F32), ALU.subtract))
                did(v.tensor_tensor(WIFL[:, :, :], WIFT[:, :, :], WIFH[:, :, :].bitcast(F32), ALU.subtract))
                for i, s in enumerate((*pj_free, tr_free, xc_ready, pt_ready, dm_free, hv_read,
                                       outg_ready, hn_ready, qs_ready)):
                    v.memset(CREDIT[:, i:i + 1], 0.0).then_inc(s, 1)
                step.settle()
                v.memset(MIN[:, :], 0.0).then_inc(attn_consts, 1)
                dve.wait_ge(attn_consts, 1)

            def norm_moments(b):
                for j in range(4):
                    did(v.bn_stats(SA[:, j, :], X[:, bass.ds(b * 4 + j, 1), :].rearrange("p a d -> p (a d)")))
                step.settle()
                moments(SA, LA, D)
                v.tensor_scalar(LA[:, 4, :], LA[:, 3, :], 1e-5, None, ALU.add).then_inc(a_var, 1)
                xs = X[:, bass.ds(b * 4, 4), :]
                do(v.tensor_tensor(UB[:, :, :], xs, bc(LA[:, 0, :], [P, 4, D]), ALU.subtract))

            def scale_norm(b):
                dve.wait_ge(a_rstd, b + 1)
                do(v.tensor_tensor(LA[:, 6, :], LA[:, 5, :], LA[:, 5, :], ALU.mult))
                do(v.tensor_tensor(LA[:, 6, :], LA[:, 6, :], LA[:, 3, :], ALU.mult))
                v.tensor_scalar(LA[:, 7, :], LA[:, 6, :], 1e-6, None, ALU.add).then_inc(a_var2, 1)
                v.tensor_tensor(UB[:, :, :], UB[:, :, :], bc(LA[:, 5, :], [P, 4, D]), ALU.mult).then_inc(u_ready, 1)
                dve.wait_ge(u_ready, b + 1)

            def second_norm(b):
                dve.wait_ge(a_rstd2, b + 1)
                v.tensor_tensor(ZB[:, :, :], UB[:, :, :], bc(LA[:, 8, :], [P, 4, D]), ALU.mult).then_inc(z_ready, 1)

            def add_u(b):
                xs = X[:, bass.ds(b * 4, 4), :]
                dve.wait_ge(ubd_ready, b + 1)
                do(v.tensor_tensor(xs, xs, UB[:, :, :], ALU.add))

            def low_weights():
                for i, (low, weights, high) in enumerate(((WVL, WVF, WVH), (WOL, WOF, WOH), (WURL, WURT, WURH))):
                    dve.wait_ge(w_high, i + 1)
                    did(v.tensor_tensor(low[:, :], weights[:, :], high[:, :].bitcast(F32), ALU.subtract))
                for i, (low, weights, high) in enumerate(((WQL, WQT, WQH), (WKL, WKT, WKH), (WSKL, WSKT, WSKH))):
                    dve.wait_ge(w_high, i + 4)
                    did(v.tensor_tensor(low[:, :, :], weights[:, :, :], high[:, :, :].bitcast(F32), ALU.subtract))
                step.settle()
                v.memset(CREDIT[:, 0:1], 0.0).then_inc(w_low, 1)

            def low_xt(b):
                dve.wait_ge(*pj_read_at(b, "z"))
                v.tensor_tensor(XTL[:, :], XT[:, :], XTH[:, :].bitcast(F32), ALU.subtract).then_inc(xt_low, 1)

            def low_xc(b):
                dve.wait_ge(xc_high, b + 1)
                v.tensor_tensor(XCL[:, :, :], XC[:, :, :], XCH[:, :, :].bitcast(F32), ALU.subtract).then_inc(xc_low, 1)

            def silu(b):
                dve.wait_ge(tanh_ready, b + 1)
                v.scalar_tensor_tensor(out=XC[:, :, :], in0=TH, scalar=1.0, in1=YH,
                                       op0=ALU.add, op1=ALU.mult).then_inc(xc_ready, 1)

            def reset_state():
                did(v.memset(CS[:, :, 0:HD], 0.0))
                v.memset(CS[:, :, HD:HD + 1], 1.0).then_inc(cs_ready, 1)

            def gate_scans(b, between=None):
                dve.wait_ge(*pj_read_at(b, "gates"))
                do(v.tensor_scalar(F15[:, :], TIF[32:32 + H, :], CAP, None, ALU.mult))
                do(v.tensor_tensor_scan(FS[:, :], const("reset")[0:H, :], F15[:, :], 0.0, ALU.mult, ALU.add))
                do(v.scalar_tensor_tensor(out=GT[0:H, :], in0=TIF[0:H, :], scalar=CAP, in1=FS[:, :],
                                          op0=ALU.mult, op1=ALU.subtract))
                for c in range(NC):
                    if c == 1 and between:
                        between()
                    at = slice(c * P, (c + 1) * P)
                    do(v.tensor_tensor_scan(MM[:, at], GT[0:H, at], GT[0:H, at], MIN[:, c:c + 1], ALU.max, ALU.max))
                    if c < NC - 1:
                        last = slice((c + 1) * P - 1, (c + 1) * P)
                        do(v.tensor_tensor(MIN[:, c + 1:c + 2], FS[:, last], MM[:, last], ALU.add))

            def gate_rows(b):
                m4 = MM[:, :].rearrange("p (c t) -> p c t", c=NC)
                a4 = GT[0:H, :].rearrange("p (c t) -> p c t", c=NC)
                did(v.tensor_tensor(GT[64:64 + H, :].rearrange("p (c t) -> p c t", c=NC), a4,
                                    bc(m4[:, :, P - 1], [H, NC, P]), ALU.subtract))
                do(v.tensor_tensor(G3[:, :], MIN[:, 0:NC], m4[:, :, P - 1], ALU.subtract))
                heads = const("decr")[0:H, :].unsqueeze(1).to_broadcast([H, NC, NP_])
                did(v.tensor_tensor(G3M[:, :, :], bc(G3[:, :], [H, NC, NP_]), heads, ALU.mult))
                do(v.tensor_tensor(MINM[:, :, :], bc(MIN[:, 0:NC], [H, NC, NP_]), heads, ALU.mult))
                v.memset(CREDIT[:, 0:1], 0.0).then_inc(rows_ready, 1)
                do(v.tensor_copy(M3[0:H, :], MM[:, :]))
                do(v.tensor_tensor(MM[:, :], MM[:, :], M3[0:H, :], ALU.subtract))
                do(v.tensor_copy(MMID[:, :], MM[:, :]))
                did(v.tensor_copy(M3[32:32 + H, :], MMID[:, :]))
                do(v.tensor_tensor(MM[:, :], MM[:, :], MMID[:, :], ALU.subtract))
                v.tensor_copy(M3[64:64 + H, :], MM[:, :]).then_inc(m3_ready, 1)

            def take_k(b, c):
                if c == 0:
                    dve.wait_ge(*dm_read_at(b, "columns"))
                dve.wait_ge(*tr_full_at(b, f"k{c}"))
                v.tensor_tensor(KW[:, c % 2, :, :], TR[:, :].rearrange("p (h d) -> p h d", h=H),
                                bc(EW[:, c, :], [P, H, HD]), ALU.mult).then_inc(tr_free, 1)

            def take_r(b, c):
                dve.wait_ge(rth_ready, b * NC + c + 1)
                i = pj_bank(f"r{c}")
                v.scalar_tensor_tensor(out=GR[c], in0=RTH[:, :], scalar=1.0, in1=PJ[i][:, :],
                                       op0=ALU.add, op1=ALU.mult).then_inc(pj_free[i], 1)

            def weigh(b, c, hf):
                n = b * NC + c
                dve.wait_ge(st_full, 2 * n + hf + 1)
                dve.wait_ge(*dm_read_at(b, f"{('even', 'odd')[hf]}{c}"))
                v.tensor_tensor(PT[:, hf, :, :].rearrange("p m t -> p (m t)"), SB[hf][:, :],
                                DT[:, hf, :, :].rearrange("p m t -> p (m t)"), ALU.mult).then_inc(pt_ready, 1)

            def scale_q(b, c):
                n = b * NC + c
                dve.wait_ge(*dm_read_at(b, f"state{c}"))
                v.tensor_tensor(QS[:, :, :], QT[:, :, c * P:(c + 1) * P], E1[:, :, :], ALU.mult).then_inc(qs_ready, 1)

            def new_state(b, c):
                dve.wait_ge(*tr_full_at(b, f"u{c}"))
                if c == 0:
                    dve.wait_ge(cs_ready, b + 1)
                do(v.tensor_tensor(CS[:, :, :], CS[:, :, :], bc(DEC[:, c, :], [P, NP_, HD + 1]), ALU.mult))
                v.tensor_tensor(CS[:, :, :], CS[:, :, :], TR[:, 0:260].rearrange("p (m d) -> p m d", m=4),
                                ALU.add).then_inc(tr_free, 1)
                dve.wait_ge(*tr_read_at(b, f"u{c}"))

            def centre(b, c):
                n = b * NC + c
                sums = [NB_[hf][:, 0:260].rearrange("p (m d) -> p m d", m=4) for hf in range(2)]
                h2 = H2[:, :, :].rearrange("p (m two) d -> p two m d", two=2)
                for hf in range(2):
                    dve.wait_ge(hv_full, 2 * n + hf + 1)
                    did(v.tensor_scalar(DN[:, 0, hf, :], sums[hf][:, :, HD], 1.0, 2.0, ALU.max, ALU.mult))
                step.settle()
                do(v.reciprocal(DN[:, 1, :, :], DN[:, 0, :, :]))
                did(v.tensor_tensor(h2[:, 0], sums[0][:, :, 0:HD], bc(DN[:, 1, 0, :], [P, NP_, HD]), ALU.mult))
                step.settle()
                v.tensor_tensor(h2[:, 1], sums[1][:, :, 0:HD], bc(DN[:, 1, 1, :], [P, NP_, HD]), ALU.mult)\
                 .then_inc(hv_read, 1)
                dve.wait_ge(hv_read, n + 2)
                dve.wait_ge(*pj_read_at(b, f"o{c}"))
                flat = H2[:, :, :].rearrange("p h d -> p (h d)")
                do(v.scalar_tensor_tensor(out=flat, in0=OT[:, c % 2, :], scalar=1.0, in1=flat,
                                          op0=ALU.add, op1=ALU.mult))
                do(v.tensor_reduce(HS[:, 0, :], H2[:, :, :], AX_X, ALU.add))
                do(v.tensor_scalar(HS[:, 0, :], HS[:, 0, :], 1.0 / HD, None, ALU.mult))
                v.tensor_tensor(H2[:, :, :], H2[:, :, :], bc(HS[:, 0, :], [P, H, HD]), ALU.subtract)\
                 .then_inc(cen_ready, 1)

            def variance(b, c):
                dve.wait_ge(sq_ready, b * NC + c + 1)
                do(v.tensor_reduce(HS[:, 1, :], SQ[:, :, :], AX_X, ALU.add))
                v.tensor_scalar(HS[:, 2, :], HS[:, 1, :], 1.0 / HD, 1e-6, ALU.mult, ALU.add).then_inc(hvar_ready, 1)

            def gate(b, c):
                dve.wait_ge(hn_ready, b * NC + c + 2)
                dve.wait_ge(*pj_read_at(b, f"r{c}"))
                if c:
                    dve.wait_ge(*tr_full_at(b, f"o{c - 1}"))
                v.tensor_tensor(OUT[:, :], H2[:, :, :].rearrange("p h d -> p (h d)"), GR[c], ALU.mult)\
                 .then_inc(outg_ready, 1)

            def update_x(b, c):
                dve.wait_ge(*tr_full_at(b, f"d{c}"))
                t = X[:, bass.ds(b * 4 + c, 1), :].rearrange("p a d -> p (a d)")
                v.tensor_tensor(t, t, TR[:, 0:D], ALU.add).then_inc(tr_free, 1)

            def chunk(b, c, last):
                more = c < NC - 1
                weigh(b, c, 0)
                if c == 0:
                    take_k(b, 0)
                if c >= 2:
                    update_x(b, c - 2)
                if c:
                    variance(b, c - 1)
                if more:
                    take_k(b, c + 1)
                if c == 2 and not last:
                    second_norm(b + 1)
                weigh(b, c, 1)
                scale_q(b, c)
                if c == 3 and not last:
                    take_r(b + 1, 0)
                    low_xc(b + 1)
                if more:
                    take_r(b, c + 1)
                if last and c == 0:
                    layer_moments(1, 0)
                if last and c == 2:
                    layer_norm(1, 0)
                if c == 1 and not last:
                    norm_moments(b + 1)
                if more:
                    new_state(b, c)
                if c == 2 and not last:
                    low_xt(b + 1)
                if c:
                    gate(b, c - 1)
                if c == 1 and not last:
                    scale_norm(b + 1)
                centre(b, c)
                if c == 2 and not last:
                    silu(b + 1)

            def sequence(b, last):
                for c in range(NC):
                    chunk(b, c, last)
                if not last:
                    reset_state()
                    gate_scans(b + 1, lambda: variance(b, 3))
                    update_x(b, 2)
                    gate_rows(b + 1)
                else:
                    variance(b, 3)
                    update_x(b, 2)
                gate(b, 3)
                if not last:
                    add_u(b + 1)
                update_x(b, 3)

            ffn(0)
            add_u(0)
            reset_state()
            silu(0)
            low_xc(0)
            take_r(0, 0)
            gate_scans(0)
            gate_rows(0)
            PER = 69
            with dve.Fori(0, NB - 1) as b:
                step.loop(b, PER)
                sequence(b, False)
            step.looped(NB - 1)
            sequence(NB - 1, True)
            dve.wait_ge(*tr_read_at(NB - 1, "d3"))
            ffn(1)


def _shape_constants(np):
    k = np.zeros((P, NCONST), np.float32)

    def put(name, a):
        at, w = CONST[name]
        k[:a.shape[0], at:at + w] = a

    p, c = np.arange(P)[:, None], np.arange(P)[None, :]
    put("ident", np.eye(P))
    put("tri", p < c)
    put("ones", np.ones((P, P)))
    put("mask", np.tile(np.where(p <= c, 0.0, NEG), (1, 4)))
    for part in range(3):
        k[32 * part:32 * part + H, CONST["sel"][0]:CONST["sel"][0] + H * P] = -np.repeat(np.eye(H), P, axis=1)
    put("decl", (np.arange(H)[:, None] % 2) == (np.arange(P)[None, :] >= HD))
    put("decr", (np.arange(H)[:, None] // 2) == np.arange(NP_)[None, :])
    put("rev", np.tile(NE - np.arange(NE), (P, 1)))
    put("thr", np.tile(P * np.arange(NT), (P, 1)))
    put("fill", NT * P + P * np.arange(NBLK)[None, :] + p)
    put("token", P * np.arange(NT)[None, :] + p)
    put("blk", np.tile(np.arange(24), (P, 1)))
    put("reset", np.tile(np.arange(S) % P != 0, (P, 1)))
    put("reset16", np.tile(np.arange(NE * NT) % NT != 0, (P, 1)))
    return k


def kernel(**inputs):
    import numpy as np
    import concourse.bacc as _bacc
    from concourse import mybir as _mybir
    from concourse.bass_utils import run_bass_kernel_spmd as _run

    a = {n.replace("L0_attn_", "").replace("L0_ffn_", "f_"): np.asarray(v) for n, v in inputs.items()}

    def kmajor(w):
        return w.T.reshape(-1, P, w.shape[0]).transpose(1, 0, 2)

    cols = np.zeros((P, NCOL), np.float32)
    cols[:, 0], cols[:, 1] = a["ln_g"], a["ln_b"]
    padded = np.concatenate([np.zeros(3, np.float32), a["b_up_l"]])
    for j in range(2):
        for m in range(4):
            cols[:, COL["bshift"] + 4 * j + m] = padded[j * P + m:j * P + m + P]
        cols[:, COL["bul"] + j] = a["b_up_l"][j * P:(j + 1) * P]
    cols[:, COL["bq"]:COL["bq"] + 4] = a["b_q"].reshape(4, P).T
    cols[:, COL["bk"]:COL["bk"] + 4] = a["b_k"].reshape(4, P).T
    cols[0:H, COL["bif"]], cols[32:32 + H, COL["bif"]] = a["b_i"], a["b_f"]
    rows = np.concatenate([a["b_v"], a["b_o"], a["b_up_r"], a["b_skip"], a["mh_b"].ravel(), a["mh_g"].ravel(),
                           a["b_down"], a["conv_w"], a["conv_b"].reshape(1)])
    gates = np.zeros((P, 2, 40), np.float32)
    gates[:, :, 0:H], gates[:, :, 32:32 + H] = kmajor(a["W_i"]), kmajor(a["W_f"])
    w1 = np.concatenate([a["f_w1"].transpose(1, 0, 2), a["f_b1"].reshape(NE, FC, P).transpose(2, 0, 1)], axis=2)
    arrays = {
        "x": a["x"].reshape(NT * P, D), "consts": _shape_constants(np), "colpack": cols, "rowpack": rows,
        "w_router": a["f_w_router"], "w1": w1, "w2": a["f_w2"].reshape(NE, FC, P, D).transpose(2, 0, 1, 3),
        "b2": a["f_b2"], "wul": a["W_up_l"].reshape(2, P, D).transpose(1, 0, 2),
        "wult": np.concatenate([np.zeros((P, 3), np.float32), a["W_up_l"].T], axis=1), "wurt": a["W_up_r"].T,
        "wqt": kmajor(a["W_q"]), "wkt": kmajor(a["W_k"]), "wskt": kmajor(a["W_skip"]), "wvt": kmajor(a["W_v"]),
        "wot": kmajor(a["W_o"]), "wift": gates, "wdt": kmajor(a["W_down"]),
    }
    nc = _bacc.Bacc("TRN2", target_bir_lowering=False, num_devices=1)
    args = []
    for name, v in arrays.items():
        arrays[name] = v = np.ascontiguousarray(v)
        args.append(nc.dram_tensor(name, v.shape, _mybir.dt.from_np(v.dtype), kind="ExternalInput").ap())
    args.append(nc.dram_tensor("out", (NT * P, D), F32, kind="ExternalOutput").ap())
    macaron(nc, *args)
    r = _run(nc, [arrays], core_ids=[0])
    return r.results[0]["out"].reshape(a["x"].shape)
```
